# Optimizing a Trainium2 kernel written in Bass

```python
import numpy as np
import jax
import jax.numpy as jnp

def _softmax(x, axis=-1):
    return jax.nn.softmax(x, axis=axis)

def _gelu(x):
    return jax.nn.gelu(x, approximate=True)

def _silu(x):
    return jax.nn.silu(x)

def _sigmoid(x):
    return jax.nn.sigmoid(x)

def _layernorm(x, axis=-1, eps=1e-05):
    m = jnp.mean(x, axis=axis, keepdims=True)
    v = jnp.var(x, axis=axis, keepdims=True)
    return (x - m) / jnp.sqrt(v + eps)

def _scatter_add(tgt, idx, src, axis=0):
    return tgt.at[idx].add(src)

def _segment_sum(src, seg, n):
    return jax.ops.segment_sum(src, seg, n)
kernel_name = 'mk_hybrid_d2_jaxref_r8_db64d8'

def setup_inputs(seed: int=0):
    np.random.seed(seed)
    _w = jnp.asarray

    def _L0_attn_a_setup():
        import jax, jax.numpy as jnp
        import numpy as np
        BATCH, SEQ, D_MODEL = (2, 512, 128)
        EXPAND, N_HEADS, D_STATE, D_CONV, CHUNK = (2, 16, 16, 4, 64)
        D_INNER = EXPAND * D_MODEL
        HEAD_DIM = D_INNER // N_HEADS
        LN_EPS = 1e-05

        def silu(v):
            return v * jax.nn.sigmoid(v)

        def _forward(x, W_in, conv_w, conv_b, W_xproj, W_dt, b_dt, A_log, D_skip, W_out, ln_g, ln_b):
            b, L, _ = x.shape
            xz = x @ W_in
            xe, z = jnp.split(xz, 2, axis=-1)
            xp = jnp.pad(xe, ((0, 0), (D_CONV - 1, 0), (0, 0)))
            xc = conv_b
            for j in range(D_CONV):
                xc = xc + conv_w[:, j] * xp[:, j:j + L, :]
            xc = silu(xc)
            proj = xc @ W_xproj
            dt_raw = proj[..., :N_HEADS]
            Bm = proj[..., N_HEADS:N_HEADS + D_STATE]
            Cm = proj[..., N_HEADS + D_STATE:]
            dt = jax.nn.softplus(dt_raw @ W_dt + b_dt)
            A = -jnp.exp(A_log)
            xh = xc.reshape(b, L, N_HEADS, HEAD_DIM)
            dth = dt.reshape(b, L, N_HEADS, HEAD_DIM)
            nc = L // CHUNK
            dt_cum = dth.reshape(b, nc, CHUNK, N_HEADS, HEAD_DIM).cumsum(axis=2)
            decay = jnp.exp(A[None, None, None, :, None] * dt_cum).reshape(b, L, N_HEADS, HEAD_DIM)
            xs = (jnp.moveaxis(xh, 1, 0), jnp.moveaxis(dth, 1, 0), jnp.moveaxis(decay, 1, 0), jnp.moveaxis(Bm, 1, 0), jnp.moveaxis(Cm, 1, 0))
            state0 = jnp.zeros((b, N_HEADS, HEAD_DIM, D_STATE), x.dtype)

            def step(state, inp):
                x_t, dt_t, dec_t, B_t, C_t = inp
                state = state * dec_t[..., None] + (dt_t * x_t)[..., None] * B_t[:, None, None, :]
                y_t = jnp.einsum('bhdn,bn->bhd', state, C_t)
                return (state, y_t)
            _, ys = jax.lax.scan(step, state0, xs)
            y = jnp.moveaxis(ys, 0, 1)
            y = y + xh * D_skip[None, None, :, None]
            y = y.reshape(b, L, D_INNER) * silu(z)
            mu = y.mean(-1, keepdims=True)
            var = ((y - mu) ** 2).mean(-1, keepdims=True)
            y = (y - mu) * jax.lax.rsqrt(var + LN_EPS) * ln_g + ln_b
            return y @ W_out
        key = jax.random.key(seed)
        ks = jax.random.split(key, 10)

        def w(k, shape, fan):
            return jax.random.normal(k, shape, jnp.float32) / np.float32(np.sqrt(fan))
        x = jax.random.normal(ks[0], (BATCH, SEQ, D_MODEL), jnp.float32)
        W_in = w(ks[1], (D_MODEL, 2 * D_INNER), D_MODEL)
        conv_w = w(ks[2], (D_INNER, D_CONV), D_CONV)
        conv_b = 0.01 * jax.random.normal(ks[3], (D_INNER,), jnp.float32)
        W_xproj = w(ks[4], (D_INNER, N_HEADS + 2 * D_STATE), D_INNER)
        W_dt = w(ks[5], (N_HEADS, D_INNER), N_HEADS)
        u = jax.random.uniform(ks[6], (N_HEADS,), jnp.float32)
        dt_init = jnp.exp(u * (np.log(0.1) - np.log(0.001)) + np.log(0.001))
        b_dt = jnp.repeat(jnp.log(jnp.expm1(dt_init)), HEAD_DIM)
        A_log = jnp.log(jnp.linspace(1.0, 16.0, N_HEADS)).astype(jnp.float32)
        D_skip = jnp.ones((N_HEADS,), jnp.float32)
        W_out = w(ks[7], (D_INNER, D_MODEL), D_INNER)
        ln_g = jnp.ones((D_INNER,), jnp.float32)
        ln_b = jnp.zeros((D_INNER,), jnp.float32)
        return {'x': x, 'W_in': W_in, 'conv_w': conv_w, 'conv_b': conv_b, 'W_xproj': W_xproj, 'W_dt': W_dt, 'b_dt': b_dt, 'A_log': A_log, 'D_skip': D_skip, 'W_out': W_out, 'ln_g': ln_g, 'ln_b': ln_b}
    _L0_attn_a_in = _L0_attn_a_setup()

    def _L0_attn_b_setup():
        import jax, jax.numpy as jnp
        import numpy as np
        EMBED_DIM = 128
        NUM_HEADS = 16
        HEAD_DIM = EMBED_DIM // NUM_HEADS
        B, N = (2, 256)
        BIAS_S = 32

        def _interp_matrix(n, s):
            pos = jnp.arange(n, dtype=jnp.float32) * ((s - 1) / (n - 1))
            i0 = jnp.floor(pos).astype(jnp.int32)
            i1 = jnp.minimum(i0 + 1, s - 1)
            frac = pos - i0.astype(jnp.float32)
            rows = jnp.arange(n)
            M = jnp.zeros((n, s), dtype=jnp.float32)
            M = M.at[rows, i0].add(1.0 - frac).at[rows, i1].add(frac)
            return M
        key = jax.random.key(seed)
        ks = jax.random.split(key, 12)
        std = 0.02
        d = {'x': jax.random.normal(ks[0], (B, N, EMBED_DIM), dtype=jnp.float32), 'Wq': jax.random.normal(ks[1], (EMBED_DIM, EMBED_DIM), dtype=jnp.float32) * std, 'bq': jnp.zeros((EMBED_DIM,), dtype=jnp.float32), 'Wk': jax.random.normal(ks[2], (EMBED_DIM, EMBED_DIM), dtype=jnp.float32) * std, 'bk': jnp.zeros((EMBED_DIM,), dtype=jnp.float32), 'Wv': jax.random.normal(ks[3], (EMBED_DIM, EMBED_DIM), dtype=jnp.float32) * std, 'bv': jnp.zeros((EMBED_DIM,), dtype=jnp.float32), 'Wo': jax.random.normal(ks[4], (EMBED_DIM, EMBED_DIM), dtype=jnp.float32) * std, 'bo': jnp.zeros((EMBED_DIM,), dtype=jnp.float32), 'gamma': jnp.ones((EMBED_DIM,), dtype=jnp.float32), 'beta': jnp.zeros((EMBED_DIM,), dtype=jnp.float32), 'rel_bias': jax.random.normal(ks[5], (NUM_HEADS, BIAS_S, BIAS_S), dtype=jnp.float32) * std}
        return d
    _L0_attn_b_in = _L0_attn_b_setup()

    def _L0_ffn_setup():
        import jax, jax.numpy as jnp
        import numpy as np
        D_MODEL = 128
        D_FF = 512
        N_EXPERTS = 8
        TOP_K = 2

        def _ffn(x, w1, b1, w2, b2):
            h = jax.nn.gelu(x @ w1.T + b1)
            return h @ w2.T + b2
        key = jax.random.key(seed)
        ks = jax.random.split(key, 12)
        s = 0.02
        x = jax.random.normal(ks[0], (4, 256, D_MODEL), dtype=jnp.float32)
        shared_w1 = jax.random.normal(ks[1], (D_FF, D_MODEL), dtype=jnp.float32) * s
        shared_b1 = jnp.zeros((D_FF,), dtype=jnp.float32)
        shared_w2 = jax.random.normal(ks[2], (D_MODEL, D_FF), dtype=jnp.float32) * s
        shared_b2 = jnp.zeros((D_MODEL,), dtype=jnp.float32)
        router_w = jax.random.normal(ks[3], (N_EXPERTS, D_MODEL), dtype=jnp.float32) * s
        router_b = jnp.zeros((N_EXPERTS,), dtype=jnp.float32)
        spec_w1 = jax.random.normal(ks[4], (N_EXPERTS, D_FF, D_MODEL), dtype=jnp.float32) * s
        spec_b1 = jnp.zeros((N_EXPERTS, D_FF), dtype=jnp.float32)
        spec_w2 = jax.random.normal(ks[5], (N_EXPERTS, D_MODEL, D_FF), dtype=jnp.float32) * s
        spec_b2 = jnp.zeros((N_EXPERTS, D_MODEL), dtype=jnp.float32)
        return dict(x=x, shared_w1=shared_w1, shared_b1=shared_b1, shared_w2=shared_w2, shared_b2=shared_b2, router_w=router_w, router_b=router_b, spec_w1=spec_w1, spec_b1=spec_b1, spec_w2=spec_w2, spec_b2=spec_b2)
    _L0_ffn_in = _L0_ffn_setup()

    def _L1_attn_a_setup():
        import math
        import jax, jax.numpy as jnp
        import numpy as np
        B, T, D, H = (4, 256, 128, 16)
        HD = D // H

        def apply_rope(x, base=10000.0):
            _, t, _, dh = x.shape
            half = dh // 2
            inv_freq = 1.0 / base ** (jnp.arange(half, dtype=jnp.float32) / float(half))
            pos = jnp.arange(t, dtype=jnp.float32)
            angles = pos[:, None] * inv_freq[None, :]
            sin = jnp.sin(angles)[None, :, None, :]
            cos = jnp.cos(angles)[None, :, None, :]
            x1 = x[..., :half]
            x2 = x[..., half:2 * half]
            rot1 = x1 * cos - x2 * sin
            rot2 = x1 * sin + x2 * cos
            return jnp.concatenate([rot1, rot2, x[..., 2 * half:]], axis=-1)
        key = jax.random.key(seed)
        k1, k2, k3 = jax.random.split(key, 3)
        x = jax.random.normal(k1, (B, T, D), dtype=jnp.float32)
        Wqkv = jax.random.normal(k2, (D, 3 * D), dtype=jnp.float32) / math.sqrt(D)
        Wo = jax.random.normal(k3, (D, D), dtype=jnp.float32) / math.sqrt(D)
        bo = jnp.zeros((D,), dtype=jnp.float32)
        return {'x': x, 'Wqkv': Wqkv, 'Wo': Wo, 'bo': bo}
    _L1_attn_a_in = _L1_attn_a_setup()

    def _L1_attn_b_setup():
        import jax, jax.numpy as jnp
        import numpy as np
        B, K, D = (8, 256, 128)
        INNER = 2 * D
        EPS = 1e-05

        def _silu(x):
            return x * jax.nn.sigmoid(x)
        key = jax.random.key(seed)
        k0, k1, k2, k3 = jax.random.split(key, 4)
        s_in = 1.0 / np.sqrt(D)
        s_inner = 1.0 / np.sqrt(INNER)
        return {'x': jax.random.normal(k0, (B, K, D), dtype=jnp.float32), 'w_norm': jnp.ones((D,), dtype=jnp.float32), 'W_in': (jax.random.normal(k1, (2 * INNER, D)) * s_in).astype(jnp.float32), 'W_dt': (jax.random.normal(k2, (INNER, INNER)) * s_inner).astype(jnp.float32), 'b_dt': jnp.zeros((INNER,), dtype=jnp.float32), 'W_out': (jax.random.normal(k3, (D, INNER)) * s_inner).astype(jnp.float32)}
    _L1_attn_b_in = _L1_attn_b_setup()

    def _L1_ffn_setup():
        import jax, jax.numpy as jnp
        import numpy as np
        EMB = 128
        FF = 4 * EMB

        def _ternary(w):
            scale = jnp.maximum(jnp.mean(jnp.abs(w)), 1e-08)
            w_t = jnp.clip(jnp.round(w / scale), -1.0, 1.0)
            return w + jax.lax.stop_gradient(w_t - w)
        key = jax.random.key(seed)
        kx, k1, k2, kb1, kb2 = jax.random.split(key, 5)
        x = jax.random.normal(kx, (4, 256, EMB), dtype=jnp.float32)
        lim1 = 1.0 / np.sqrt(EMB)
        lim2 = 1.0 / np.sqrt(FF)
        W1 = jax.random.uniform(k1, (FF, EMB), jnp.float32, -lim1, lim1)
        b1 = jax.random.uniform(kb1, (FF,), jnp.float32, -lim1, lim1)
        W2 = jax.random.uniform(k2, (EMB, FF), jnp.float32, -lim2, lim2)
        b2 = jax.random.uniform(kb2, (EMB,), jnp.float32, -lim2, lim2)
        return {'x': x, 'W1': W1, 'b1': b1, 'W2': W2, 'b2': b2}
    _L1_ffn_in = _L1_ffn_setup()
    _d = {'L0_attn_a_x': _L0_attn_a_in['x'], 'L0_attn_a_W_in': _L0_attn_a_in['W_in'], 'L0_attn_a_conv_w': _L0_attn_a_in['conv_w'], 'L0_attn_a_conv_b': _L0_attn_a_in['conv_b'], 'L0_attn_a_W_xproj': _L0_attn_a_in['W_xproj'], 'L0_attn_a_W_dt': _L0_attn_a_in['W_dt'], 'L0_attn_a_b_dt': _L0_attn_a_in['b_dt'], 'L0_attn_a_A_log': _L0_attn_a_in['A_log'], 'L0_attn_a_D_skip': _L0_attn_a_in['D_skip'], 'L0_attn_a_W_out': _L0_attn_a_in['W_out'], 'L0_attn_a_ln_g': _L0_attn_a_in['ln_g'], 'L0_attn_a_ln_b': _L0_attn_a_in['ln_b'], 'L0_attn_b_Wq': _L0_attn_b_in['Wq'], 'L0_attn_b_bq': _L0_attn_b_in['bq'], 'L0_attn_b_Wk': _L0_attn_b_in['Wk'], 'L0_attn_b_bk': _L0_attn_b_in['bk'], 'L0_attn_b_Wv': _L0_attn_b_in['Wv'], 'L0_attn_b_bv': _L0_attn_b_in['bv'], 'L0_attn_b_Wo': _L0_attn_b_in['Wo'], 'L0_attn_b_bo': _L0_attn_b_in['bo'], 'L0_attn_b_gamma': _L0_attn_b_in['gamma'], 'L0_attn_b_beta': _L0_attn_b_in['beta'], 'L0_attn_b_rel_bias': _L0_attn_b_in['rel_bias'], 'L0_ffn_shared_w1': _L0_ffn_in['shared_w1'], 'L0_ffn_shared_b1': _L0_ffn_in['shared_b1'], 'L0_ffn_shared_w2': _L0_ffn_in['shared_w2'], 'L0_ffn_shared_b2': _L0_ffn_in['shared_b2'], 'L0_ffn_router_w': _L0_ffn_in['router_w'], 'L0_ffn_router_b': _L0_ffn_in['router_b'], 'L0_ffn_spec_w1': _L0_ffn_in['spec_w1'], 'L0_ffn_spec_b1': _L0_ffn_in['spec_b1'], 'L0_ffn_spec_w2': _L0_ffn_in['spec_w2'], 'L0_ffn_spec_b2': _L0_ffn_in['spec_b2'], 'L1_attn_a_Wqkv': _L1_attn_a_in['Wqkv'], 'L1_attn_a_Wo': _L1_attn_a_in['Wo'], 'L1_attn_a_bo': _L1_attn_a_in['bo'], 'L1_attn_b_w_norm': _L1_attn_b_in['w_norm'], 'L1_attn_b_W_in': _L1_attn_b_in['W_in'], 'L1_attn_b_W_dt': _L1_attn_b_in['W_dt'], 'L1_attn_b_b_dt': _L1_attn_b_in['b_dt'], 'L1_attn_b_W_out': _L1_attn_b_in['W_out'], 'L1_ffn_W1': _L1_ffn_in['W1'], 'L1_ffn_b1': _L1_ffn_in['b1'], 'L1_ffn_W2': _L1_ffn_in['W2'], 'L1_ffn_b2': _L1_ffn_in['b2']}
    _x0 = _d['L0_attn_a_x']
    _d['L0_attn_a_x'] = jax.random.normal(jax.random.fold_in(jax.random.key(seed), 1), (4, 1024, 128), dtype=_x0.dtype)
    del _x0
    return _d

def reference(L0_attn_a_x, L0_attn_a_W_in, L0_attn_a_conv_w, L0_attn_a_conv_b, L0_attn_a_W_xproj, L0_attn_a_W_dt, L0_attn_a_b_dt, L0_attn_a_A_log, L0_attn_a_D_skip, L0_attn_a_W_out, L0_attn_a_ln_g, L0_attn_a_ln_b, L0_attn_b_Wq, L0_attn_b_bq, L0_attn_b_Wk, L0_attn_b_bk, L0_attn_b_Wv, L0_attn_b_bv, L0_attn_b_Wo, L0_attn_b_bo, L0_attn_b_gamma, L0_attn_b_beta, L0_attn_b_rel_bias, L0_ffn_shared_w1, L0_ffn_shared_b1, L0_ffn_shared_w2, L0_ffn_shared_b2, L0_ffn_router_w, L0_ffn_router_b, L0_ffn_spec_w1, L0_ffn_spec_b1, L0_ffn_spec_w2, L0_ffn_spec_b2, L1_attn_a_Wqkv, L1_attn_a_Wo, L1_attn_a_bo, L1_attn_b_w_norm, L1_attn_b_W_in, L1_attn_b_W_dt, L1_attn_b_b_dt, L1_attn_b_W_out, L1_ffn_W1, L1_ffn_b1, L1_ffn_W2, L1_ffn_b2):

    def _L0_attn_a_ref(x, W_in, conv_w, conv_b, W_xproj, W_dt, b_dt, A_log, D_skip, W_out, ln_g, ln_b):
        import jax, jax.numpy as jnp
        import numpy as np
        BATCH, SEQ, D_MODEL = (2, 512, 128)
        EXPAND, N_HEADS, D_STATE, D_CONV, CHUNK = (2, 16, 16, 4, 64)
        D_INNER = EXPAND * D_MODEL
        HEAD_DIM = D_INNER // N_HEADS
        LN_EPS = 1e-05

        def silu(v):
            return v * jax.nn.sigmoid(v)

        def _forward(x, W_in, conv_w, conv_b, W_xproj, W_dt, b_dt, A_log, D_skip, W_out, ln_g, ln_b):
            b, L, _ = x.shape
            xz = x @ W_in
            xe, z = jnp.split(xz, 2, axis=-1)
            xp = jnp.pad(xe, ((0, 0), (D_CONV - 1, 0), (0, 0)))
            xc = conv_b
            for j in range(D_CONV):
                xc = xc + conv_w[:, j] * xp[:, j:j + L, :]
            xc = silu(xc)
            proj = xc @ W_xproj
            dt_raw = proj[..., :N_HEADS]
            Bm = proj[..., N_HEADS:N_HEADS + D_STATE]
            Cm = proj[..., N_HEADS + D_STATE:]
            dt = jax.nn.softplus(dt_raw @ W_dt + b_dt)
            A = -jnp.exp(A_log)
            xh = xc.reshape(b, L, N_HEADS, HEAD_DIM)
            dth = dt.reshape(b, L, N_HEADS, HEAD_DIM)
            nc = L // CHUNK
            dt_cum = dth.reshape(b, nc, CHUNK, N_HEADS, HEAD_DIM).cumsum(axis=2)
            decay = jnp.exp(A[None, None, None, :, None] * dt_cum).reshape(b, L, N_HEADS, HEAD_DIM)
            xs = (jnp.moveaxis(xh, 1, 0), jnp.moveaxis(dth, 1, 0), jnp.moveaxis(decay, 1, 0), jnp.moveaxis(Bm, 1, 0), jnp.moveaxis(Cm, 1, 0))
            state0 = jnp.zeros((b, N_HEADS, HEAD_DIM, D_STATE), x.dtype)

            def step(state, inp):
                x_t, dt_t, dec_t, B_t, C_t = inp
                state = state * dec_t[..., None] + (dt_t * x_t)[..., None] * B_t[:, None, None, :]
                y_t = jnp.einsum('bhdn,bn->bhd', state, C_t)
                return (state, y_t)
            _, ys = jax.lax.scan(step, state0, xs)
            y = jnp.moveaxis(ys, 0, 1)
            y = y + xh * D_skip[None, None, :, None]
            y = y.reshape(b, L, D_INNER) * silu(z)
            mu = y.mean(-1, keepdims=True)
            var = ((y - mu) ** 2).mean(-1, keepdims=True)
            y = (y - mu) * jax.lax.rsqrt(var + LN_EPS) * ln_g + ln_b
            return y @ W_out
        return _forward(x, W_in, conv_w, conv_b, W_xproj, W_dt, b_dt, A_log, D_skip, W_out, ln_g, ln_b)

    def _L0_attn_b_ref(x, Wq, bq, Wk, bk, Wv, bv, Wo, bo, gamma, beta, rel_bias):
        import jax, jax.numpy as jnp
        import numpy as np
        EMBED_DIM = 128
        NUM_HEADS = 16
        HEAD_DIM = EMBED_DIM // NUM_HEADS
        B, N = (2, 256)
        BIAS_S = 32

        def _interp_matrix(n, s):
            pos = jnp.arange(n, dtype=jnp.float32) * ((s - 1) / (n - 1))
            i0 = jnp.floor(pos).astype(jnp.int32)
            i1 = jnp.minimum(i0 + 1, s - 1)
            frac = pos - i0.astype(jnp.float32)
            rows = jnp.arange(n)
            M = jnp.zeros((n, s), dtype=jnp.float32)
            M = M.at[rows, i0].add(1.0 - frac).at[rows, i1].add(frac)
            return M
        Bx, Nx, C = x.shape
        H, D = (NUM_HEADS, HEAD_DIM)
        scale = 1.0 / jnp.sqrt(jnp.float32(D))
        mu = jnp.mean(x, axis=-1, keepdims=True)
        var = jnp.mean(jnp.square(x - mu), axis=-1, keepdims=True)
        xn = (x - mu) * jax.lax.rsqrt(var + 1e-05) * gamma + beta
        q = (xn @ Wq.T + bq).reshape(Bx, Nx, H, D).transpose(0, 2, 1, 3)
        k = (xn @ Wk.T + bk).reshape(Bx, Nx, H, D).transpose(0, 2, 1, 3)
        v = (xn @ Wv.T + bv).reshape(Bx, Nx, H, D).transpose(0, 2, 1, 3)
        attn = jnp.einsum('bhnd,bhmd->bhnm', q, k) * scale
        M = _interp_matrix(Nx, BIAS_S)
        rel = jnp.einsum('ni,hij,mj->hnm', M, rel_bias, M)
        rel = rel.at[:, -1, :].set(0.0).at[:, :, -1].set(0.0)
        attn = attn + rel[None]
        mask = jnp.triu(jnp.ones((Nx, Nx), dtype=bool), k=1)
        attn = jnp.where(mask, -jnp.inf, attn)
        attn = jax.nn.softmax(attn, axis=-1)
        out = jnp.einsum('bhnm,bhmd->bhnd', attn, v)
        out = out.transpose(0, 2, 1, 3).reshape(Bx, Nx, C)
        out = out @ Wo.T + bo
        return out

    def _L0_ffn_ref(x, shared_w1, shared_b1, shared_w2, shared_b2, router_w, router_b, spec_w1, spec_b1, spec_w2, spec_b2):
        import jax, jax.numpy as jnp
        import numpy as np
        D_MODEL = 128
        D_FF = 512
        N_EXPERTS = 8
        TOP_K = 2

        def _ffn(x, w1, b1, w2, b2):
            h = jax.nn.gelu(x @ w1.T + b1)
            return h @ w2.T + b2
        B, T, D = x.shape
        xf = x.reshape(-1, D)
        U = xf.shape[0]
        logits = xf @ router_w.T + router_b
        routing = jax.nn.softmax(logits, axis=-1)
        sel_w, sel_idx = jax.lax.top_k(routing, TOP_K)
        sel_w = sel_w / sel_w.sum(axis=-1, keepdims=True)
        comb = jnp.zeros_like(routing).at[jnp.arange(U)[:, None], sel_idx].set(sel_w)
        shared_out = _ffn(xf, shared_w1, shared_b1, shared_w2, shared_b2)

        def body(acc, params):
            w1, b1, w2, b2, we = params
            return (acc + we[:, None] * _ffn(xf, w1, b1, w2, b2), None)
        acc0 = jnp.zeros_like(shared_out)
        acc, _ = jax.lax.scan(body, acc0, (spec_w1, spec_b1, spec_w2, spec_b2, comb.T))
        return (shared_out + acc).reshape(B, T, D)

    def _L1_attn_a_ref(x, Wqkv, Wo, bo):
        import math
        import jax, jax.numpy as jnp
        import numpy as np
        B, T, D, H = (4, 256, 128, 16)
        HD = D // H

        def apply_rope(x, base=10000.0):
            _, t, _, dh = x.shape
            half = dh // 2
            inv_freq = 1.0 / base ** (jnp.arange(half, dtype=jnp.float32) / float(half))
            pos = jnp.arange(t, dtype=jnp.float32)
            angles = pos[:, None] * inv_freq[None, :]
            sin = jnp.sin(angles)[None, :, None, :]
            cos = jnp.cos(angles)[None, :, None, :]
            x1 = x[..., :half]
            x2 = x[..., half:2 * half]
            rot1 = x1 * cos - x2 * sin
            rot2 = x1 * sin + x2 * cos
            return jnp.concatenate([rot1, rot2, x[..., 2 * half:]], axis=-1)
        b, t, d = x.shape
        qkv = x @ Wqkv
        q, k, v = jnp.split(qkv, 3, axis=-1)
        q = q.reshape(b, t, H, HD)
        k = k.reshape(b, t, H, HD)
        v = v.reshape(b, t, H, HD)
        q = apply_rope(q)
        k = apply_rope(k)
        q = q / jnp.sqrt(jnp.sum(q * q, axis=-1, keepdims=True) + 1e-06)
        k = k / jnp.sqrt(jnp.sum(k * k, axis=-1, keepdims=True) + 1e-06)
        attn = jnp.einsum('bthd,bshd->bhts', q, k) / math.sqrt(HD)
        attn = jax.nn.softmax(attn, axis=-1)
        out = jnp.einsum('bhts,bshd->bthd', attn, v).reshape(b, t, d)
        return out @ Wo + bo

    def _L1_attn_b_ref(x, w_norm, W_in, W_dt, b_dt, W_out):
        import jax, jax.numpy as jnp
        import numpy as np
        B, K, D = (8, 256, 128)
        INNER = 2 * D
        EPS = 1e-05

        def _silu(x):
            return x * jax.nn.sigmoid(x)
        h = x * jax.lax.rsqrt(jnp.mean(x * x, axis=-1, keepdims=True) + EPS) * w_norm
        uv = jnp.einsum('bkd,ed->bke', h, W_in)
        u, z = (uv[..., :INNER], uv[..., INNER:])
        u = _silu(u)
        lam = jax.nn.sigmoid(jnp.einsum('bki,ji->bkj', u, W_dt) + b_dt)

        def step(s, inp):
            lam_t, u_t = inp
            s = lam_t * s + (1.0 - lam_t) * u_t
            return (s, s)
        lam_k = jnp.moveaxis(lam, 1, 0)
        u_k = jnp.moveaxis(u, 1, 0)
        s0 = jnp.zeros((x.shape[0], INNER), dtype=x.dtype)
        _, ys = jax.lax.scan(step, s0, (lam_k, u_k))
        s = jnp.moveaxis(ys, 0, 1)
        s = s * _silu(z)
        y = jnp.einsum('bki,di->bkd', s, W_out)
        return x + y

    def _L1_ffn_ref(x, W1, b1, W2, b2):
        import jax, jax.numpy as jnp
        import numpy as np
        EMB = 128
        FF = 4 * EMB

        def _ternary(w):
            scale = jnp.maximum(jnp.mean(jnp.abs(w)), 1e-08)
            w_t = jnp.clip(jnp.round(w / scale), -1.0, 1.0)
            return w + jax.lax.stop_gradient(w_t - w)
        h = jnp.einsum('bsd,fd->bsf', x, _ternary(W1)) + b1
        h = jax.nn.gelu(h, approximate=False)
        out = jnp.einsum('bsf,df->bsd', h, _ternary(W2)) + b2
        return out
    x = L0_attn_a_x
    x = x + _L0_attn_a_ref(_layernorm(x, axis=-1), L0_attn_a_W_in, L0_attn_a_conv_w, L0_attn_a_conv_b, L0_attn_a_W_xproj, L0_attn_a_W_dt, L0_attn_a_b_dt, L0_attn_a_A_log, L0_attn_a_D_skip, L0_attn_a_W_out, L0_attn_a_ln_g, L0_attn_a_ln_b)
    x = x + _L0_ffn_ref(_layernorm(x, axis=-1), L0_ffn_shared_w1, L0_ffn_shared_b1, L0_ffn_shared_w2, L0_ffn_shared_b2, L0_ffn_router_w, L0_ffn_router_b, L0_ffn_spec_w1, L0_ffn_spec_b1, L0_ffn_spec_w2, L0_ffn_spec_b2)
    x = x + _L0_attn_b_ref(_layernorm(x, axis=-1), L0_attn_b_Wq, L0_attn_b_bq, L0_attn_b_Wk, L0_attn_b_bk, L0_attn_b_Wv, L0_attn_b_bv, L0_attn_b_Wo, L0_attn_b_bo, L0_attn_b_gamma, L0_attn_b_beta, L0_attn_b_rel_bias)
    x = x + _L0_ffn_ref(_layernorm(x, axis=-1), L0_ffn_shared_w1, L0_ffn_shared_b1, L0_ffn_shared_w2, L0_ffn_shared_b2, L0_ffn_router_w, L0_ffn_router_b, L0_ffn_spec_w1, L0_ffn_spec_b1, L0_ffn_spec_w2, L0_ffn_spec_b2)
    x = x + _L1_attn_a_ref(_layernorm(x, axis=-1), L1_attn_a_Wqkv, L1_attn_a_Wo, L1_attn_a_bo)
    x = x + _L1_ffn_ref(_layernorm(x, axis=-1), L1_ffn_W1, L1_ffn_b1, L1_ffn_W2, L1_ffn_b2)
    x = x + _L1_attn_b_ref(_layernorm(x, axis=-1), L1_attn_b_w_norm, L1_attn_b_W_in, L1_attn_b_W_dt, L1_attn_b_b_dt, L1_attn_b_W_out)
    x = x + _L1_ffn_ref(_layernorm(x, axis=-1), L1_ffn_W1, L1_ffn_b1, L1_ffn_W2, L1_ffn_b2)
    return x

_drawn_inputs = setup_inputs


def setup_inputs(seed=0):
    import zlib

    import numpy as np

    out = dict(_drawn_inputs(seed))
    spreads = {'L0_attn_a_D_skip': (1.0, 0.2),
     'L0_attn_a_ln_g': (1.0, 0.2),
     'L0_attn_a_ln_b': (0.0, 0.1),
     'L0_attn_b_bq': (0.0, 0.8),
     'L0_attn_b_bk': (0.0, 2.0),
     'L0_attn_b_bv': (0.0, 0.418),
     'L0_attn_b_bo': (0.0, 0.1),
     'L0_attn_b_gamma': (1.0, 0.6),
     'L0_attn_b_beta': (0.0, 0.8),
     'L0_ffn_shared_b1': (0.0, 0.1),
     'L0_ffn_shared_b2': (0.0, 0.1),
     'L0_ffn_router_b': (0.0, 0.1),
     'L0_ffn_spec_b1': (0.0, 0.368),
     'L0_ffn_spec_b2': (0.0, 0.1),
     'L1_attn_a_bo': (0.0, 0.1),
     'L1_attn_b_w_norm': (1.0, 0.6),
     'L1_attn_b_b_dt': (0.0, 0.8)}
    factors = {'L0_attn_a_conv_b': 7.65,
     'L0_attn_a_A_log': 6.395,
     'L0_attn_b_Wq': 8.0,
     'L0_attn_b_Wk': 8.0,
     'L0_attn_b_Wv': 8.0,
     'L0_attn_b_Wo': 2.882,
     'L0_attn_b_rel_bias': 8.0,
     'L1_attn_b_W_in': 8.0,
     'L1_attn_b_W_dt': 8.0,
     'L1_attn_b_W_out': 8.0,
     'L1_ffn_b1': 8.0,
     'L1_ffn_b2': 64.0}
    for name, (base, spread) in spreads.items():
        noise = np.random.default_rng([zlib.crc32(name.encode()), seed]).standard_normal(out[name].shape)
        drawn = base * np.exp(spread * noise) if base else spread * noise
        out[name] = jnp.asarray(drawn.astype(out[name].dtype))
    for name, factor in factors.items():
        out[name] = (out[name] * factor).astype(out[name].dtype)
    return out
```

```python
import concourse.bass as bass
import numpy as np
from concourse import mybir
from contextlib import ExitStack

F32 = mybir.dt.float32
F32R = mybir.dt.float32r
U32 = mybir.dt.uint32
ALU = mybir.AluOpType
ACT = mybir.ActivationFunctionType
AX = mybir.AxisListType

P = 128
D = 128
BATCH, SEQ = 4, 1024
TOK = BATCH * SEQ
CH = 512
NCH = TOK // CH
HEADS, HD = 16, 8
EPS = 1e-5


class Phase:

    def __init__(self, nc, ctx, name):
        self.nc, self.ctx, self.name, self.sems = nc, ctx, name, []
        ctx.callback(self.close)

    def close(self):
        if self.sems:
            self.nc.clear_and_free_semaphores(self.sems)
            self.nc.all_engine_barrier()

    def sb(self, name, shape, dt=F32):
        return self.ctx.enter_context(self.nc.sbuf_tensor(f"{self.name}_{name}", shape, dt))

    def ps(self, name, shape=(P, CH)):
        return self.ctx.enter_context(self.nc.psum_tensor(f"{self.name}_{name}", list(shape), F32))

    def sem(self, name):
        self.sems.append(self.nc.alloc_semaphore(f"{self.name}_{name}"))
        return self.sems[-1]


def tok(c, n=CH):
    return bass.ds(c * n, n)


class Norm:
    SUB = CH // P

    def __init__(self, ph, name, consts, banks, rms=False):
        self.rms, self.banks, self.consts, self.G = rms, banks, consts, len(banks)
        self.mean_done = ph.sem(f"{name}_mean_done")
        self.centred_done = ph.sem(f"{name}_centred_done")
        self.squared_done = ph.sem(f"{name}_squared_done")
        self.var_done = ph.sem(f"{name}_var_done")
        self.var_copied = ph.sem(f"{name}_var_copied")
        self.power_done = ph.sem(f"{name}_power_done")
        self.diag_done = ph.sem(f"{name}_diag_done")
        self.spread_done = ph.sem(f"{name}_spread_done")
        self.centred = [None if rms else ph.sb(f"{name}_centred{g}", [P, CH]) for g in range(self.G)]
        self.squared = [ph.sb(f"{name}_squared{g}", [P, CH]) for g in range(self.G)]
        self.diag = [ph.sb(f"{name}_diag{g}", [P, self.SUB, P]) for g in range(self.G)]
        self.var = [ph.sb(f"{name}_var{g}", [P, self.SUB]) for g in range(self.G)]
        self.rsd = [ph.sb(f"{name}_rsd{g}", [P, self.SUB]) for g in range(self.G)]

    def tensor_mean(self, pe, group, g, x):
        pe.matmul(self.banks[g][:], self.consts["mean"][:], x, start=True, stop=True).then_inc(self.mean_done, 1)

    def vector_centre(self, dve, group, g, x):
        dve.wait_ge(self.mean_done, group * self.G + g + 1)
        dve.tensor_tensor(self.centred[g][:], x, self.banks[g][:], ALU.subtract).then_inc(self.centred_done, 1)

    def scalar_square(self, act, group, g, x=None):
        if not self.rms:
            act.wait_ge(self.centred_done, group * self.G + g + 1)
            x = self.centred[g][:]
        act.activation(self.squared[g][:], x, ACT.Square).then_inc(self.squared_done, 1)

    def tensor_var(self, pe, group, g):
        pe.wait_ge(self.squared_done, group * self.G + g + 1)
        for u in range(self.SUB):
            m = pe.matmul(self.banks[g][:, u:u + 1], self.squared[g][:, u * P:(u + 1) * P], self.consts["mean"][:, 0:1],
                          start=True, stop=True)
        m.then_inc(self.var_done, 1)

    def vector_var(self, dve, group, g):
        dve.wait_ge(self.var_done, group * self.G + g + 1)
        dve.tensor_scalar(self.var[g][:], self.banks[g][:, 0:self.SUB], EPS, None, ALU.add).then_inc(self.var_copied, 1)

    def pool_power(self, pool, group, g):
        pool.wait_ge(self.var_copied, group * self.G + g + 1)
        pool.tensor_tensor(self.rsd[g][:], self.var[g][:], self.consts["neg_half"][:, 0:self.SUB], ALU.pow).then_inc(self.power_done, 1)

    def vector_diag(self, dve, group, g):
        dve.wait_ge(self.power_done, group * self.G + g + 1)
        shape = [P, self.SUB, P]
        dve.tensor_tensor(self.diag[g][:], self.consts["ident"][:].unsqueeze(1).to_broadcast(shape),
                          self.rsd[g][:].unsqueeze(2).to_broadcast(shape), ALU.mult).then_inc(self.diag_done, 1)

    def tensor_spread(self, pe, group, g):
        pe.wait_ge(self.diag_done, group * self.G + g + 1)
        pe.matmul(self.banks[g][:], self.consts["ones"][:], self.diag[g][:].rearrange("p u m -> p (u m)"),
                  start=True, stop=True).then_inc(self.spread_done, 1)

    def vector_wait_spread(self, dve, group, g):
        dve.wait_ge(self.spread_done, group * self.G + g + 1)


N_EXP, N_FFN, FF = 8, 9, 512
NF = FF // P


def ffn_setup(nc, ctx, name, w):
    keep = Phase(nc, ctx, name)
    W = {}
    for m in ("w1", "w2"):
        W[m + "_hi"] = keep.sb(m + "_hi", [P, N_FFN * FF], F32R)
        W[m + "_lo"] = keep.sb(m + "_lo", [P, N_FFN * FF], F32R)
    W["b1"] = keep.sb("b1", [P, N_FFN * NF])
    W["b2"] = keep.sb("b2", [P, 1])
    W["eb2"] = keep.sb("eb2", [N_EXP, D])
    W["rw"] = keep.sb("rw", [P, N_EXP])
    W["rb"] = keep.sb("rb", [1, N_EXP])
    W["pick"] = keep.sb("pick", [N_EXP, N_EXP * P], F32R)
    W["iota"] = keep.sb("iota", [P, N_EXP])
    with ExitStack() as c2:
        ph = Phase(nc, c2, name + "_load")
        raw = [ph.sb(f"raw{i}", [P, N_FFN * FF]) for i in range(2)]
        pickf = ph.sb("pickf", [N_EXP, N_EXP * P])
        loaded, small_loaded, hi_done, lo_done = (ph.sem(n) for n in ("loaded", "small_loaded", "hi_done", "lo_done"))
        block = c2.enter_context(nc.Block())

        @block.sync
        def _(sp):
            for i, name in enumerate(("ffn_w1", "ffn_w2")):
                sp.dma_start(raw[i][:], w[name]).then_inc(loaded, 16)
            smalls = [("b1", "ffn_b1"), ("b2", "ffn_b2"), ("eb2", "ffn_eb2"), ("rw", "ffn_rw"), ("rb", "ffn_rb"), ("iota", "iota8")]
            for dst, src in smalls:
                sp.dma_start(W[dst][:], w[src]).then_inc(small_loaded, 16)
            sp.dma_start(pickf[:], w["pick8"]).then_inc(small_loaded, 16)
            sp.wait_ge(small_loaded, 16 * (len(smalls) + 1))
            sp.wait_ge(loaded, 32)

        @block.scalar
        def _(act):
            for i, name in enumerate(("w1", "w2")):
                act.wait_ge(loaded, 32)
                act.activation(W[name + "_hi"][:], raw[i][:], ACT.Copy).then_inc(hi_done, 1)
            act.wait_ge(small_loaded, 16 * 7)
            act.activation(W["pick"][:], pickf[:], ACT.Copy).then_inc(hi_done, 1)

        @block.vector
        def _(dve):
            for i, name in enumerate(("w1", "w2")):
                dve.wait_ge(hi_done, i + 1)
                dve.tensor_tensor(W[name + "_lo"][:], raw[i][:], W[name + "_hi"][:].bitcast(F32), ALU.subtract).then_inc(lo_done, 1)
    return W


def split_matmul(pe, out, w_hi, w_lo, x_hi, x_lo, start, stop):
    pe.matmul(out, w_hi, x_hi, start=start, stop=False)
    pe.matmul(out, w_hi, x_lo, start=False, stop=False)
    return pe.matmul(out, w_lo, x_hi, start=False, stop=stop)


def ffn_phase(nc, name, X, K, W):
    SUB = CH // P
    with ExitStack() as ctx:
        ph = Phase(nc, ctx, name)
        xn = ph.sb("xn", [P, CH])
        xn_hi = [ph.sb(f"xn_hi{i}", [P, CH], F32R) for i in range(2)]
        xn_lo = [ph.sb(f"xn_lo{i}", [P, CH], F32R) for i in range(2)]
        h = [ph.sb(f"h{i}", [P, NF, CH]) for i in range(2)]
        h_hi = [ph.sb(f"h_hi{i}", [P, NF, CH], F32R) for i in range(2)]
        h_lo = [ph.sb(f"h_lo{i}", [P, NF, CH], F32R) for i in range(2)]
        lg = ph.sb("lg", [P, SUB, N_EXP])
        best = ph.sb("best", [P, SUB, 8])
        besti = ph.sb("besti", [P, SUB, 8], U32)
        bestf = ph.sb("bestf", [P, SUB, 8])
        gap = ph.sb("gap", [P, SUB])
        th = ph.sb("th", [P, SUB])
        wt = ph.sb("wt", [P, 2, SUB])
        comb1 = ph.sb("comb1", [P, SUB, N_EXP])
        comb2 = ph.sb("comb2", [P, SUB, N_EXP])
        comb = ph.sb("comb", [P, SUB, N_EXP])
        combT = [ph.sb(f"combT{i}", [N_EXP, CH]) for i in range(2)]
        comb_hi = [ph.sb(f"comb_hi{i}", [N_EXP, CH], F32R) for i in range(2)]
        comb_lo = [ph.sb(f"comb_lo{i}", [N_EXP, CH], F32R) for i in range(2)]
        wide = [ph.sb(f"wide{i}", [P, CH]) for i in range(2)]
        part = [ph.sb(f"part{i}", [P, CH]) for i in range(2)]
        bank_h = [ph.ps(f"bank_h{i}") for i in range(NF)]
        bank_o = [ph.ps(f"bank_o{i}") for i in range(2)]
        bank_prep = ph.ps("bank_prep")
        bank_wide = ph.ps("bank_wide")
        norm = Norm(ph, "norm", K, [bank_prep])
        s = {n: ph.sem(n) for n in (
            "normed", "split_x", "logits", "logits_copied", "best", "besti", "bestf", "gap", "tanh", "weights",
            "picked", "comb", "combT", "combT_copied", "comb_hi", "comb_split", "up", "gelu_hi", "gelu_lo",
            "gelu_lo_pool", "down", "wide", "wide_copied", "weighted", "added", "adding", "shared_added")}
        block = ctx.enter_context(nc.Block())

        def prepare_tensor(pe, c, par, step):
            if step == 0:
                pe.wait_ge(s["comb_hi"], c)
                norm.tensor_mean(pe, c, 0, X[:, tok(c)])
            if step == 1:
                norm.tensor_var(pe, c, 0)
            if step == 2:
                norm.tensor_spread(pe, c, 0)
            if step == 3:
                pe.wait_ge(s["normed"], c + 1)
                for u in range(SUB):
                    out = bank_prep[:, u * N_EXP:(u + 1) * N_EXP]
                    pe.matmul(out, xn[:, u * P:(u + 1) * P], W["rw"][:], start=True, stop=False)
                    m = pe.matmul(out, K["ones_row"][:], W["rb"][:], start=False, stop=True)
                m.then_inc(s["logits"], 1)
            if step == 4:
                pe.wait_ge(s["comb"], c + 1)
                for u in range(SUB):
                    m = pe.transpose(bank_prep[0:N_EXP, u * P:(u + 1) * P], comb[:, u, :], K["ident"][:])
                m.then_inc(s["combT"], 1)

        def prepare_scalar(act, c, par, step):
            if step == 0:
                norm.scalar_square(act, c, 0)
            if step == 1:
                act.wait_ge(s["gap"], c + 1)
                act.activation(th[:], gap[:], ACT.Tanh, scale=0.5).then_inc(s["tanh"], 1)

        def prepare_vector(dve, c, par, step):
            if step == 0:
                norm.vector_centre(dve, c, 0, X[:, tok(c)])
            if step == 1:
                norm.vector_var(dve, c, 0)
            if step == 2:
                norm.vector_diag(dve, c, 0)
            if step == 3:
                norm.vector_wait_spread(dve, c, 0)
                dve.tensor_tensor(xn[:], norm.centred[0][:], bank_prep[:], ALU.mult).then_inc(s["normed"], 1)
                dve.wait_ge(s["normed"], c + 1)
                if not isinstance(c, int):
                    dve.wait_ge(s["up"], (c - 1) * (N_FFN * NF))
                dve.tensor_copy(xn_hi[par][:], xn[:]).then_inc(s["split_x"], 1)
                dve.wait_ge(s["split_x"], 2 * c + 1)
                dve.tensor_tensor(xn_lo[par][:], xn[:], xn_hi[par][:].bitcast(F32), ALU.subtract).then_inc(s["split_x"], 1)
            if step == 4:
                dve.wait_ge(s["logits"], c + 1)
                dve.tensor_copy(lg[:], bank_prep[:, 0:SUB * N_EXP].rearrange("p (u e) -> p u e", u=SUB)).then_inc(s["logits_copied"], 1)
                dve.wait_ge(s["logits_copied"], 1)
                dve.wait_ge(s["logits_copied"], c + 1)
                for u in range(SUB):
                    m = dve.max(best[:, u, :], lg[:, u, :])
                m.then_inc(s["best"], 1)
                dve.wait_ge(s["best"], c + 1)
                dve.tensor_tensor(gap[:], best[:, :, 0], best[:, :, 1], ALU.subtract).then_inc(s["gap"], 1)
                for u in range(SUB):
                    m = dve.max_index(besti[:, u, :], best[:, u, :], lg[:, u, :])
                m.then_inc(s["besti"], 1)
                dve.wait_ge(s["besti"], c + 1)
                dve.tensor_copy(bestf[:], besti[:]).then_inc(s["bestf"], 1)
            if step == 5:
                dve.wait_ge(s["tanh"], c + 1)
                dve.tensor_scalar(wt[:, 0, :], th[:], 0.5, 0.5, ALU.mult, ALU.add)
                dve.tensor_scalar(wt[:, 1, :], th[:], -0.5, 0.5, ALU.mult, ALU.add).then_inc(s["weights"], 1)
                dve.wait_ge(s["weights"], c + 1)
                dve.wait_ge(s["bestf"], c + 1)
                for u in range(SUB):
                    dve.tensor_scalar(comb1[:, u, :], W["iota"][:], bestf[:, u, 0:1], wt[:, 0, u:u + 1], ALU.is_equal, ALU.mult)
                    m = dve.tensor_scalar(comb2[:, u, :], W["iota"][:], bestf[:, u, 1:2], wt[:, 1, u:u + 1], ALU.is_equal, ALU.mult)
                m.then_inc(s["picked"], 1)
                dve.wait_ge(s["picked"], c + 1)
                dve.tensor_tensor(comb[:], comb1[:], comb2[:], ALU.add).then_inc(s["comb"], 1)
            if step == 6:
                dve.wait_ge(s["combT"], c + 1)
                dve.tensor_copy(combT[par][:], bank_prep[0:N_EXP, :]).then_inc(s["combT_copied"], 1)
                dve.tensor_copy(comb_hi[par][:], bank_prep[0:N_EXP, :]).then_inc(s["comb_hi"], 1)
                dve.wait_ge(s["combT_copied"], c + 1)
                dve.wait_ge(s["comb_hi"], c + 1)
                dve.tensor_tensor(comb_lo[par][:], combT[par][:], comb_hi[par][:].bitcast(F32), ALU.subtract).then_inc(s["comb_split"], 1)

        PE_AT, ACT_AT, DVE_AT = {0: 0, 1: 1, 3: 2, 5: 3, 7: 4}, {0: 0, 5: 1}, {0: 0, 1: 1, 2: 2, 3: 3, 5: 4, 6: 5, 7: 6}
        POOL_AT = 1
        AHEAD = {"gelu_hi": NF, "down": 1, "weighted": 2, "added": 1}

        def up(pe, c, par, e):
            n = c * N_FFN + e
            if e == 0:
                pe.wait_ge(s["split_x"], 2 * c + 2)
            for f in range(NF):
                pe.wait_ge(s["gelu_hi"], n * NF + f + 1)
                w = slice(e * FF + f * P, e * FF + (f + 1) * P)
                split_matmul(pe, bank_h[f][:], W["w1_hi"][:, w], W["w1_lo"][:, w], xn_hi[par][:], xn_lo[par][:],
                             True, True).then_inc(s["up"], 1)

        def down(pe, c, par, e):
            n = c * N_FFN + e
            ep = (par + e) % 2
            if e:
                if e == 1:
                    pe.wait_ge(s["comb_split"], c + 1)
                pe.wait_ge(s["wide_copied"], c * N_EXP + e - 1)
                pick = W["pick"][:, (e - 1) * P:e * P]
                pe.matmul(bank_wide[:], pick, comb_hi[par][:], start=True, stop=False)
                pe.matmul(bank_wide[:], pick, comb_lo[par][:], start=False, stop=True).then_inc(s["wide"], 1)
            if e == 0:
                pe.wait_ge(s["weighted"], c * N_EXP - 1 + 2)
            elif e == 1:
                pe.wait_ge(s["weighted"], c * N_EXP + 2)
            elif e == 2:
                pe.wait_ge(s["shared_added"], c + 1)
            else:
                pe.wait_ge(s["weighted"], c * N_EXP + e - 2 + 2)
            out = bank_o[ep][:]
            if e == 0:
                pe.wait_ge(s["comb_split"], c + 1)
                pe.matmul(out, W["eb2"][:], combT[par][:], start=True, stop=False)
            for f in range(NF):
                w = slice((e * NF + f) * D, (e * NF + f + 1) * D)
                if f < NF - 1:
                    pe.wait_ge(s["gelu_lo"], n * (NF - 1) + f + 1)
                else:
                    pe.wait_ge(s["gelu_lo_pool"], n + 1)
                m = split_matmul(pe, out, W["w2_hi"][:, w], W["w2_lo"][:, w], h_hi[ep][:, f, :], h_lo[ep][:, f, :],
                                 f == 0 and e > 0, f == NF - 1)
            m.then_inc(s["down"], 1)

        @block.tensor
        def _(pe):
            def chunk(c, par):
                for e in range(N_FFN + 1):
                    if e < N_FFN:
                        up(pe, c, par, e)
                    if e:
                        down(pe, c, par, e - 1)
                    if e in PE_AT:
                        prepare_tensor(pe, c + 1, 1 - par, PE_AT[e])
            pe.sem_inc(s["down"], AHEAD["down"])
            for step in range(5):
                prepare_tensor(pe, 0, 0, step)
            with pe.Fori(0, NCH // 2) as pair:
                for par in range(2):
                    chunk(pair * 2 + par, par)

        @block.scalar
        def _(act):
            def chunk(c, par):
                for e in range(N_FFN + 1):
                    n = c * N_FFN + e
                    ep = (par + e) % 2
                    if e < N_FFN:
                        for f in range(NF):
                            act.wait_ge(s["up"], n * NF + f + 1)
                            if f == 0:
                                act.wait_ge(s["down"], n - 1 + 1)
                            b1 = W["b1"][:, e * NF + f:e * NF + f + 1]
                            act.activation(h[ep][:, f, :], bank_h[f][:], ACT.Gelu_apprx_tanh, bias=b1)
                            act.activation(h_hi[ep][:, f, :], bank_h[f][:], ACT.Gelu_apprx_tanh, bias=b1).then_inc(s["gelu_hi"], 1)
                    if e >= 2:
                        q = c * N_EXP + e - 2
                        act.wait_ge(s["wide"], q + 1)
                        act.wait_ge(s["weighted"], q - 1 + 2)
                        act.activation(wide[e % 2][:], bank_wide[:], ACT.Copy).then_inc(s["wide_copied"], 1)
                    if e in ACT_AT:
                        prepare_scalar(act, c + 1, 1 - par, ACT_AT[e])
            act.sem_inc(s["gelu_hi"], AHEAD["gelu_hi"])
            for step in range(2):
                prepare_scalar(act, 0, 0, step)
            with act.Fori(0, NCH // 2) as pair:
                for par in range(2):
                    chunk(pair * 2 + par, par)

        @block.vector
        def _(dve):
            def chunk(c, par):
                for e in range(N_FFN + 1):
                    n = c * N_FFN + e
                    ep = (par + e) % 2
                    if e < N_FFN:
                        for f in range(NF - 1):
                            dve.wait_ge(s["gelu_hi"], n * NF + f + 1 + NF)
                            dve.tensor_tensor(h_lo[ep][:, f, :], h[ep][:, f, :], h_hi[ep][:, f, :].bitcast(F32), ALU.subtract).then_inc(s["gelu_lo"], 1)
                    if e == 1:
                        dve.wait_ge(s["down"], n + 1)
                        dve.scalar_tensor_tensor(X[:, tok(c)], bank_o[(par + e - 1) % 2][:], W["b2"][:, 0:1], X[:, tok(c)],
                                                 ALU.add, ALU.add).then_inc(s["shared_added"], 1)
                    if e >= 2:
                        q = c * N_EXP + e - 2
                        dve.wait_ge(s["down"], n + 1)
                        dve.wait_ge(s["wide_copied"], q + 1)
                        dve.wait_ge(s["added"], q - 1 + 1)
                        dve.tensor_tensor(part[e % 2][:], bank_o[(par + e - 1) % 2][:], wide[e % 2][:], ALU.mult).then_inc(s["weighted"], 1)
                    if e in DVE_AT:
                        prepare_vector(dve, c + 1, 1 - par, DVE_AT[e])
            dve.sem_inc(s["weighted"], AHEAD["weighted"])
            for step in range(7):
                prepare_vector(dve, 0, 0, step)
            with dve.Fori(0, NCH // 2) as pair:
                for par in range(2):
                    chunk(pair * 2 + par, par)

        @block.gpsimd
        def _(pool):
            def chunk(c, par):
                for e in range(N_FFN + 1):
                    n = c * N_FFN + e
                    ep = (par + e) % 2
                    if e < N_FFN:
                        pool.wait_ge(s["gelu_hi"], n * NF + NF + NF)
                        pool.tensor_tensor(h_lo[ep][:, NF - 1, :], h[ep][:, NF - 1, :], h_hi[ep][:, NF - 1, :].bitcast(F32), ALU.subtract).then_inc(s["gelu_lo_pool"], 1)
                    if e >= 2:
                        q = c * N_EXP + e - 2
                        pool.wait_ge(s["weighted"], q + 1 + 2)
                        if e == 2:
                            pool.wait_ge(s["shared_added"], c + 1)
                        pool.wait_ge(s["added"], q + 1)
                        pool.sem_inc(s["adding"], 1)
                        pool.tensor_tensor(X[:, tok(c)], X[:, tok(c)], part[e % 2][:], ALU.add).then_inc(s["added"], 1)
                    if e == POOL_AT:
                        norm.pool_power(pool, c + 1, 0)
            pool.sem_inc(s["added"], AHEAD["added"])
            norm.pool_power(pool, 0, 0)
            with pool.Fori(0, NCH // 2) as pair:
                for par in range(2):
                    chunk(pair * 2 + par, par)


def ffn_stage(nc, name, X, K, w):
    with ExitStack() as ctx:
        W = ffn_setup(nc, ctx, name + "_w", w)
        ffn_phase(nc, name, X, K, W)


N_STATE = 16
INNER = 2 * D
CONV = 4
SCAN_CHUNK = 64


def mamba_phase(nc, name, X, K, w):
    G, NH = 2, 2
    AHEAD = 2
    with ExitStack() as ctx:
        ph = Phase(nc, ctx, name)
        w_in = ph.sb("w_in", [P, 4, P])
        conv_w = ph.sb("conv_w", [P, NH, CONV])
        vecs = ph.sb("vecs", [P, 6, NH])
        w_proj = ph.sb("w_proj", [P, NH, P])
        w_dt = ph.sb("w_dt", [HEADS, INNER])
        w_out = ph.sb("w_out", [P, NH, D])
        w_gain = ph.sb("w_gain", [P, NH, D])
        out_bias = ph.sb("out_bias", [P, 1])
        select = ph.sb("select", [P, 2 * N_STATE + 1])
        pick = ph.sb("pick", [P, 2 * N_STATE, P], F32R)
        mean_inner = ph.sb("mean_inner", [P, P])
        restart = ph.sb("restart", [P, SEQ])
        a_exp = ph.sb("a_exp", [P, NH])
        a_neg = ph.sb("a_neg", [P, NH])
        xn = [ph.sb(f"xn{g}", [P, CH]) for g in range(G)]
        xe = ph.sb("xe", [P, NH, CONV - 1 + SEQ])
        z = ph.sb("z", [P, NH, SEQ])
        conv = ph.sb("conv", [P, NH, SEQ])
        xc = ph.sb("xc", [P, NH, SEQ])
        proj_hi = ph.sb("proj_hi", [P, SEQ], F32R)
        proj = ph.sb("proj", [P, SEQ], F32R)
        dt_raw = ph.sb("dt_raw", [HEADS, SEQ])
        v_abs = ph.sb("v_abs", [P, NH, SEQ])
        v_relu = ph.sb("v_relu", [P, NH, SEQ])
        dt = ph.sb("dt", [P, NH, SEQ])
        decay = ph.sb("decay", [P, NH, SEQ])
        u = ph.sb("u", [P, NH, SEQ])
        b_wide = [ph.sb(f"b_wide{i}", [P, SEQ]) for i in range(2)]
        c_wide = [ph.sb(f"c_wide{i}", [P, SEQ]) for i in range(2)]
        drive = [[ph.sb(f"drive{h}", [P, SEQ]) for h in range(NH)]]
        part = [[ph.sb(f"part{h}", [P, SEQ]) for h in range(NH)]]
        var = ph.sb("var", [P, SEQ // P])
        rsd = ph.sb("rsd", [P, SEQ // P])
        neg_half = ph.sb("neg_half", [P, SEQ // P])
        state = [v_relu[:, h, :] for h in range(NH)]
        drive.append([v_abs[:, h, :] for h in range(NH)])
        part.append([dt[:, h, :] for h in range(NH)])
        squared, diag, centred, spread = v_abs, conv, u, c_wide[0]
        bank_y = [ph.ps(f"bank_y{h}", (P, SEQ)) for h in range(NH)]
        bank_b, bank_c = ph.ps("bank_b", (P, SEQ)), ph.ps("bank_c", (P, SEQ))
        cols = [slice(g * CH, (g + 1) * CH) for g in range(G)]
        n1 = Norm(ph, "n1", K, [bank_c[:, cols[g]] for g in range(G)])
        s = {n: ph.sem(n) for n in (
            "loaded", "const", "a_exp", "setup", "bias", "out_bias", "xn", "proj_in", "xe", "z", "conv", "xc", "proj", "proj_hi", "dt_raw",
            "split", "v", "v_abs", "v_relu", "v_exp", "v_log", "dt", "cum", "decay", "u", "b_bank", "c_bank",
            "b_wide", "c_wide", "drive", "state", "part", "summed", "y1", "y2", "mean", "centred", "squared",
            "var", "var_copied", "power", "diag", "spread", "spread_copied", "out", "weighted", "added")}
        block = ctx.enter_context(nc.Block())
        LOADS = ((w_in, "m_win"), (conv_w, "m_conv"), (vecs, "m_vecs"), (w_proj, "m_wproj"), (w_dt, "m_wdt"),
                 (w_out, "m_wout"), (select, "m_select"))
        CONV_B, B_DT, A_LOG, D_SKIP, LN_G, LN_B = range(6)

        @block.sync
        def _(sp):
            for dst, src in LOADS:
                sp.dma_start(dst[:], w[src]).then_inc(s["loaded"], 16)

        @block.tensor
        def _(pe):
            pe.wait_ge(s["loaded"], 16 * len(LOADS))
            for h in range(NH):
                m = pe.matmul(bank_b[:, 0:1], w_out[:, h, :], vecs[:, LN_B, h:h + 1], start=h == 0, stop=h == NH - 1)
            m.then_inc(s["bias"], 1)
            pe.wait_ge(s["setup"], 2)
            pe.wait_ge(s["out_bias"], 1)
            with pe.Fori(0, BATCH) as b:
                for g in range(G):
                    pe.wait_ge(s["added"], b * G)
                    n1.tensor_mean(pe, b, g, X[:, tok(b * G + g)])
                for g in range(G):
                    n1.tensor_var(pe, b, g)
                for g in range(G):
                    n1.tensor_spread(pe, b, g)
                for i, bank in enumerate((*bank_y, bank_b, bank_c)):
                    for g in range(G):
                        pe.wait_ge(s["xn"], b * G + (G if i == 3 else g + 1))
                        m = pe.matmul(bank[:, cols[g]], w_in[:, i, :], xn[g][:], start=True, stop=True)
                    m.then_inc(s["proj_in"], 1)
                for g in range(G):
                    for h in range(NH):
                        pe.wait_ge(s["xc"], b * NH + h + 1)
                        m = pe.matmul(bank_y[0][:, cols[g]], w_proj[:, h, :], xc[:, h, cols[g]], start=h == 0, stop=h == NH - 1)
                m.then_inc(s["proj"], 1)
                pe.wait_ge(s["dt_raw"], b + 1)
                for h, bank in enumerate((bank_b, bank_c)):
                    pe.wait_ge(s["z"], b * NH + h + 1)
                    for g in range(G):
                        m = pe.matmul(bank[:, cols[g]], w_dt[:, h * P:(h + 1) * P], dt_raw[:, cols[g]], start=True, stop=True)
                    m.then_inc(s["v"], 1)

                def broadcast(n):
                    k = b * N_STATE + n
                    for bank, row, bank_done, wide_done in ((bank_b, n, "b_bank", "b_wide"), (bank_c, N_STATE + n, "c_bank", "c_wide")):
                        if n:
                            pe.wait_ge(s[wide_done], k)
                        for g in range(G):
                            m = pe.matmul(bank[:, cols[g]], pick[0:112, row, :], proj[0:112, cols[g]], start=True, stop=True)
                        m.then_inc(s[bank_done], 1)

                pe.wait_ge(s["split"], b + 1)
                pe.wait_ge(s["v_relu"], (b + 1) * NH)
                for n in range(AHEAD):
                    broadcast(n)
                for n in range(N_STATE):
                    if n + AHEAD < N_STATE:
                        broadcast(n + AHEAD)
                    for h in range(NH):
                        pe.wait_ge(s["part"], (b * N_STATE + n) * NH + h + 1)
                        for g in range(G):
                            m = pe.matmul(bank_y[h][:, cols[g]], K["ident"][:], part[n % 2][h][:, cols[g]], start=n == 0, stop=n == N_STATE - 1)
                        m.then_inc(s["summed"], 1)
                for g in range(G):
                    for h in range(NH):
                        pe.wait_ge(s["y2"], b * NH + h + 1)
                        m = pe.matmul(bank_b[:, cols[g]], mean_inner[:], conv[:, h, cols[g]], start=h == 0, stop=h == NH - 1)
                    m.then_inc(s["mean"], 1)
                for t in range(SEQ // P):
                    for h in range(NH):
                        pe.wait_ge(s["squared"], b * NH * G + (t * P // CH) * NH + h + 1)
                        m = pe.matmul(bank_c[:, t:t + 1], squared[:, h, t * P:(t + 1) * P], mean_inner[:, 0:1], start=h == 0, stop=h == NH - 1)
                m.then_inc(s["var"], 1)
                for g in range(G):
                    for h in range(NH):
                        pe.wait_ge(s["centred"], b * NH * G + g * NH + h + 1)
                        m = pe.matmul(bank_b[:, cols[g]], w_gain[:, h, :], centred[:, h, cols[g]], start=h == 0, stop=h == NH - 1)
                    m.then_inc(s["out"], 1)
                pe.wait_ge(s["diag"], b + 1)
                for g in range(G):
                    pe.matmul(bank_c[:, cols[g]], K["ones"][:], diag[:, 0, cols[g]], start=True, stop=True).then_inc(s["spread"], 1)

        @block.scalar
        def _(act):
            act.wait_ge(s["loaded"], 16 * len(LOADS))
            act.activation(a_exp[:], vecs[:, A_LOG, :], ACT.Exp).then_inc(s["a_exp"], 1)
            act.wait_ge(s["a_exp"], 1)
            act.activation(a_neg[:], a_exp[:], ACT.Copy, scale=-1.0).then_inc(s["a_exp"], 1)
            act.wait_ge(s["bias"], 1)
            act.activation(out_bias[:], bank_b[:, 0:1], ACT.Copy).then_inc(s["out_bias"], 1)
            act.wait_ge(s["a_exp"], 2)
            act.wait_ge(s["const"], 1)
            with act.Fori(0, BATCH) as b:
                for g in range(G):
                    n1.scalar_square(act, b, g)
                for h in range(NH):
                    act.wait_ge(s["proj_in"], b * 4 + h + 1)
                    act.activation(xe[:, h, CONV - 1:], bank_y[h][:], ACT.Copy).then_inc(s["xe"], 1)
                for h, bank in enumerate((bank_b, bank_c)):
                    act.wait_ge(s["proj_in"], b * 4 + 2 + h + 1)
                    act.activation(z[:, h, :], bank[:], ACT.Silu).then_inc(s["z"], 1)
                for h in range(NH):
                    act.wait_ge(s["conv"], (b * CONV + CONV - 1) * NH + h + 1)
                    act.activation(xc[:, h, :], conv[:, h, :], ACT.Silu).then_inc(s["xc"], 1)
                act.wait_ge(s["proj"], b + 1)
                act.activation(dt_raw[:], bank_y[0][0:HEADS, :], ACT.Copy).then_inc(s["dt_raw"], 1)
                act.activation(proj_hi[:], bank_y[0][:], ACT.Copy).then_inc(s["proj_hi"], 1)
                for h, bank in enumerate((bank_b, bank_c)):
                    act.wait_ge(s["v"], b * NH + h + 1)
                    act.activation(v_abs[:, h, :], bank[:], ACT.Abs, bias=vecs[:, B_DT, h:h + 1]).then_inc(s["v_abs"], 1)
                    act.activation(v_relu[:, h, :], bank[:], ACT.Relu, bias=vecs[:, B_DT, h:h + 1]).then_inc(s["v_relu"], 1)
                for h in range(NH):
                    act.wait_ge(s["v_abs"], b * NH + h + 1)
                    act.activation(v_abs[:, h, :], v_abs[:, h, :], ACT.Exp, scale=-1.0).then_inc(s["v_exp"], 1)
                for h in range(NH):
                    act.wait_ge(s["v_exp"], b * NH + h + 1)
                    act.activation(v_abs[:, h, :], v_abs[:, h, :], ACT.Ln, bias=K["ones"][:, 0:1]).then_inc(s["v_log"], 1)
                for h in range(NH):
                    act.wait_ge(s["cum"], b * NH + h + 1)
                    act.activation(decay[:, h, :], decay[:, h, :], ACT.Exp, scale=a_neg[:, h:h + 1]).then_inc(s["decay"], 1)
                for n in range(N_STATE):
                    k = b * N_STATE + n
                    act.wait_ge(s["b_bank"], k + 1)
                    if n >= 2:
                        act.wait_ge(s["drive"], (k - 1) * NH)
                    act.activation(b_wide[n % 2][:], bank_b[:], ACT.Copy).then_inc(s["b_wide"], 1)
                    act.wait_ge(s["c_bank"], k + 1)
                    if n >= 2:
                        act.wait_ge(s["part"], (k - 1) * NH)
                    act.activation(c_wide[n % 2][:], bank_c[:], ACT.Copy).then_inc(s["c_wide"], 1)
                for g in range(G):
                    for h in range(NH):
                        act.wait_ge(s["centred"], b * NH * G + g * NH + h + 1)
                        act.activation(squared[:, h, cols[g]], centred[:, h, cols[g]], ACT.Square).then_inc(s["squared"], 1)
                for g in range(G):
                    act.wait_ge(s["spread"], b * G + g + 1)
                    act.activation(spread[:, cols[g]], bank_c[:, cols[g]], ACT.Copy).then_inc(s["spread_copied"], 1)

        @block.vector
        def _(dve):
            dve.wait_ge(s["loaded"], 16 * len(LOADS))
            shape = [P, 2 * N_STATE, P]
            dve.tensor_copy(pick[:], select[:, 0:2 * N_STATE].unsqueeze(2).to_broadcast(shape)).then_inc(s["setup"], 1)
            for h in range(NH):
                m = dve.tensor_scalar(w_gain[:, h, :], w_out[:, h, :], vecs[:, LN_G, h:h + 1], None, ALU.mult)
            m.then_inc(s["setup"], 1)
            dve.wait_ge(s["const"], 1)
            dve.wait_ge(s["out_bias"], 1)
            with dve.Fori(0, BATCH) as b:
                for g in range(G):
                    n1.vector_centre(dve, b, g, X[:, tok(b * G + g)])
                for g in range(G):
                    n1.vector_var(dve, b, g)
                for g in range(G):
                    n1.vector_diag(dve, b, g)
                for g in range(G):
                    n1.vector_wait_spread(dve, b, g)
                    dve.tensor_tensor(xn[g][:], n1.centred[g][:], bank_c[:, cols[g]], ALU.mult).then_inc(s["xn"], 1)
                for j in range(CONV):
                    for h in range(NH):
                        if j == 0:
                            dve.wait_ge(s["xe"], b * NH + h + 1)
                            dve.tensor_scalar(conv[:, h, :], xe[:, h, 0:SEQ], conv_w[:, h, 0:1], vecs[:, CONV_B, h:h + 1],
                                              ALU.mult, ALU.add).then_inc(s["conv"], 1)
                        else:
                            dve.wait_ge(s["conv"], (b * CONV + j - 1) * NH + h + 1)
                            dve.scalar_tensor_tensor(conv[:, h, :], xe[:, h, j:j + SEQ], conv_w[:, h, j:j + 1], conv[:, h, :],
                                                     ALU.mult, ALU.add).then_inc(s["conv"], 1)
                dve.wait_ge(s["proj_hi"], b + 1)
                dve.scalar_tensor_tensor(proj[:], proj_hi[:].bitcast(F32), select[:, 2 * N_STATE:], bank_y[0][:], ALU.mult, ALU.add).then_inc(s["split"], 1)
                for h in range(NH):
                    dve.wait_ge(s["v_log"], b * NH + h + 1)
                    dve.tensor_tensor(dt[:, h, :], v_relu[:, h, :], v_abs[:, h, :], ALU.add).then_inc(s["dt"], 1)
                for h in range(NH):
                    dve.wait_ge(s["dt"], b * NH + h + 1)
                    dve.tensor_tensor_scan(decay[:, h, :], restart[:], dt[:, h, :], 0.0, ALU.mult, ALU.add).then_inc(s["cum"], 1)
                for h in range(NH):
                    dve.tensor_tensor(u[:, h, :], dt[:, h, :], xc[:, h, :], ALU.mult).then_inc(s["u"], 1)
                for n in range(N_STATE):
                    k = b * N_STATE + n
                    for h in range(NH):
                        dve.wait_ge(s["decay"], b * NH + h + 1)
                        dve.wait_ge(s["drive"], k * NH + h + 1)
                        dve.wait_ge(s["part"], k * NH)
                        dve.tensor_tensor_scan(state[h][:], decay[:, h, :], drive[n % 2][h][:], 0.0, ALU.mult, ALU.add).then_inc(s["state"], 1)
                    for h in range(NH):
                        dve.wait_ge(s["c_wide"], k + 1)
                        if n >= 2:
                            dve.wait_ge(s["summed"], (k - 2) * NH + h + 1)
                        dve.wait_ge(s["state"], k * NH + h + 1)
                        dve.tensor_tensor(part[n % 2][h][:], state[h][:], c_wide[n % 2][:], ALU.mult).then_inc(s["part"], 1)
                for h in range(NH):
                    dve.wait_ge(s["summed"], (b + 1) * N_STATE * NH - NH + h + 1)
                    dve.scalar_tensor_tensor(state[h][:], xc[:, h, :], vecs[:, D_SKIP, h:h + 1], bank_y[h][:], ALU.mult, ALU.add).then_inc(s["y1"], 1)
                for h in range(NH):
                    dve.wait_ge(s["y1"], b * NH + h + 1)
                    dve.tensor_tensor(conv[:, h, :], state[h][:], z[:, h, :], ALU.mult).then_inc(s["y2"], 1)
                for g in range(G):
                    for h in range(NH):
                        dve.wait_ge(s["mean"], b * G + g + 1)
                        dve.tensor_tensor(centred[:, h, cols[g]], conv[:, h, cols[g]], bank_b[:, cols[g]], ALU.subtract).then_inc(s["centred"], 1)
                dve.wait_ge(s["var"], b + 1)
                dve.tensor_scalar(var[:], bank_c[:, 0:SEQ // P], EPS, None, ALU.add).then_inc(s["var_copied"], 1)
                dve.wait_ge(s["power"], b + 1)
                shape = [P, SEQ // P, P]
                dve.tensor_tensor(diag[:, 0, :].rearrange("p (t m) -> p t m", m=P), K["ident"][:].unsqueeze(1).to_broadcast(shape),
                                  rsd[:].unsqueeze(2).to_broadcast(shape), ALU.mult).then_inc(s["diag"], 1)
                for g in range(G):
                    dve.wait_ge(s["spread_copied"], b * G + g + 1)
                    dve.wait_ge(s["out"], b * G + g + 1)
                    dve.tensor_tensor(state[g][:, 0:CH], bank_b[:, cols[g]], spread[:, cols[g]], ALU.mult).then_inc(s["weighted"], 1)
                for g in range(G):
                    dve.wait_ge(s["weighted"], b * G + g + 1)
                    dve.scalar_tensor_tensor(X[:, tok(b * G + g)], state[g][:, 0:CH], out_bias[:, 0:1], X[:, tok(b * G + g)],
                                             ALU.add, ALU.add).then_inc(s["added"], 1)

        @block.gpsimd
        def _(pool):
            pool.memset(mean_inner[:], 1.0 / INNER)
            pool.memset(neg_half[:], -0.5)
            pool.memset(xe[:, :, 0:CONV - 1], 0.0)
            pool.memset(restart[:].rearrange("p (t m) -> p t m", m=SCAN_CHUNK)[:, :, 0:1], 0.0)
            pool.memset(restart[:].rearrange("p (t m) -> p t m", m=SCAN_CHUNK)[:, :, 1:], 1.0).then_inc(s["const"], 1)
            with pool.Fori(0, BATCH) as b:
                for g in range(G):
                    n1.pool_power(pool, b, g)
                for n in range(N_STATE):
                    k = b * N_STATE + n
                    for h in range(NH):
                        pool.wait_ge(s["u"], b * NH + h + 1)
                        pool.wait_ge(s["b_wide"], k + 1)
                        if n >= 2:
                            pool.wait_ge(s["state"], (k - 2) * NH + h + 1)
                        pool.tensor_tensor(drive[n % 2][h][:], u[:, h, :], b_wide[n % 2][:], ALU.mult).then_inc(s["drive"], 1)
                pool.wait_ge(s["var_copied"], b + 1)
                pool.tensor_tensor(rsd[:], var[:], neg_half[:], ALU.pow).then_inc(s["power"], 1)


QUADS = HEADS // 4
NSTEP = QUADS * BATCH
NT = SEQ // P
GRID = 32
NEG = -1e30
REL, QK = 3 * GRID, 3 * HD
ROWS_A = REL + QK
ROWS_B = ROWS_A + 2


def attnb_phase(nc, name, X, K, w):
    q_dram = nc.dram_tensor(f"{name}_q", (NSTEP, 4, 2 * HD, SEQ), F32, kind="Internal").ap()
    k_dram = nc.dram_tensor(f"{name}_k", (NSTEP, 4, 2 * HD, SEQ), F32, kind="Internal").ap()
    rel_dram = nc.dram_tensor(f"{name}_rel", (QUADS, 4, REL, SEQ), F32, kind="Internal").ap()
    o_dram = nc.dram_tensor(f"{name}_o", (NSTEP + 1, 64, SEQ), F32, kind="Internal").ap()
    with ExitStack() as ctx:
        keep = Phase(nc, ctx, name)
        V = keep.sb("V", [P, BATCH * NT, D])
        grid_k = keep.sb("grid_k", [REL, SEQ], F32R)
        attnb_rel(nc, name, w, rel_dram, grid_k)
        attnb_project(nc, name, X, K, w, q_dram, k_dram, V)
        attnb_scores(nc, name, K, w, q_dram, k_dram, rel_dram, grid_k, V, o_dram)
        attnb_out(nc, name, X, w, o_dram)


def attnb_rel(nc, name, w, rel_dram, grid_k):
    with ExitStack() as ctx:
        ph = Phase(nc, ctx, name + "r")
        grid = ph.sb("grid", [REL, SEQ])
        biases = ph.sb("biases", [GRID, HEADS, REL])
        masks = ph.sb("masks", [REL, 2])
        grid_high = ph.sb("grid_high", [REL, SEQ], F32R)
        high = [ph.sb(f"high{p}", [REL, SEQ], F32R) for p in range(2)]
        rows = [ph.sb(f"rows{p}", [REL, SEQ], F32R) for p in range(2)]
        bias = [ph.sb(f"bias{p}", [GRID, REL]) for p in range(2)]
        bank = [ph.ps(f"bank{p}", (P, SEQ)) for p in range(2)]
        loaded, picked, made, grid_high_done, high_done, rows_done, grid_done, stored0, stored1 = (ph.sem(n) for n in (
            "loaded", "picked", "made", "grid_high_done", "high_done", "rows_done", "grid_done", "stored0", "stored1"))
        stored = [stored0, stored1]
        block = ctx.enter_context(nc.Block())

        @block.sync
        def _(sp):
            sp.dma_start(grid[:], w["grid3"]).then_inc(loaded, 16)
            sp.dma_start(biases[:], w["ab_rel"].rearrange("p (h r) -> p h r", h=HEADS)).then_inc(loaded, 16)
            sp.dma_start(masks[:], w["negmask"]).then_inc(loaded, 16)
            with sp.Fori(0, HEADS // 2) as pair:
                for p in range(2):
                    h = pair * 2 + p
                    sp.wait_ge(rows_done, h + 1)
                    sp.dma_start(rel_dram.rearrange("q g r t -> (q g) r t")[bass.ds(h, 1), :, :], rows[p][:].bitcast(F32)).then_inc(stored[p], 16)
            for p in range(2):
                sp.wait_ge(stored[p], 16 * HEADS // 2)

        @block.tensor
        def _(pe):
            pe.wait_ge(loaded, 48)
            with pe.Fori(0, HEADS // 2) as pair:
                for p in range(2):
                    h = pair * 2 + p
                    pe.wait_ge(picked, h + 1)
                    if p == 0:
                        pe.wait_ge(rows_done, h)
                    for half in range(2):
                        n = slice(half * CH, (half + 1) * CH)
                        m = pe.matmul(bank[p][0:REL, n], bias[p][:], grid[0:GRID, n], start=True, stop=True)
                    m.then_inc(made, 1)

        @block.scalar
        def _(act):
            act.wait_ge(loaded, 48)
            act.activation(grid_high[:], grid[:], ACT.Copy).then_inc(grid_high_done, 1)
            with act.Fori(0, HEADS // 2) as pair:
                for p in range(2):
                    h = pair * 2 + p
                    act.wait_ge(made, h + 1)
                    act.activation(high[p][:], bank[p][0:REL, :], ACT.Copy).then_inc(high_done, 1)

        @block.vector
        def _(dve):
            dve.wait_ge(loaded, 48)
            dve.wait_ge(grid_high_done, 1)
            dve.scalar_tensor_tensor(grid_k[:], grid_high[:].bitcast(F32), masks[:, 1:2], grid[:], ALU.mult, ALU.add).then_inc(grid_done, 1)
            with dve.Fori(0, HEADS // 2) as pair:
                for p in range(2):
                    dve.wait_ge(made, pair * 2)
                    dve.tensor_copy(bias[p][:], biases[:, bass.ds(pair * 2 + p, 1), :]).then_inc(picked, 1)
                for p in range(2):
                    h = pair * 2 + p
                    dve.wait_ge(high_done, h + 1)
                    dve.wait_ge(stored[p], pair * 16)
                    dve.scalar_tensor_tensor(rows[p][:], high[p][:].bitcast(F32), masks[:, 0:1], bank[p][0:REL, :], ALU.mult, ALU.add).then_inc(rows_done, 1)


def attnb_project(nc, name, X, K, w, q_dram, k_dram, V):
    SUB = CH // P
    G = 2
    with ExitStack() as ctx:
        ph = Phase(nc, ctx, name + "p")
        wqk = [ph.sb("wq", [P, D]), ph.sb("wk", [P, D])]
        wv = ph.sb("wv", [P, D])
        vecs = ph.sb("vecs", [P, 4])
        bv = ph.sb("bv", [1, D])
        x1 = [ph.sb(f"x1{g}", [P, CH]) for g in range(G)]
        x2 = [ph.sb(f"x2{g}", [P, CH]) for g in range(G)]
        xg = [ph.sb(f"xg{g}", [P, CH]) for g in range(G)]
        whole = [ph.sb(f"whole{i}", [P, CH]) for i in range(2)]
        hi = [[ph.sb(f"hi{i}{p}", [P, CH], F32R) for i in range(2)] for p in range(G)]
        lo = [[ph.sb(f"lo{i}{p}", [P, CH], F32R) for i in range(2)] for p in range(G)]
        bank1, bank2 = [[ph.ps(f"bank{n}{g}") for g in range(G)] for n in range(2)]
        bank_qk = [ph.ps(f"bank_qk{i}") for i in range(2)]
        bank_v = [ph.ps(f"bank_v{g}") for g in range(G)]
        n1, n2 = Norm(ph, "n1", K, bank1), Norm(ph, "n2", K, bank2)
        s = {n: ph.sem(n) for n in ("loaded", "x1", "x2", "gained", "qk", "v", "v_copied", "whole", "hi", "lo", "stored0", "stored1")}
        stored = [s["stored0"], s["stored1"]]
        block = ctx.enter_context(nc.Block())
        scale = [float(np.float32(1) / np.sqrt(np.float32(HD))), 1.0]

        @block.sync
        def _(sp):
            for dst, src in ((wqk[0], "ab_wq"), (wqk[1], "ab_wk"), (wv, "ab_wv"), (vecs, "ab_vecs"), (bv, "ab_bv")):
                sp.dma_start(dst[:], w[src]).then_inc(s["loaded"], 16)
            with sp.Fori(0, BATCH) as b:
                for g in range(G):
                    c = b * G + g
                    for i, dram in enumerate((q_dram, k_dram)):
                        sp.wait_ge(s["lo"], c * 2 + i + 1)
                        for part, src in enumerate((hi, lo)):
                            for quad in range(QUADS):
                                dst = dram[bass.ds(b + quad * BATCH, 1), :, part * HD:(part + 1) * HD, g * CH:(g + 1) * CH]
                                sp.dma_start(dst.rearrange("o g d t -> (o g) d t"), src[g][i][32 * quad:32 * quad + 32, :].bitcast(F32)).then_inc(stored[g], 16)
            for g in range(G):
                sp.wait_ge(stored[g], 16 * 16 * BATCH)

        @block.tensor
        def _(pe):
            pe.wait_ge(s["loaded"], 80)
            with pe.Fori(0, BATCH) as b:
                for g in range(G):
                    n1.tensor_mean(pe, b, g, X[:, tok(b * G + g)])
                for g in range(G):
                    n1.tensor_var(pe, b, g)
                for g in range(G):
                    n1.tensor_spread(pe, b, g)
                for g in range(G):
                    pe.wait_ge(s["x1"], b * G + g + 1)
                    n2.tensor_mean(pe, b, g, x1[g][:])
                for g in range(G):
                    n2.tensor_var(pe, b, g)
                for g in range(G):
                    n2.tensor_spread(pe, b, g)
                for g in range(G):
                    c = b * G + g
                    pe.wait_ge(s["gained"], c + 1)
                    for i in range(2):
                        pe.wait_ge(s["whole"], c * 2 + i)
                        pe.matmul(bank_qk[i][:], wqk[i][:], xg[g][:], start=True, stop=True).then_inc(s["qk"], 1)
                    for u in range(SUB):
                        out = bank_v[g][:, u * D:(u + 1) * D]
                        pe.matmul(out, xg[g][:, u * P:(u + 1) * P], wv[:], start=True, stop=False)
                        m = pe.matmul(out, K["ones_row"][:], bv[:], start=False, stop=True)
                    m.then_inc(s["v"], 1)

        @block.scalar
        def _(act):
            act.wait_ge(s["loaded"], 80)
            with act.Fori(0, BATCH) as b:
                for n in (n1, n2):
                    for g in range(G):
                        n.scalar_square(act, b, g)
                for g in range(G):
                    c = b * G + g
                    act.wait_ge(s["v"], c + 1)
                    act.activation(V[:, bass.ds(c * SUB, SUB), :], bank_v[g][:].rearrange("p (u d) -> p u d", u=SUB), ACT.Copy).then_inc(s["v_copied"], 1)

        @block.gpsimd
        def _(pool):
            with pool.Fori(0, BATCH) as b:
                for n in (n1, n2):
                    for g in range(G):
                        n.pool_power(pool, b, g)

        @block.vector
        def _(dve):
            dve.wait_ge(s["loaded"], 80)
            with dve.Fori(0, BATCH) as b:
                for g in range(G):
                    n1.vector_centre(dve, b, g, X[:, tok(b * G + g)])
                for g in range(G):
                    n1.vector_var(dve, b, g)
                for g in range(G):
                    n1.vector_diag(dve, b, g)
                for g in range(G):
                    n1.vector_wait_spread(dve, b, g)
                    dve.tensor_tensor(x1[g][:], n1.centred[g][:], bank1[g][:], ALU.mult).then_inc(s["x1"], 1)
                for g in range(G):
                    dve.wait_ge(s["x1"], b * G + g + 1)
                    n2.vector_centre(dve, b, g, x1[g][:])
                for g in range(G):
                    n2.vector_var(dve, b, g)
                for g in range(G):
                    n2.vector_diag(dve, b, g)
                for g in range(G):
                    n2.vector_wait_spread(dve, b, g)
                    dve.scalar_tensor_tensor(x2[g][:], n2.centred[g][:], vecs[:, 2:3], bank2[g][:], ALU.mult, ALU.mult).then_inc(s["x2"], 1)
                for g in range(G):
                    c = b * G + g
                    dve.wait_ge(s["x2"], c + 1)
                    dve.tensor_scalar(xg[g][:], x2[g][:], vecs[:, 3:4], None, ALU.add).then_inc(s["gained"], 1)
                for g in range(G):
                    c = b * G + g
                    dve.wait_ge(s["lo"], c * 2)
                    for i in range(2):
                        dve.wait_ge(s["qk"], c * 2 + i + 1)
                        dve.tensor_scalar(whole[i][:], bank_qk[i][:], vecs[:, i:i + 1], scale[i], ALU.add, ALU.mult).then_inc(s["whole"], 1)
                    for i in range(2):
                        dve.wait_ge(s["whole"], c * 2 + i + 1)
                        dve.wait_ge(stored[g], b * 256)
                        dve.tensor_copy(hi[g][i][:], whole[i][:]).then_inc(s["hi"], 1)
                    for i in range(2):
                        dve.wait_ge(s["hi"], c * 2 + i + 1)
                        dve.tensor_tensor(lo[g][i][:], whole[i][:], hi[g][i][:].bitcast(F32), ALU.subtract).then_inc(s["lo"], 1)


def attnb_scores(nc, name, K, w, q_dram, k_dram, rel_dram, grid_k, V, o_dram):
    HI, LO = 0, 1
    RING = 3
    with ExitStack() as ctx:
        ph = Phase(nc, ctx, name + "s")
        QA = [ph.sb(f"QA{p}", [ROWS_B, 4, SEQ], F32R) for p in range(2)]
        KA = [ph.sb(f"KA{p}", [ROWS_B, 4, SEQ], F32R) for p in range(2)]
        VA = [ph.sb(f"VA{p}", [P, NT, 4, 32]) for p in range(2)]
        PT = [[ph.sb(f"PT{r}{g}", [P, CH]) for g in range(4)] for r in range(RING)]
        sums = ph.sb("sums", [P, SEQ])
        res = ph.sb("res", [64, SEQ])
        halves = ph.sb("halves", [P, 4, NT, 2])
        mx = ph.sb("mx", [P, 4, NT])
        nm = ph.sb("nm", [P, 4, 4, NT])
        nm_hi = ph.sb("nm_hi", [P, 4, NT], F32R)
        nmT = ph.sb("nmT", [2 * 4 * NT, P])
        ident_r = ph.sb("ident_r", [P, P], F32R)
        masks = ph.sb("masks", [P, 2, P])
        masks_r = ph.sb("masks_r", [P, 2, P], F32R)
        ones2 = ph.sb("ones2", [2, SEQ], F32R)
        sel = ph.sb("sel", [P, 64])
        bank_a = [ph.ps(f"bank_a{r}") for r in range(RING)]
        bank_b = [ph.ps(f"bank_b{r}") for r in range(RING)]
        bank_o = ph.ps("bank_o", (P, SEQ))
        s = {n: ph.sem(n) for n in ("const", "consts", "filled", "loaded00", "loaded01", "loaded10", "loaded11", "tile", "maxed", "nm_hi", "nm", "nmT", "nmT_copied",
                                    "maxima_loaded", "st", "exp", "pv", "cleared", "va", "sums", "sel", "res", "stored", "mx", "mx_clear")}
        loaded = [[s[f"loaded{p}{half}"] for half in range(2)] for p in range(2)]
        block = ctx.enter_context(nc.Block())

        groups = [(t, half) for t in range(NT) for half in range(t // 4, 2)]
        pieces = [(t, half, g) for t in range(NT) for half in range(t // 4 + 1) for g in range(4)]
        NGROUP, NPIECE = len(groups), len(pieces)
        NUNIT = NGROUP * 4
        FIRST_HALF = NT // 2 * 4
        A_UNITS = 38
        TRANSPOSE_AT, SELECT_AT = A_UNITS + 2, A_UNITS + 5
        slots = [list(enumerate(pieces))[NPIECE * u // A_UNITS:NPIECE * (u + 1) // A_UNITS] if u < A_UNITS else [] for u in range(NUNIT)]

        def load(sp, quad, b, i, half):
            p, n = b % 2, slice(half * CH, (half + 1) * CH)
            if b >= 2:
                sp.sem_inc(loaded[p][half], 16)
            else:
                sp.dma_start(QA[p][0:REL, :, n].bitcast(F32), rel_dram[bass.ds(quad, 1), :, :, n].rearrange("o g r t -> (o r) g t")).then_inc(loaded[p][half], 16)
            q = q_dram[bass.ds(i, 1), :, :, n].rearrange("o g r t -> (o r) g t")
            k = k_dram[bass.ds(i, 1), :, :, n].rearrange("o g r t -> (o r) g t")
            sp.dma_start(QA[p][REL:REL + 2 * HD, :, n].bitcast(F32), q).then_inc(loaded[p][half], 16)
            sp.dma_start(QA[p][REL + 2 * HD:ROWS_A, :, n].bitcast(F32), q[0:HD]).then_inc(loaded[p][half], 16)
            sp.dma_start(KA[p][REL:REL + HD, :, n].bitcast(F32), k[0:HD]).then_inc(loaded[p][half], 16)
            sp.dma_start(KA[p][REL + HD:ROWS_A, :, n].bitcast(F32), k).then_inc(loaded[p][half], 16)

        def loaded_count(pair):
            return (pair + 1) * 5 * 16

        @block.sync
        def _(sp):
            sp.dma_start(masks[:], w["causal"].rearrange("p (a m) -> p a m", a=2)).then_inc(s["const"], 16)
            sp.dma_start(sel[:], w["sel_b"]).then_inc(s["const"], 16)
            sp.wait_ge(s["consts"], 3)
            for p in range(2):
                for g in range(4):
                    sp.dma_start(KA[p][0:REL, g, :].bitcast(F32), grid_k[:].bitcast(F32)).then_inc(s["filled"], 16)
                    sp.dma_start(KA[p][ROWS_A:ROWS_B, g, :].bitcast(F32), ones2[:].bitcast(F32)).then_inc(s["filled"], 16)
            for b in range(2):
                for half in range(2):
                    load(sp, 0, b, b, half)

            def maxima(i, p):
                sp.wait_ge(s["nmT_copied"], i + 1)
                sp.dma_start(QA[p][ROWS_A:ROWS_B, :, :].rearrange("o g (t m) -> o (g t) m", t=NT).bitcast(F32),
                             nmT[:]).then_inc(s["maxima_loaded"], 16)

            def store(i):
                sp.wait_ge(s["res"], i + 1)
                sp.dma_start(o_dram[bass.ds(i, 1), :, :], res[:]).then_inc(s["stored"], 16)

            def step(quad, b, last):
                i = quad * BATCH + b
                if not (last and b >= 2):
                    sp.wait_ge(s["st"], i * NUNIT + NUNIT * 2 // 3)
                    load(sp, quad + (b + 2) // 4, (b + 2) % 4, i + 2, 0)
                if not (last and b == 3):
                    maxima(i + 1, (b + 1) % 2)
                store(i)
                if not (last and b >= 2):
                    sp.wait_ge(s["st"], (i + 1) * NUNIT)
                    load(sp, quad + (b + 2) // 4, (b + 2) % 4, i + 2, 1)

            maxima(0, 0)
            with sp.Fori(0, QUADS - 1) as quad:
                for b in range(BATCH):
                    step(quad, b, False)
            for b in range(BATCH):
                step(QUADS - 1, b, True)
            store(NSTEP)
            sp.wait_ge(s["stored"], 16 * (NSTEP + 1))

        @block.tensor
        def _(pe):
            pe.wait_ge(s["consts"], 3)
            pe.wait_ge(s["const"], 32)
            pe.wait_ge(s["filled"], 16 * 16)

            def pass_a(i, p, at, nt, half, g):
                pe.wait_ge(s["maxed"], i * (2 * NPIECE) + 2 * (at + 1))
                m0, m1 = half * CH, min((half + 1) * CH, (nt + 1) * P)
                diag = nt // 4 == half
                bank = bank_a[at % RING]
                m = pe.matmul(bank[:, 0:m1 - m0], QA[p][0:ROWS_A, g, nt * P:(nt + 1) * P], KA[p][0:ROWS_A, g, m0:m1], start=True, stop=not diag)
                if diag:
                    m = pe.matmul(bank[:, m1 - m0 - P:m1 - m0], ident_r[:], masks_r[:, 0, :], start=False, stop=True)
                m.then_inc(s["tile"], 1)

            def transpose_maxima(i):
                pe.wait_ge(s["nm"], i + 1)
                pe.transpose(bank_a[0][:, 0:P], nm[:].rearrange("p a g t -> p (a g t)"), K["ident"][:]).then_inc(s["nmT"], 1)

            def pass_b(i, p, u, mt, half, g):
                pe.wait_ge(s["exp"], i * NUNIT + u + 1)
                n0, n1 = max(half * CH, mt * P), (half + 1) * CH
                diag = half == mt // 4
                out = bank_b[u % RING]
                m = pe.matmul(out[:, 0:n1 - n0], KA[p][:, g, mt * P:(mt + 1) * P], QA[p][:, g, n0:n1], start=True, stop=not diag)
                if diag:
                    m = pe.matmul(out[:, 0:P], ident_r[:], masks_r[:, 1, :], start=False, stop=True)
                m.then_inc(s["st"], 1)

            def values(i, p, q, mt, half):
                if q == 0:
                    pe.wait_ge(s["va"], i + 1)
                    pe.wait_ge(s["sums"], i + 1)
                pe.wait_ge(s["exp"], i * NUNIT + (q + 1) * 4 + RING)
                n0, n1 = max(half * CH, mt * P), (half + 1) * CH
                for g in range(4):
                    m = pe.matmul(bank_o[32 * g:32 * g + 32, n0:n1], VA[p][:, mt, g, :], PT[q % RING][g][:, 0:n1 - n0],
                                  start=mt == 0, stop=mt == n1 // P - 1)
                m.then_inc(s["pv"], 1)

            def select(i):
                pe.wait_ge(s["sums"], i + 1)
                for half in range(2):
                    n = slice(half * CH, (half + 1) * CH)
                    m = pe.matmul(bank_a[1 + half][0:64, :], sel[:], sums[:, n], start=True, stop=True)
                m.then_inc(s["sel"], 1)

            def wait_piece(at, p, pair):
                if at == 0:
                    pe.wait_ge(loaded[p][0], loaded_count(pair))
                if at == FIRST_HALF:
                    pe.wait_ge(loaded[p][1], loaded_count(pair))

            def step(pair, p, last):
                i = pair * 2 + p
                more = not (last and p == 1)
                pe.wait_ge(s["maxima_loaded"], (i + 1) * 16)
                for u in range(NUNIT):
                    q, g = u // 4, u % 4
                    pass_b(i, p, u, *groups[q], g)
                    if more:
                        for at, piece in slots[u]:
                            wait_piece(at, 1 - p, pair + p)
                            pass_a(i + 1, 1 - p, at, *piece)
                    if u == TRANSPOSE_AT and more:
                        transpose_maxima(i + 1)
                    if u == SELECT_AT:
                        pe.wait_ge(s["maxed"], (i + 1 + more) * (2 * NPIECE) + 2 * RING)
                        select(i)
                    if q and g == 2:
                        values(i, p, q - 1, *groups[q - 1])
                values(i, p, NGROUP - 1, *groups[-1])
                pe.wait_ge(s["res"], i + 1)

            for at, piece in enumerate(pieces):
                wait_piece(at, 0, 0)
                pass_a(0, 0, at, *piece)
            transpose_maxima(0)
            with pe.Fori(0, NSTEP // 2 - 1) as pair:
                for p in range(2):
                    step(pair, p, False)
            for p in range(2):
                step(NSTEP // 2 - 1, p, True)
            select(NSTEP)

        @block.scalar
        def _(act):
            act.wait_ge(s["const"], 32)
            act.activation(ident_r[:], K["ident"][:], ACT.Copy).then_inc(s["consts"], 1)
            act.activation(masks_r[:], masks[:], ACT.Copy).then_inc(s["consts"], 1)
            act.activation(ones2[:], K["ones_wide"][0:2, :], ACT.Copy).then_inc(s["consts"], 1)
            act.sem_inc(s["exp"], RING)

            def copy_sums(i):
                act.wait_ge(s["pv"], (i + 1) * NGROUP)
                act.activation(sums[:], bank_o[:], ACT.Copy).then_inc(s["sums"], 1)

            def step(pair, p):
                i = pair * 2 + p
                for u in range(NUNIT):
                    q, g = u // 4, u % 4
                    t, half = groups[q]
                    width = (half + 1) * CH - max(half * CH, t * P)
                    act.wait_ge(s["st"], i * NUNIT + u + 1)
                    if g == 0:
                        act.wait_ge(s["pv"], (i + 1) * NGROUP + q + 1 - RING)
                    act.activation(PT[q % RING][g][:, 0:width], bank_b[u % RING][:, 0:width], ACT.Exp).then_inc(s["exp"], 1)
                    if u == 3:
                        copy_sums(i)

            with act.Fori(0, NSTEP // 2) as pair:
                for p in range(2):
                    step(pair, p)
            copy_sums(NSTEP)

        @block.vector
        def _(dve):
            def reduce_piece(i, at, nt, half, g):
                dve.wait_ge(s["tile"], i * NPIECE + at + 1)
                width = min((half + 1) * CH, (nt + 1) * P) - half * CH
                dve.tensor_reduce(halves[:, g, nt, half:half + 1], bank_a[at % RING][:, 0:width], AX.X, ALU.max).then_inc(s["maxed"], 2)

            def negate(i):
                dve.wait_ge(s["maxed"], (i + 1) * (2 * NPIECE) + 2 * RING)
                dve.tensor_reduce(mx[:], halves[:], AX.X, ALU.max).then_inc(s["mx"], 1)
                dve.wait_ge(s["mx"], i + 1)
                dve.wait_ge(s["nmT"], i)
                dve.tensor_scalar(nm_hi[:], mx[:], -1.0, None, ALU.mult).then_inc(s["nm_hi"], 1)
                dve.wait_ge(s["nm_hi"], i + 1)
                dve.tensor_copy(nm[:, HI], nm_hi[:].bitcast(F32))
                dve.scalar_tensor_tensor(nm[:, LO], mx[:], -1.0, nm_hi[:].bitcast(F32), ALU.mult, ALU.subtract).then_inc(s["nm"], 1)
                dve.wait_ge(s["nmT"], i + 1)
                dve.wait_ge(s["maxima_loaded"], i * 16)
                dve.tensor_copy(nmT[:], bank_a[0][0:2 * 4 * NT, 0:P]).then_inc(s["nmT_copied"], 1)

            def unload(i):
                dve.wait_ge(s["sel"], i + 1)
                dve.wait_ge(s["stored"], i * 16)
                for half in range(2):
                    m = dve.tensor_copy(res[:, half * CH:(half + 1) * CH], bank_a[1 + half][0:64, :])
                m.then_inc(s["res"], 1)

            def step(pair, p, last):
                i = pair * 2 + p
                more = not (last and p == 1)
                if more:
                    for at, piece in enumerate(pieces):
                        reduce_piece(i + 1, at, *piece)
                    negate(i + 1)
                unload(i)

            dve.memset(bank_o[:], 1.0).then_inc(s["pv"], NGROUP)
            dve.sem_inc(s["maxed"], RING * 2)
            dve.memset(nm[:], 0.0).then_inc(s["mx_clear"], 1)
            dve.memset(halves[:], -3e38).then_inc(s["mx_clear"], 1)
            dve.wait_ge(s["mx_clear"], 2)
            for at, piece in enumerate(pieces):
                reduce_piece(0, at, *piece)
            negate(0)
            with dve.Fori(0, NSTEP // 2 - 1) as pair:
                for p in range(2):
                    step(pair, p, False)
            for p in range(2):
                step(NSTEP // 2 - 1, p, True)
            unload(NSTEP)

        @block.gpsimd
        def _(pool):
            for p in range(2):
                pool.memset(VA[p][:], 0.0).then_inc(s["cleared"], 1)
            pool.wait_ge(s["cleared"], 2)
            for p in range(2):
                pool.memset(VA[p][:, :, :, HD:HD + 1], 1.0)
            def step(quad, b):
                i = quad * BATCH + b
                pool.wait_ge(s["pv"], i * NGROUP)
                for g in range(4):
                    m = pool.tensor_copy(VA[b % 2][:, :, g, 0:HD], V[:, b * NT:(b + 1) * NT, bass.ds(quad * 32 + g * HD, HD)])
                m.then_inc(s["va"], 1)
            with pool.Fori(0, QUADS) as quad:
                for b in range(BATCH):
                    step(quad, b)


def attnb_out(nc, name, X, w, o_dram):
    with ExitStack() as ctx:
        ph = Phase(nc, ctx, name + "o")
        wo = ph.sb("wo", [P, D])
        bo = ph.sb("bo", [P, 1])
        den = [ph.sb(f"den{b}", [P, SEQ]) for b in range(BATCH)]
        num = [ph.sb(f"num{b}", [P, SEQ]) for b in range(BATCH)]
        inv = [ph.sb(f"inv{i}", [P, CH]) for i in range(2)]
        heads = [ph.sb(f"heads{i}", [P, CH]) for i in range(2)]
        bank = [ph.ps(f"bank{i}") for i in range(2)]
        loaded, inverted, divided, made, added = (ph.sem(n) for n in ("loaded", "inverted", "divided", "made", "added"))
        arrived = [ph.sem(f"arrived{b}") for b in range(BATCH)]
        block = ctx.enter_context(nc.Block())

        @block.sync
        def _(sp):
            sp.dma_start(wo[:], w[name + "_wo"]).then_inc(loaded, 16)
            sp.dma_start(bo[:], w[name + "_bo"]).then_inc(loaded, 16)
            for b in range(BATCH):
                for quad in range(QUADS):
                    rows = slice(32 * quad, 32 * quad + 32)
                    sp.dma_start(den[b][rows, :], o_dram[quad * BATCH + b + 1, 0:32, :]).then_inc(arrived[b], 16)
                    sp.dma_start(num[b][rows, :], o_dram[quad * BATCH + b + 1, 32:64, :]).then_inc(arrived[b], 16)

        @block.tensor
        def _(pe):
            pe.wait_ge(loaded, 32)
            for c in range(NCH):
                pe.wait_ge(divided, c + 1)
                if c >= 2:
                    pe.wait_ge(added, c - 1)
                pe.matmul(bank[c % 2][:], wo[:], heads[c % 2][:], start=True, stop=True).then_inc(made, 1)

        @block.vector
        def _(dve):
            dve.wait_ge(loaded, 32)
            for c in range(NCH + 1):
                if c < NCH:
                    n = slice((c % 2) * CH, (c % 2 + 1) * CH)
                    dve.wait_ge(arrived[c // 2], 8 * 16)
                    dve.reciprocal(inv[c % 2][:], den[c // 2][:, n]).then_inc(inverted, 1)
                    dve.wait_ge(inverted, c + 1)
                    if c >= 2:
                        dve.wait_ge(made, c - 1)
                    dve.tensor_tensor(heads[c % 2][:], num[c // 2][:, n], inv[c % 2][:], ALU.mult).then_inc(divided, 1)
                if c:
                    dve.wait_ge(made, c)
                    dve.scalar_tensor_tensor(X[:, tok(c - 1)], bank[(c - 1) % 2][:], bo[:, 0:1], X[:, tok(c - 1)], ALU.add, ALU.add).then_inc(added, 1)


def attna_phase(nc, name, X, K, w):
    q_dram = nc.dram_tensor(f"{name}_q", (NSTEP, 4, 2 * HD, SEQ), F32, kind="Internal").ap()
    k_dram = nc.dram_tensor(f"{name}_k", (NSTEP, 4, 2 * HD, SEQ), F32, kind="Internal").ap()
    o_dram = nc.dram_tensor(f"{name}_o", (NSTEP + 1, 64, SEQ), F32, kind="Internal").ap()
    with ExitStack() as ctx:
        keep = Phase(nc, ctx, name)
        V = keep.sb("V", [P, BATCH * NT, D])
        attna_project(nc, name, X, K, w, q_dram, k_dram, V)
        attna_scores(nc, name, w, q_dram, k_dram, V, o_dram)
        attnb_out(nc, name, X, w, o_dram)


def attna_project(nc, name, X, K, w, q_dram, k_dram, V):
    SUB = CH // P
    G = 2
    with ExitStack() as ctx:
        ph = Phase(nc, ctx, name + "p")
        wq = ph.sb("wq", [P, 4, D])
        wv = ph.sb("wv", [P, D])
        turn = ph.sb("turn", [P, 2, SEQ])
        head_ones = ph.sb("head_ones", [P, P])
        tiny = ph.sb("tiny", [P, 1])
        xn = [ph.sb(f"xn{g}", [P, CH]) for g in range(G)]
        tc = [ph.sb(f"tc{i}", [P, CH]) for i in range(2)]
        ts_ = [ph.sb(f"ts{i}", [P, CH]) for i in range(2)]
        turned = [ph.sb(f"turned{i}", [P, CH]) for i in range(2)]
        sq = [ph.sb(f"sq{i}", [P, CH]) for i in range(2)]
        length = [ph.sb(f"length{i}", [P, CH]) for i in range(2)]
        inv = [ph.sb(f"inv{i}", [P, CH]) for i in range(2)]
        whole = [ph.sb(f"whole{i}", [P, CH]) for i in range(2)]
        hi = [[ph.sb(f"hi{i}{p}", [P, CH], F32R) for i in range(2)] for p in range(G)]
        lo = [[ph.sb(f"lo{i}{p}", [P, CH], F32R) for i in range(2)] for p in range(G)]
        bank_n = [ph.ps(f"bank_n{g}") for g in range(G)]
        bank_q = [ph.ps(f"bank_q{i}") for i in range(4)]
        bank_ss = ph.ps("bank_ss")
        bank_v = ph.ps("bank_v")
        n1 = Norm(ph, "n1", K, bank_n)
        s = {n: ph.sem(n) for n in ("loaded", "tiny", "xn", "qk", "products", "turned", "sq", "ss", "length", "inv", "v", "v_copied", "whole", "hi", "lo", "stored0", "stored1")}
        stored = [s["stored0"], s["stored1"]]
        block = ctx.enter_context(nc.Block())
        scale = [float(1 / np.sqrt(HD)), 1.0]

        @block.sync
        def _(sp):
            sp.dma_start(wq[:], w["aa_wq"].rearrange("p (a d) -> p a d", a=4)).then_inc(s["loaded"], 16)
            sp.dma_start(wv[:], w["aa_wv"]).then_inc(s["loaded"], 16)
            sp.dma_start(turn[:], w["turn"].rearrange("p (a t) -> p a t", a=2)).then_inc(s["loaded"], 16)
            sp.dma_start(head_ones[:], w["head_ones"]).then_inc(s["loaded"], 16)
            with sp.Fori(0, BATCH) as b:
                for g in range(G):
                    c = b * G + g
                    for i, dram in enumerate((q_dram, k_dram)):
                        sp.wait_ge(s["lo"], c * 2 + i + 1)
                        for part, src in enumerate((hi, lo)):
                            for quad in range(QUADS):
                                dst = dram[bass.ds(b + quad * BATCH, 1), :, part * HD:(part + 1) * HD, g * CH:(g + 1) * CH]
                                sp.dma_start(dst.rearrange("o g d t -> (o g) d t"), src[g][i][32 * quad:32 * quad + 32, :].bitcast(F32)).then_inc(stored[g], 16)
            for g in range(G):
                sp.wait_ge(stored[g], 16 * 16 * BATCH)

        @block.tensor
        def _(pe):
            pe.wait_ge(s["loaded"], 64)
            with pe.Fori(0, BATCH) as b:
                for g in range(G):
                    n1.tensor_mean(pe, b, g, X[:, tok(b * G + g)])
                for g in range(G):
                    n1.tensor_var(pe, b, g)
                for g in range(G):
                    n1.tensor_spread(pe, b, g)
                for g in range(G):
                    c = b * G + g
                    pe.wait_ge(s["xn"], c + 1)
                    pe.wait_ge(s["products"], c * 4)
                    for i in range(4):
                        pe.matmul(bank_q[i][:], wq[:, i, :], xn[g][:], start=True, stop=True).then_inc(s["qk"], 1)
                    pe.wait_ge(s["v_copied"], c)
                    for u in range(SUB):
                        m = pe.matmul(bank_v[:, u * D:(u + 1) * D], xn[g][:, u * P:(u + 1) * P], wv[:], start=True, stop=True)
                    m.then_inc(s["v"], 1)
                    for i in range(2):
                        pe.wait_ge(s["sq"], c * 2 + i + 1)
                        pe.wait_ge(s["length"], c * 2 + i)
                        pe.matmul(bank_ss[:], head_ones[:], sq[i][:], start=True, stop=True).then_inc(s["ss"], 1)

        @block.scalar
        def _(act):
            act.wait_ge(s["tiny"], 1)
            with act.Fori(0, BATCH) as b:
                for g in range(G):
                    n1.scalar_square(act, b, g)
                for g in range(G):
                    c = b * G + g
                    act.wait_ge(s["v"], c + 1)
                    act.activation(V[:, bass.ds(c * SUB, SUB), :], bank_v[:].rearrange("p (u d) -> p u d", u=SUB), ACT.Copy).then_inc(s["v_copied"], 1)
                    for i in range(2):
                        act.wait_ge(s["turned"], c * 2 + i + 1)
                        act.activation(sq[i][:], turned[i][:], ACT.Square).then_inc(s["sq"], 1)
                    for i in range(2):
                        act.wait_ge(s["ss"], c * 2 + i + 1)
                        act.activation(length[i][:], bank_ss[:], ACT.Sqrt, bias=tiny[:, 0:1]).then_inc(s["length"], 1)

        @block.gpsimd
        def _(pool):
            pool.memset(tiny[:], 1e-6).then_inc(s["tiny"], 1)
            with pool.Fori(0, BATCH) as b:
                for g in range(G):
                    n1.pool_power(pool, b, g)

        @block.vector
        def _(dve):
            dve.wait_ge(s["loaded"], 64)
            with dve.Fori(0, BATCH) as b:
                for g in range(G):
                    n1.vector_centre(dve, b, g, X[:, tok(b * G + g)])
                for g in range(G):
                    n1.vector_var(dve, b, g)
                for g in range(G):
                    n1.vector_diag(dve, b, g)
                for g in range(G):
                    n1.vector_wait_spread(dve, b, g)
                    dve.tensor_tensor(xn[g][:], n1.centred[g][:], bank_n[g][:], ALU.mult).then_inc(s["xn"], 1)
                for g in range(G):
                    c = b * G + g
                    pos = slice(g * CH, (g + 1) * CH)
                    dve.wait_ge(s["lo"], c * 2)
                    for i in range(2):
                        dve.wait_ge(s["qk"], c * 4 + 2 * i + 2)
                        dve.tensor_tensor(tc[i][:], bank_q[2 * i][:], turn[:, 0, pos], ALU.mult).then_inc(s["products"], 1)
                        dve.tensor_tensor(ts_[i][:], bank_q[2 * i + 1][:], turn[:, 1, pos], ALU.mult).then_inc(s["products"], 1)
                    for i in range(2):
                        dve.wait_ge(s["products"], c * 4 + 2 * i + 2)
                        dve.tensor_tensor(turned[i][:], tc[i][:], ts_[i][:], ALU.add).then_inc(s["turned"], 1)
                    for i in range(2):
                        dve.wait_ge(s["length"], c * 2 + i + 1)
                        dve.reciprocal(inv[i][:], length[i][:]).then_inc(s["inv"], 1)
                    for i in range(2):
                        dve.wait_ge(s["inv"], c * 2 + i + 1)
                        dve.scalar_tensor_tensor(whole[i][:], turned[i][:], scale[i], inv[i][:], ALU.mult, ALU.mult).then_inc(s["whole"], 1)
                    for i in range(2):
                        dve.wait_ge(s["whole"], c * 2 + i + 1)
                        dve.wait_ge(stored[g], b * 256)
                        dve.tensor_copy(hi[g][i][:], whole[i][:]).then_inc(s["hi"], 1)
                    for i in range(2):
                        dve.wait_ge(s["hi"], c * 2 + i + 1)
                        dve.tensor_tensor(lo[g][i][:], whole[i][:], hi[g][i][:].bitcast(F32), ALU.subtract).then_inc(s["lo"], 1)


def attna_scores(nc, name, w, q_dram, k_dram, V, o_dram):
    UNITS = NT * 2
    RING = 4
    with ExitStack() as ctx:
        ph = Phase(nc, ctx, name + "s")
        QA = [ph.sb(f"QA{p}", [P, SEQ], F32R) for p in range(2)]
        KA = [ph.sb(f"KA{p}", [P, SEQ], F32R) for p in range(2)]
        VA = [ph.sb(f"VA{p}", [P, NT, 4, 32]) for p in range(2)]
        PT = [ph.sb(f"PT{r}", [P, 4, CH]) for r in range(RING)]
        sums = ph.sb("sums", [P, SEQ])
        res = ph.sb("res", [64, SEQ])
        sel = ph.sb("sel", [P, 64])
        ST = [ph.ps(f"ST{i}", (P, 2, CH)) for i in range(2)]
        O = [ph.ps(f"O{p}", (P, SEQ)) for p in range(2)]
        s = {n: ph.sem(n) for n in ("const", "loaded0", "loaded1", "st", "exp", "pv", "cleared", "va", "sums", "sel", "res", "stored")}
        loaded = [s["loaded0"], s["loaded1"]]
        block = ctx.enter_context(nc.Block())

        @block.sync
        def _(sp):
            sp.dma_start(sel[:], w["sel_b"]).then_inc(s["const"], 16)

            def load(i, p):
                for tile, dram, order in ((QA[p], q_dram, ((0, 0, 16), (16, 0, 16))), (KA[p], k_dram, ((0, 0, 8), (8, 0, 16), (24, 8, 16)))):
                    for at, r0, r1 in order:
                        for g in range(4):
                            sp.dma_start(tile[32 * g + at:32 * g + at + r1 - r0, :].bitcast(F32), dram[bass.ds(i, 1), g, r0:r1, :]).then_inc(loaded[p], 16)

            def store(i):
                sp.wait_ge(s["res"], i + 1)
                sp.dma_start(o_dram[bass.ds(i + 1, 1), :, :], res[:]).then_inc(s["stored"], 16)

            load(0, 0)
            load(1, 1)
            with sp.Fori(0, NSTEP // 2 - 1) as pair:
                for p in range(2):
                    i = pair * 2 + p
                    sp.wait_ge(s["pv"], (i + 1) * UNITS)
                    load(i + 2, p)
                    store(i)
            store(NSTEP - 2)
            store(NSTEP - 1)
            sp.wait_ge(s["stored"], 16 * NSTEP)

        def load_count(i):
            return 20 * 16

        @block.tensor
        def _(pe):
            pe.wait_ge(s["const"], 16)

            def scores(i, p, u):
                mt, half = u // 2, u % 2
                for pr in range(2):
                    n = i * 2 * UNITS + 2 * u + pr
                    pe.wait_ge(s["exp"], n + 1)
                    for g in (2 * pr, 2 * pr + 1):
                        rows = slice(32 * g, 32 * g + 32)
                        m = pe.matmul(ST[pr][:, g % 2, :], KA[p][rows, mt * P:(mt + 1) * P], QA[p][rows, half * CH:(half + 1) * CH],
                                      start=True, stop=True)
                    m.then_inc(s["st"], 1)

            def values(i, p, u):
                mt, half = u // 2, u % 2
                if u == 0:
                    pe.wait_ge(s["va"], i + 1)
                pe.wait_ge(s["exp"], i * 2 * UNITS + 2 * u + 2 + 2)
                for g in range(4):
                    m = pe.matmul(O[p][32 * g:32 * g + 32, half * CH:(half + 1) * CH], VA[p][:, mt, g, :], PT[u % RING][:, g, :],
                                  start=mt == 0, stop=mt == NT - 1)
                m.then_inc(s["pv"], 1)

            def select(i, p):
                pe.wait_ge(s["sums"], i + 1)
                for half in range(2):
                    n = slice(half * CH, (half + 1) * CH)
                    m = pe.matmul(O[p][0:64, n], sel[:], sums[:, n], start=True, stop=True)
                m.then_inc(s["sel"], 1)

            def step(i, p, first):
                pe.wait_ge(loaded[p], (i // 2 + 1) * 320 if isinstance(i, int) else pair_of[0] * 320 + 320)
                for u in range(UNITS):
                    if u == 2 and not (first and p == 0):
                        pe.wait_ge(s["va"], i)
                    scores(i, p, u)
                    if u < 2:
                        if not (first and p == 0):
                            values(i - 1, 1 - p, UNITS - 2 + u)
                    else:
                        if u == 2 and not (first and i_is_small(i)):
                            pe.wait_ge(s["res"], i - 1)
                        values(i, p, u - 2)
                    if u == 6 and not (first and p == 0):
                        select(i - 1, 1 - p)

            def i_is_small(i):
                return isinstance(i, int) and i < 2

            pair_of = [None]
            for p in range(2):
                step(p, p, True)
            with pe.Fori(1, NSTEP // 2) as pair:
                pair_of[0] = pair
                for p in range(2):
                    step(pair * 2 + p, p, False)
            for u in (UNITS - 2, UNITS - 1):
                values(NSTEP - 1, 1, u)
            select(NSTEP - 1, 1)

        @block.scalar
        def _(act):
            act.sem_inc(s["exp"], 2)

            def exponentials(i, u):
                for pr in range(2):
                    act.wait_ge(s["st"], i * 2 * UNITS + 2 * u + pr + 1)
                    if pr == 0 and not (isinstance(i, int) and i == 0 and u < RING):
                        act.wait_ge(s["pv"], i * UNITS + u - RING + 1)
                    act.activation(PT[u % RING][:, 2 * pr:2 * pr + 2, :], ST[pr][:], ACT.Exp).then_inc(s["exp"], 1)

            for u in range(UNITS):
                exponentials(0, u)
            with act.Fori(1, NSTEP) as i:
                for u in range(UNITS):
                    exponentials(i, u)

        @block.vector
        def _(dve):
            def collect(i, p, first):
                dve.wait_ge(s["pv"], (i + 1) * UNITS)
                if not first:
                    dve.wait_ge(s["sel"], i)
                dve.tensor_copy(sums[:], O[p][:]).then_inc(s["sums"], 1)
                dve.wait_ge(s["sel"], i + 1)
                if not first:
                    dve.wait_ge(s["stored"], i * 16)
                dve.tensor_copy(res[:], O[p][0:64, :]).then_inc(s["res"], 1)

            collect(0, 0, True)
            collect(1, 1, False)
            with dve.Fori(1, NSTEP // 2) as pair:
                for p in range(2):
                    collect(pair * 2 + p, p, False)

        @block.gpsimd
        def _(pool):
            for p in range(2):
                pool.memset(VA[p][:], 0.0).then_inc(s["cleared"], 1)
            pool.wait_ge(s["cleared"], 2)
            for p in range(2):
                pool.memset(VA[p][:, :, :, HD:HD + 1], 1.0)

            def place(quad, b, i, first):
                if not first:
                    pool.wait_ge(s["pv"], (i - 1) * UNITS)
                for g in range(4):
                    m = pool.tensor_copy(VA[b % 2][:, :, g, 0:HD], V[:, b * NT:(b + 1) * NT, bass.ds(quad * 32 + g * HD, HD)])
                m.then_inc(s["va"], 1)

            for b in range(BATCH):
                place(0, b, b, b < 2)
            with pool.Fori(1, QUADS) as quad:
                for b in range(BATCH):
                    place(quad, b, quad * BATCH + b, False)


def tern_phase(nc, name, X, K, w):
    G = 2
    NGROUP = NCH // G
    COUNT = FF * D
    with ExitStack() as ctx:
        ph = Phase(nc, ctx, name)
        raw = [ph.sb(f"raw{i}", [P, FF]) for i in range(2)]
        wt = [ph.sb(f"wt{i}", [P, FF], F32R) for i in range(2)]
        above = [ph.sb(f"above{i}", [P, FF]) for i in range(2)]
        below = [ph.sb(f"below{i}", [P, FF]) for i in range(2)]
        total = ph.sb("total", [P, 2])
        scale = ph.sb("scale", [P, 2])
        limit = ph.sb("limit", [P, 2, 2])
        b1 = ph.sb("b1", [P, NF])
        b2 = ph.sb("b2", [P, 1])
        xn = [ph.sb(f"xn{g}", [P, CH]) for g in range(G)]
        x_hi = [[ph.sb(f"x_hi{p}{g}", [P, CH], F32R) for g in range(G)] for p in range(2)]
        x_lo = [[ph.sb(f"x_lo{p}{g}", [P, CH], F32R) for g in range(G)] for p in range(2)]
        h = [ph.sb(f"h{g}", [P, NF, CH]) for g in range(G)]
        h_hi = [ph.sb(f"h_hi{g}", [P, NF, CH], F32R) for g in range(G)]
        h_lo = [ph.sb(f"h_lo{g}", [P, NF, CH], F32R) for g in range(G)]
        bank_n = [ph.ps(f"bank_n{g}") for g in range(G)]
        bank_h = [ph.ps(f"bank_h{f}") for f in range(NF)]
        bank_o = [ph.ps(f"bank_o{g}") for g in range(G)]
        n1 = Norm(ph, "n1", K, bank_n)
        s = {n: ph.sem(n) for n in ("loaded", "total", "total_all", "scale", "limit", "compared", "ternary",
                                    "xn", "x_hi", "x_lo", "up", "h_hi", "h_lo", "h_lo_pool", "down", "added")}
        block = ctx.enter_context(nc.Block())

        @block.sync
        def _(sp):
            for dst, src in ((raw[0], "tern_w1"), (raw[1], "tern_w2"), (b1, "tern_b1"), (b2, "tern_b2")):
                sp.dma_start(dst[:], w[src]).then_inc(s["loaded"], 16)

        def norm_tensor(pe, group, step, g):
            if step == 0:
                pe.wait_ge(s["xn"], group * G)
                n1.tensor_mean(pe, group, g, X[:, tok(group * G + g)])
            if step == 1:
                n1.tensor_var(pe, group, g)
            if step == 2:
                n1.tensor_spread(pe, group, g)

        def norm_vector(dve, group, par, step, g):
            c = group * G + g
            if step == 0:
                n1.vector_centre(dve, group, g, X[:, tok(c)])
            if step == 1:
                n1.vector_var(dve, group, g)
            if step == 2:
                n1.vector_diag(dve, group, g)
            if step == 3:
                n1.vector_wait_spread(dve, group, g)
                dve.tensor_tensor(xn[g][:], n1.centred[g][:], bank_n[g][:], ALU.mult).then_inc(s["xn"], 1)
            if step == 4:
                dve.wait_ge(s["xn"], c + 1)
                dve.tensor_copy(x_hi[par][g][:], xn[g][:]).then_inc(s["x_hi"], 1)
            if step == 5:
                dve.wait_ge(s["x_hi"], c + 1)
                dve.tensor_tensor(x_lo[par][g][:], xn[g][:], x_hi[par][g][:].bitcast(F32), ALU.subtract).then_inc(s["x_lo"], 1)

        @block.tensor
        def _(pe):
            for g in range(G):
                norm_tensor(pe, 0, 0, g)
            pe.wait_ge(s["total"], 1)
            pe.matmul(bank_h[0][:, 0:2], K["ones"][:], total[:], start=True, stop=True).then_inc(s["total_all"], 1)
            for step in range(1, 3):
                for g in range(G):
                    norm_tensor(pe, 0, step, g)
            pe.wait_ge(s["ternary"], 2)

            def group(j, par):
                for g in range(G):
                    c = j * G + g
                    pe.wait_ge(s["x_lo"], c + 1)
                    for f in range(NF):
                        pe.wait_ge(s["h_hi"], c * NF + f + 1)
                        wf = wt[0][:, f * P:(f + 1) * P]
                        pe.matmul(bank_h[f][:], wf, x_hi[par][g][:], start=True, stop=False)
                        pe.matmul(bank_h[f][:], wf, x_lo[par][g][:], start=False, stop=True).then_inc(s["up"], 1)
                    norm_tensor(pe, j + 1, g, 0)
                    norm_tensor(pe, j + 1, g, 1)
                for g in range(G):
                    c = j * G + g
                    pe.wait_ge(s["added"], c - 1 + 1)
                    for f in range(NF):
                        pe.wait_ge(*((s["h_lo"], c * 2 + f + 1) if f < 2 else (s["h_lo_pool"], c * 2 + f - 1)))
                        wf = wt[1][:, f * D:(f + 1) * D]
                        pe.matmul(bank_o[g][:], wf, h_hi[g][:, f, :], start=f == 0, stop=False)
                        m = pe.matmul(bank_o[g][:], wf, h_lo[g][:, f, :], start=False, stop=f == NF - 1)
                    m.then_inc(s["down"], 1)
                for g in range(G):
                    norm_tensor(pe, j + 1, 2, g)

            with pe.Fori(0, NGROUP // 2) as jj:
                for par in range(2):
                    group(jj * 2 + par, par)

        @block.scalar
        def _(act):
            for g in range(G):
                n1.scalar_square(act, 0, g)
            act.wait_ge(s["loaded"], 64)
            act.sem_inc(s["h_hi"], NF)

            def group(j, par):
                for g in range(G):
                    c = j * G + g
                    for f in range(NF):
                        act.wait_ge(s["up"], c * NF + f + 1)
                        if f == 0:
                            act.wait_ge(s["down"], j * G - G + g + 1 + G - 1)
                        act.activation(h[g][:, f, :], bank_h[f][:], ACT.Gelu, bias=b1[:, f:f + 1])
                        act.activation(h_hi[g][:, f, :], bank_h[f][:], ACT.Gelu, bias=b1[:, f:f + 1]).then_inc(s["h_hi"], 1)
                    if g == 0:
                        for gg in range(G):
                            n1.scalar_square(act, j + 1, gg)

            with act.Fori(0, NGROUP // 2) as jj:
                for par in range(2):
                    group(jj * 2 + par, par)

        @block.vector
        def _(dve):
            for g in range(G):
                norm_vector(dve, 0, 0, 0, g)
            dve.wait_ge(s["loaded"], 64)
            for i in range(2):
                m = dve.tensor_reduce(total[:, i:i + 1], raw[i][:], AX.X, ALU.add, apply_absolute_value=True)
            m.then_inc(s["total"], 1)
            for g in range(G):
                norm_vector(dve, 0, 0, 1, g)
            dve.wait_ge(s["total_all"], 1)
            dve.tensor_scalar(scale[:], bank_h[0][:, 0:2], 1.0 / COUNT, 1e-8, ALU.mult, ALU.max).then_inc(s["scale"], 1)
            dve.wait_ge(s["scale"], 1)
            dve.tensor_scalar(limit[:, 0, :], scale[:], 0.5, None, ALU.mult).then_inc(s["limit"], 1)
            dve.tensor_scalar(limit[:, 1, :], scale[:], -0.5, None, ALU.mult).then_inc(s["limit"], 1)
            dve.wait_ge(s["limit"], 2)
            for i in range(2):
                dve.tensor_scalar(above[i][:], raw[i][:], limit[:, 0, i:i + 1], None, ALU.is_gt)
                dve.tensor_scalar(below[i][:], raw[i][:], limit[:, 1, i:i + 1], None, ALU.is_lt).then_inc(s["compared"], 1)
            for i in range(2):
                dve.wait_ge(s["compared"], i + 1)
                dve.tensor_tensor(wt[i][:], above[i][:], below[i][:], ALU.subtract).then_inc(s["ternary"], 1)
            for step in range(2, 6):
                for g in range(G):
                    norm_vector(dve, 0, 0, step, g)
            dve.sem_inc(s["added"], 1)

            def group(j, par):
                for g in range(G):
                    c = j * G + g
                    norm_vector(dve, j + 1, 1 - par, 0, g) if g == 0 else None
                    for f in range(2):
                        dve.wait_ge(s["h_hi"], c * NF + f + 1 + NF)
                        dve.tensor_tensor(h_lo[g][:, f, :], h[g][:, f, :], h_hi[g][:, f, :].bitcast(F32), ALU.subtract).then_inc(s["h_lo"], 1)
                    if g == 0:
                        norm_vector(dve, j + 1, 1 - par, 0, 1)
                    else:
                        norm_vector(dve, j + 1, 1 - par, 1, 0)
                        norm_vector(dve, j + 1, 1 - par, 1, 1)
                for step in range(2, 3):
                    for g in range(G):
                        norm_vector(dve, j + 1, 1 - par, step, g)
                for g in range(G):
                    c = j * G + g
                    dve.wait_ge(s["down"], c + 1 + G - 1)
                    dve.scalar_tensor_tensor(X[:, tok(c)], bank_o[g][:], b2[:, 0:1], X[:, tok(c)], ALU.add, ALU.add).then_inc(s["added"], 1)
                for step in range(3, 6):
                    for g in range(G):
                        norm_vector(dve, j + 1, 1 - par, step, g)

            with dve.Fori(0, NGROUP // 2) as jj:
                for par in range(2):
                    group(jj * 2 + par, par)

        @block.gpsimd
        def _(pool):
            pool.sem_inc(s["down"], G - 1)
            for g in range(G):
                n1.pool_power(pool, 0, g)

            def group(j, par):
                for g in range(G):
                    c = j * G + g
                    for f in range(2, NF):
                        pool.wait_ge(s["h_hi"], c * NF + f + 1 + NF)
                        pool.tensor_tensor(h_lo[g][:, f, :], h[g][:, f, :], h_hi[g][:, f, :].bitcast(F32), ALU.subtract).then_inc(s["h_lo_pool"], 1)
                for g in range(G):
                    n1.pool_power(pool, j + 1, g)

            with pool.Fori(0, NGROUP // 2) as jj:
                for par in range(2):
                    group(jj * 2 + par, par)


def lru_phase(nc, name, X, K, w):
    G = 2
    NH = 2
    with ExitStack() as ctx:
        ph = Phase(nc, ctx, name)
        w_in = ph.sb("w_in", [P, 4, P])
        w_dt = ph.sb("w_dt", [P, NH, NH, P])
        w_out = ph.sb("w_out", [P, NH, D])
        vecs = ph.sb("vecs", [P, 1 + NH])
        half_b = ph.sb("half_b", [P, NH])
        xn = [ph.sb(f"xn{g}", [P, CH]) for g in range(G)]
        hh = [ph.sb(f"hh{g}", [P, CH]) for g in range(G)]
        u = [ph.sb(f"u{g}", [P, NH, CH]) for g in range(G)]
        z = [ph.sb(f"z{g}", [P, NH, CH]) for g in range(G)]
        th = [ph.sb(f"th{g}", [P, NH, CH]) for g in range(G)]
        lam = [ph.sb(f"lam{g}", [P, NH, CH]) for g in range(G)]
        oml = [ph.sb(f"oml{g}", [P, NH, CH]) for g in range(G)]
        drive = [ph.sb(f"drive{g}", [P, NH, CH]) for g in range(G)]
        state = [ph.sb(f"state{g}", [P, NH, CH]) for g in range(G)]
        gated = [ph.sb(f"gated{g}", [P, NH, CH]) for g in range(G)]
        xy = [ph.sb(f"xy{g}", [P, CH]) for g in range(G)]
        bank_n = [ph.ps(f"bank_n{g}") for g in range(G)]
        bank_u = [ph.ps(f"bank_u{i}") for i in range(4)]
        bank_o = [ph.ps(f"bank_o{g}") for g in range(G)]
        n1, n2 = Norm(ph, "n1", K, bank_n), Norm(ph, "n2", K, bank_n, rms=True)
        s = {n: ph.sem(n) for n in ("loaded", "half_b", "xn", "hh", "uv", "silu", "gate", "tanh", "lam", "drive", "state", "gated", "down", "xy", "added")}
        block = ctx.enter_context(nc.Block())

        @block.sync
        def _(sp):
            sp.dma_start(w_in[:], w["lru_win"].rearrange("p (a d) -> p a d", a=4)).then_inc(s["loaded"], 16)
            sp.dma_start(w_dt[:], w["lru_wdt"].rearrange("p (a b d) -> p a b d", a=NH, b=NH)).then_inc(s["loaded"], 16)
            sp.dma_start(w_out[:], w["lru_wout"].rearrange("p (a d) -> p a d", a=NH)).then_inc(s["loaded"], 16)
            sp.dma_start(vecs[:], w["lru_vecs"]).then_inc(s["loaded"], 16)

        @block.tensor
        def _(pe):
            pe.wait_ge(s["loaded"], 64)
            with pe.Fori(0, BATCH) as b:
                for g in range(G):
                    pe.wait_ge(s["hh"], b * G)
                    n1.tensor_mean(pe, b, g, X[:, tok(b * G + g)])
                for g in range(G):
                    n1.tensor_var(pe, b, g)
                for g in range(G):
                    n1.tensor_spread(pe, b, g)
                for g in range(G):
                    pe.wait_ge(s["xn"], b * G + g + 1)
                    n2.tensor_var(pe, b, g)
                for g in range(G):
                    n2.tensor_spread(pe, b, g)
                for g in range(G):
                    c = b * G + g
                    pe.wait_ge(s["hh"], c + 1)
                    for i in range(4):
                        if i < NH:
                            pe.wait_ge(s["tanh"], c * NH)
                        pe.wait_ge(s["silu"], c * 4)
                        pe.matmul(bank_u[i][:], w_in[:, i, :], hh[g][:], start=True, stop=True).then_inc(s["uv"], 1)
                    for o in range(NH):
                        pe.wait_ge(s["silu"], c * 4 + NH)
                        for i in range(NH):
                            m = pe.matmul(bank_u[o][:], w_dt[:, i, o, :], u[g][:, i, :], start=i == 0, stop=i == NH - 1)
                        m.then_inc(s["gate"], 1)
                for g in range(G):
                    c = b * G + g
                    pe.wait_ge(s["added"], b * G)
                    for i in range(NH):
                        pe.wait_ge(s["gated"], c * NH + i + 1)
                        m = pe.matmul(bank_o[g][:], w_out[:, i, :], gated[g][:, i, :], start=i == 0, stop=i == NH - 1)
                    m.then_inc(s["down"], 1)

        @block.scalar
        def _(act):
            act.wait_ge(s["loaded"], 64)
            act.activation(half_b[:], vecs[:, 1:1 + NH], ACT.Copy, scale=0.5).then_inc(s["half_b"], 1)
            act.wait_ge(s["half_b"], 1)
            with act.Fori(0, BATCH) as b:
                for g in range(G):
                    n1.scalar_square(act, b, g)
                for g in range(G):
                    act.wait_ge(s["xn"], b * G + g + 1)
                    n2.scalar_square(act, b, g, xn[g][:])
                for g in range(G):
                    c = b * G + g
                    act.wait_ge(s["gated"], (b * G) * NH)
                    for i in range(4):
                        act.wait_ge(s["uv"], c * 4 + i + 1)
                        act.activation((u, z)[i // NH][g][:, i % NH, :], bank_u[i][:], ACT.Silu).then_inc(s["silu"], 1)
                    for i in range(NH):
                        act.wait_ge(s["gate"], c * NH + i + 1)
                        act.activation(th[g][:, i, :], bank_u[i][:], ACT.Tanh, bias=half_b[:, i:i + 1], scale=0.5).then_inc(s["tanh"], 1)

        @block.gpsimd
        def _(pool):
            with pool.Fori(0, BATCH) as b:
                for n in (n1, n2):
                    for g in range(G):
                        n.pool_power(pool, b, g)

        @block.vector
        def _(dve):
            dve.wait_ge(s["loaded"], 64)
            with dve.Fori(0, BATCH) as b:
                for g in range(G):
                    n1.vector_centre(dve, b, g, X[:, tok(b * G + g)])
                for g in range(G):
                    n1.vector_var(dve, b, g)
                for g in range(G):
                    n1.vector_diag(dve, b, g)
                for g in range(G):
                    n1.vector_wait_spread(dve, b, g)
                    dve.tensor_tensor(xn[g][:], n1.centred[g][:], bank_n[g][:], ALU.mult).then_inc(s["xn"], 1)
                for g in range(G):
                    n2.vector_var(dve, b, g)
                for g in range(G):
                    n2.vector_diag(dve, b, g)
                for g in range(G):
                    n2.vector_wait_spread(dve, b, g)
                    dve.scalar_tensor_tensor(hh[g][:], xn[g][:], vecs[:, 0:1], bank_n[g][:], ALU.mult, ALU.mult).then_inc(s["hh"], 1)
                for g in range(G):
                    c = b * G + g
                    dve.tensor_tensor(xy[g][:], X[:, tok(c)], xn[g][:], ALU.add).then_inc(s["xy"], 1)
                for g in range(G):
                    c = b * G + g
                    for i in range(NH):
                        k = c * NH + i
                        dve.wait_ge(s["tanh"], k + 1)
                        dve.tensor_scalar(lam[g][:, i, :], th[g][:, i, :], 0.5, 0.5, ALU.mult, ALU.add)
                        dve.tensor_scalar(oml[g][:, i, :], th[g][:, i, :], -0.5, 0.5, ALU.mult, ALU.add).then_inc(s["lam"], 1)
                    for i in range(NH):
                        k = c * NH + i
                        dve.wait_ge(s["lam"], k + 1)
                        dve.tensor_tensor(drive[g][:, i, :], oml[g][:, i, :], u[g][:, i, :], ALU.mult).then_inc(s["drive"], 1)
                    for i in range(NH):
                        k = c * NH + i
                        dve.wait_ge(s["drive"], k + 1)
                        if g:
                            dve.wait_ge(s["state"], k - 1)
                        start = state[0][:, i, CH - 1:CH] if g else 0.0
                        dve.tensor_tensor_scan(state[g][:, i, :], lam[g][:, i, :], drive[g][:, i, :], start, ALU.mult, ALU.add).then_inc(s["state"], 1)
                    for i in range(NH):
                        k = c * NH + i
                        dve.wait_ge(s["state"], k + 1)
                        dve.wait_ge(s["silu"], c * 4 + NH + i + 1)
                        dve.wait_ge(s["down"], b * G)
                        dve.tensor_tensor(gated[g][:, i, :], state[g][:, i, :], z[g][:, i, :], ALU.mult).then_inc(s["gated"], 1)
                for g in range(G):
                    c = b * G + g
                    dve.wait_ge(s["xy"], c + 1)
                    dve.wait_ge(s["down"], c + 1)
                    dve.tensor_tensor(X[:, tok(c)], bank_o[g][:], xy[g][:], ALU.add).then_inc(s["added"], 1)


def load_constants(nc, ctx, w, X):
    keep = Phase(nc, ctx, "const")
    K = {"mean": keep.sb("mean", [P, P]), "ones_row": keep.sb("ones_row", [1, P]), "ident": keep.sb("ident", [P, P]),
         "ones": keep.sb("ones", [P, P]), "neg_half": keep.sb("neg_half", [P, CH // P]), "ones_wide": keep.sb("ones_wide", [2, SEQ])}
    with ExitStack() as c2:
        ph = Phase(nc, c2, "const_load")
        loaded = ph.sem("loaded")
        block = c2.enter_context(nc.Block())

        @block.sync
        def _(sp):
            sp.dma_start(X[:, 0:TOK], w["x"]).then_inc(loaded, 16)
            sp.dma_start(K["ident"][:], w["ident"]).then_inc(loaded, 16)
            sp.wait_ge(loaded, 32)

        @block.gpsimd
        def _(pool):
            pool.memset(X[:, TOK:TOK + 2 * CH], 0.0)
            pool.memset(K["mean"][:], 1.0 / D)
            pool.memset(K["ones_row"][:], 1.0)
            pool.memset(K["ones_wide"][:], 1.0)
            pool.memset(K["ones"][:], 1.0)
            pool.memset(K["neg_half"][:], -0.5)
    return K


def store_output(nc, X, out):
    with ExitStack() as ctx:
        ph = Phase(nc, ctx, "store")
        stored = ph.sem("stored")
        block = ctx.enter_context(nc.Block())

        @block.sync
        def _(sp):
            sp.dma_start(out, X[:, 0:TOK]).then_inc(stored, 16)
            sp.wait_ge(stored, 16)


def shape_constants():
    t = {}
    pos = np.arange(SEQ, dtype=np.float32) * np.float32((GRID - 1) / (SEQ - 1))
    low = np.floor(pos).astype(np.int32)
    frac = pos - low.astype(np.float32)
    grid = np.zeros((SEQ, GRID), np.float32)
    np.add.at(grid, (np.arange(SEQ), low), np.float32(1) - frac)
    np.add.at(grid, (np.arange(SEQ), np.minimum(low + 1, GRID - 1)), frac)
    grid[-1] = 0
    t["grid3"] = np.tile(grid.T, (3, 1))
    negmask = np.zeros((REL, 2), np.float32)
    negmask[GRID:2 * GRID, 0] = -1
    negmask[2 * GRID:, 1] = -1
    t["negmask"] = negmask
    row, col = np.meshgrid(np.arange(P), np.arange(P), indexing="ij")
    t["causal"] = np.concatenate([np.where(col > row, NEG, 0), np.where(row > col, NEG, 0)], axis=1).astype(np.float32)
    sel = np.zeros((P, 64), np.float32)
    for g in range(4):
        sel[32 * g + HD, g * HD:(g + 1) * HD] = 1
        sel[32 * g + np.arange(HD), 32 + g * HD + np.arange(HD)] = 1
    t["sel_b"] = sel
    half = HD // 2
    inv_freq = (np.float32(1) / np.float32(10000.0) ** (np.arange(half, dtype=np.float32) / np.float32(half))).astype(np.float32)
    angles = np.arange(SEQ, dtype=np.float32)[None, :] * inv_freq[:, None]
    cos, sin = np.cos(angles), np.sin(angles)
    t["turn"] = np.concatenate([np.tile(cos, (2 * HEADS, 1)), np.tile(np.concatenate([-sin, sin]), (HEADS, 1))], axis=1)
    select = np.zeros((P, 2 * N_STATE + 1), np.float32)
    for r in range(2 * N_STATE):
        select[[HEADS + r, 64 + HEADS + r], r] = 1
    select[64:, 2 * N_STATE] = -1
    t["m_select"] = select
    t["head_ones"] = np.kron(np.eye(HEADS, dtype=np.float32), np.ones((HD, HD), np.float32))
    return t


def host_layout(i):
    a = {k: np.ascontiguousarray(v) for k, v in i.items()}
    t = {}
    t["x"] = a["L0_attn_a_x"].reshape(TOK, D).T
    m = "L0_attn_a_"
    t["m_win"] = a[m + "W_in"].reshape(D, 4, P)
    t["m_conv"] = a[m + "conv_w"].reshape(2, P, CONV).transpose(1, 0, 2)
    per_channel = [a[m + "conv_b"], a[m + "b_dt"], np.repeat(a[m + "A_log"], INNER // HEADS), np.repeat(a[m + "D_skip"], INNER // HEADS),
                   a[m + "ln_g"], a[m + "ln_b"]]
    t["m_vecs"] = np.stack(per_channel).reshape(6, 2, P).transpose(2, 0, 1)
    wp = a[m + "W_xproj"].reshape(2, P, HEADS + 2 * N_STATE).transpose(1, 0, 2)
    gap = np.zeros((P, 2, 64 - wp.shape[2]), np.float32)
    t["m_wproj"] = np.concatenate([wp, gap, wp, gap], axis=2)
    t["m_wdt"] = a[m + "W_dt"]
    t["m_wout"] = a[m + "W_out"].reshape(2, P, D).transpose(1, 0, 2)
    m = "L0_ffn_"
    w1 = np.concatenate([a[m + "shared_w1"][None], a[m + "spec_w1"]])
    t["ffn_w1"] = w1.transpose(2, 0, 1).reshape(D, N_FFN * FF)
    w2 = np.concatenate([a[m + "shared_w2"][None], a[m + "spec_w2"]])
    t["ffn_w2"] = w2.reshape(N_FFN, D, NF, P).transpose(3, 0, 2, 1).reshape(P, N_FFN * NF * D)
    b1 = np.concatenate([a[m + "shared_b1"][None], a[m + "spec_b1"]])
    t["ffn_b1"] = b1.reshape(N_FFN * NF, P).T
    t["ffn_b2"] = a[m + "shared_b2"].reshape(D, 1)
    t["ffn_eb2"] = a[m + "spec_b2"]
    t["ffn_rw"] = a[m + "router_w"].T
    t["ffn_rb"] = a[m + "router_b"].reshape(1, N_EXP)
    t["iota8"] = np.tile(np.arange(N_EXP, dtype=np.float32), (P, 1))
    t["ident"] = np.eye(P, dtype=np.float32)
    t["pick8"] = np.repeat(np.eye(N_EXP, dtype=np.float32), P, axis=1)
    m = "L0_attn_b_"
    t["ab_wq"], t["ab_wk"], t["ab_wv"], t["attnb_wo"] = (a[m + n].T for n in ("Wq", "Wk", "Wv", "Wo"))
    t["ab_vecs"] = np.stack([a[m + n] for n in ("bq", "bk", "gamma", "beta")], axis=1)
    t["ab_bv"] = a[m + "bv"].reshape(1, D)
    t["attnb_bo"] = a[m + "bo"].reshape(D, 1)
    t["ab_rel"] = np.tile(a[m + "rel_bias"].transpose(1, 0, 2)[:, :, None, :], (1, 1, 3, 1)).reshape(GRID, HEADS * REL)
    wqkv = a["L1_attn_a_Wqkv"]
    partner = np.arange(D) ^ (HD // 2)
    t["aa_wq"] = np.concatenate([wqkv[:, 0:D], wqkv[:, 0:D][:, partner], wqkv[:, D:2 * D], wqkv[:, D:2 * D][:, partner]], axis=1)
    t["aa_wv"] = wqkv[:, 2 * D:]
    t["attna_wo"] = a["L1_attn_a_Wo"]
    t["attna_bo"] = a["L1_attn_a_bo"].reshape(D, 1)
    t["tern_w1"] = a["L1_ffn_W1"].T
    t["tern_w2"] = a["L1_ffn_W2"].reshape(D, NF, P).transpose(2, 1, 0).reshape(P, NF * D)
    t["tern_b1"] = a["L1_ffn_b1"].reshape(NF, P).T
    t["tern_b2"] = a["L1_ffn_b2"].reshape(D, 1)
    m = "L1_attn_b_"
    t["lru_win"] = a[m + "W_in"].T
    t["lru_wdt"] = a[m + "W_dt"].reshape(2, P, 2, P).transpose(3, 2, 0, 1).reshape(P, 4 * P)
    t["lru_wout"] = a[m + "W_out"].reshape(D, 2, P).transpose(2, 1, 0).reshape(P, 2 * D)
    t["lru_vecs"] = np.concatenate([a[m + "w_norm"].reshape(D, 1), a[m + "b_dt"].reshape(2, P).T], axis=1)
    t.update(shape_constants())
    return {k: np.ascontiguousarray(v) for k, v in t.items()}


def hybrid_stack(nc, w, out):
    with ExitStack() as ctx:
        X = ctx.enter_context(nc.sbuf_tensor("X", [P, TOK + 2 * CH], F32))
        K = load_constants(nc, ctx, w, X)
        mamba_phase(nc, "mamba", X, K, w)
        ffn_stage(nc, "moe_a", X, K, w)
        attnb_phase(nc, "attnb", X, K, w)
        ffn_stage(nc, "moe_b", X, K, w)
        attna_phase(nc, "attna", X, K, w)
        tern_phase(nc, "tern_a", X, K, w)
        lru_phase(nc, "lru", X, K, w)
        tern_phase(nc, "tern_b", X, K, w)
        store_output(nc, X, out)


def kernel(**inputs):
    import concourse.bacc as _bacc
    from concourse.bass_utils import run_bass_kernel_spmd as _run

    nc = _bacc.Bacc("TRN2", target_bir_lowering=False, num_devices=1)
    arrays = {f"in_{k}": v for k, v in host_layout(inputs).items()}
    w = {k[3:]: nc.dram_tensor(k, v.shape, F32, kind="ExternalInput").ap() for k, v in arrays.items()}
    out = nc.dram_tensor("out", (D, TOK), F32, kind="ExternalOutput").ap()
    hybrid_stack(nc, w, out)
    r = _run(nc, [arrays], core_ids=[0])
    return np.ascontiguousarray(r.results[0]["out"].T).reshape(BATCH, SEQ, D)
```

```python
import concourse.bass as bass
import numpy as np
from concourse import mybir
from contextlib import ExitStack

F32 = mybir.dt.float32
F32R = mybir.dt.float32r
U32 = mybir.dt.uint32
ALU = mybir.AluOpType
ACT = mybir.ActivationFunctionType
AX = mybir.AxisListType

P = 128
D = 128
BATCH, SEQ = 4, 1024
TOK = BATCH * SEQ
CH = 512
NCH = TOK // CH
HEADS, HD = 16, 8
EPS = 1e-5


class Phase:

    def __init__(self, nc, ctx, name):
        self.nc, self.ctx, self.name, self.sems = nc, ctx, name, []
        ctx.callback(self.close)

    def close(self):
        if self.sems:
            self.nc.clear_and_free_semaphores(self.sems)
            self.nc.all_engine_barrier()

    def sb(self, name, shape, dt=F32):
        return self.ctx.enter_context(self.nc.sbuf_tensor(f"{self.name}_{name}", shape, dt))

    def ps(self, name, shape=(P, CH)):
        return self.ctx.enter_context(self.nc.psum_tensor(f"{self.name}_{name}", list(shape), F32))

    def sem(self, name):
        self.sems.append(self.nc.alloc_semaphore(f"{self.name}_{name}"))
        return self.sems[-1]


def tok(c, n=CH):
    return bass.ds(c * n, n)


class Norm:
    SUB = CH // P

    def __init__(self, ph, name, consts, banks, rms=False):
        self.rms, self.banks, self.consts, self.G = rms, banks, consts, len(banks)
        self.mean_done = ph.sem(f"{name}_mean_done")
        self.centred_done = ph.sem(f"{name}_centred_done")
        self.squared_done = ph.sem(f"{name}_squared_done")
        self.var_done = ph.sem(f"{name}_var_done")
        self.var_copied = ph.sem(f"{name}_var_copied")
        self.power_done = ph.sem(f"{name}_power_done")
        self.diag_done = ph.sem(f"{name}_diag_done")
        self.spread_done = ph.sem(f"{name}_spread_done")
        self.centred = [None if rms else ph.sb(f"{name}_centred{g}", [P, CH]) for g in range(self.G)]
        self.squared = [ph.sb(f"{name}_squared{g}", [P, CH]) for g in range(self.G)]
        self.diag = [ph.sb(f"{name}_diag{g}", [P, self.SUB, P]) for g in range(self.G)]
        self.var = [ph.sb(f"{name}_var{g}", [P, self.SUB]) for g in range(self.G)]
        self.rsd = [ph.sb(f"{name}_rsd{g}", [P, self.SUB]) for g in range(self.G)]

    def tensor_mean(self, pe, group, g, x):
        pe.matmul(self.banks[g][:], self.consts["mean"][:], x, start=True, stop=True).then_inc(self.mean_done, 1)

    def vector_centre(self, dve, group, g, x):
        dve.wait_ge(self.mean_done, group * self.G + g + 1)
        dve.tensor_tensor(self.centred[g][:], x, self.banks[g][:], ALU.subtract).then_inc(self.centred_done, 1)

    def scalar_square(self, act, group, g, x=None):
        if not self.rms:
            act.wait_ge(self.centred_done, group * self.G + g + 1)
            x = self.centred[g][:]
        act.activation(self.squared[g][:], x, ACT.Square).then_inc(self.squared_done, 1)

    def tensor_var(self, pe, group, g):
        pe.wait_ge(self.squared_done, group * self.G + g + 1)
        for u in range(self.SUB):
            m = pe.matmul(self.banks[g][:, u:u + 1], self.squared[g][:, u * P:(u + 1) * P], self.consts["mean"][:, 0:1],
                          start=True, stop=True)
        m.then_inc(self.var_done, 1)

    def vector_var(self, dve, group, g):
        dve.wait_ge(self.var_done, group * self.G + g + 1)
        dve.tensor_scalar(self.var[g][:], self.banks[g][:, 0:self.SUB], EPS, None, ALU.add).then_inc(self.var_copied, 1)

    def pool_power(self, pool, group, g):
        pool.wait_ge(self.var_copied, group * self.G + g + 1)
        pool.tensor_tensor(self.rsd[g][:], self.var[g][:], self.consts["neg_half"][:, 0:self.SUB], ALU.pow).then_inc(self.power_done, 1)

    def vector_diag(self, dve, group, g):
        dve.wait_ge(self.power_done, group * self.G + g + 1)
        shape = [P, self.SUB, P]
        dve.tensor_tensor(self.diag[g][:], self.consts["ident"][:].unsqueeze(1).to_broadcast(shape),
                          self.rsd[g][:].unsqueeze(2).to_broadcast(shape), ALU.mult).then_inc(self.diag_done, 1)

    def tensor_spread(self, pe, group, g):
        pe.wait_ge(self.diag_done, group * self.G + g + 1)
        pe.matmul(self.banks[g][:], self.consts["ones"][:], self.diag[g][:].rearrange("p u m -> p (u m)"),
                  start=True, stop=True).then_inc(self.spread_done, 1)

    def vector_wait_spread(self, dve, group, g):
        dve.wait_ge(self.spread_done, group * self.G + g + 1)


N_EXP, N_FFN, FF = 8, 9, 512
NF = FF // P


def expert_buffers(nc, ctx, name):
    ph = Phase(nc, ctx, name)
    return [ph.sb(f"raw{i}", [P, N_FFN * FF]) for i in range(2)], ph.sem("loaded")


def load_experts(sp, w, raw, loaded):
    for i, weight in enumerate(("ffn_w1", "ffn_w2")):
        sp.dma_start(raw[i][:], w[weight]).then_inc(loaded, 16)


def ffn_setup(nc, ctx, name, w, raw, loaded):
    keep = Phase(nc, ctx, name)
    W = {}
    for m in ("w1", "w2"):
        W[m + "_hi"] = keep.sb(m + "_hi", [P, N_FFN * FF], F32R)
        W[m + "_lo"] = keep.sb(m + "_lo", [P, N_FFN * FF], F32R)
    W["spare"] = raw[0]
    W["b1"] = keep.sb("b1", [P, N_FFN * NF])
    W["b2"] = keep.sb("b2", [P, 1])
    W["eb2"] = keep.sb("eb2", [2 * N_EXP, D])
    W["rw"] = keep.sb("rw", [P, N_EXP])
    W["rb"] = keep.sb("rb", [1, N_EXP])
    W["pick"] = keep.sb("pick", [2 * N_EXP, N_EXP * P], F32R)
    W["iota"] = keep.sb("iota", [P, N_EXP])
    with ExitStack() as c2:
        ph = Phase(nc, c2, name + "_load")
        pickf = ph.sb("pickf", [2 * N_EXP, N_EXP * P])
        small_loaded, hi_done, lo_done = (ph.sem(n) for n in ("small_loaded", "hi_done", "lo_done"))
        block = c2.enter_context(nc.Block())

        @block.sync
        def _(sp):
            smalls = [("b1", "ffn_b1"), ("b2", "ffn_b2"), ("eb2", "ffn_eb2"), ("rw", "ffn_rw"), ("rb", "ffn_rb"), ("iota", "iota8")]
            for dst, src in smalls:
                sp.dma_start(W[dst][:], w[src]).then_inc(small_loaded, 16)
            sp.dma_start(pickf[:], w["pick8"]).then_inc(small_loaded, 16)
            sp.wait_ge(small_loaded, 16 * (len(smalls) + 1))

        @block.scalar
        def _(act):
            for i, name in enumerate(("w1", "w2")):
                act.wait_ge(loaded, 32)
                act.activation(W[name + "_hi"][:], raw[i][:], ACT.Copy).then_inc(hi_done, 1)
            act.wait_ge(small_loaded, 16 * 7)
            act.activation(W["pick"][:], pickf[:], ACT.Copy).then_inc(hi_done, 1)

        @block.vector
        def _(dve):
            for i, name in enumerate(("w1", "w2")):
                dve.wait_ge(hi_done, i + 1)
                dve.tensor_tensor(W[name + "_lo"][:], raw[i][:], W[name + "_hi"][:].bitcast(F32), ALU.subtract).then_inc(lo_done, 1)
    return W


def split_matmul(pe, out, w_hi, w_lo, x_hi, x_lo, start, stop):
    pe.matmul(out, w_hi, x_hi, start=start, stop=False)
    pe.matmul(out, w_hi, x_lo, start=False, stop=False)
    return pe.matmul(out, w_lo, x_hi, start=False, stop=stop)


def ffn_phase(nc, name, X, K, W):
    SUB = CH // P
    with ExitStack() as ctx:
        ph = Phase(nc, ctx, name)
        xn = ph.sb("xn", [P, CH])
        xn_hi = [ph.sb(f"xn_hi{i}", [P, CH], F32R) for i in range(2)]
        xn_lo = [ph.sb(f"xn_lo{i}", [P, CH], F32R) for i in range(2)]
        h = [W["spare"][:, i * NF * CH:(i + 1) * NF * CH].rearrange("p (f t) -> p f t", f=NF) for i in range(2)]
        h_hi = [ph.sb(f"h_hi{i}", [P, NF, CH], F32R) for i in range(2)]
        h_lo = [ph.sb(f"h_lo{i}", [P, NF, CH], F32R) for i in range(2)]
        lg = ph.sb("lg", [P, SUB, N_EXP])
        best = ph.sb("best", [P, SUB, 8])
        besti = ph.sb("besti", [P, SUB, 8], U32)
        bestf = ph.sb("bestf", [P, SUB, 8])
        gap = ph.sb("gap", [P, SUB])
        th = ph.sb("th", [P, SUB])
        wt = ph.sb("wt", [P, 2, SUB])
        comb1 = ph.sb("comb1", [P, SUB, N_EXP])
        comb2 = ph.sb("comb2", [P, SUB, N_EXP])
        comb = ph.sb("comb", [P, SUB, N_EXP])
        comb_parts = ph.sb("comb_parts", [P, SUB, 2, N_EXP], F32R)
        combT = [ph.sb(f"combT{i}", [2 * N_EXP, CH], F32R) for i in range(2)]
        wide = [ph.sb(f"wide{i}", [P, CH]) for i in range(2)]
        part = [ph.sb(f"part{i}", [P, CH]) for i in range(2)]
        bank_h = [ph.ps(f"bank_h{i}") for i in range(NF)]
        bank_o = [ph.ps(f"bank_o{i}") for i in range(2)]
        bank_prep = ph.ps("bank_prep")
        bank_wide = ph.ps("bank_wide")
        norm = Norm(ph, "norm", K, [bank_prep])
        s = {n: ph.sem(n) for n in (
            "normed", "split_x", "logits", "logits_copied", "best", "besti", "bestf", "gap", "tanh", "weights",
            "picked", "comb", "comb_hi", "comb_parts", "combT", "combT_copied", "up", "gelu_hi", "gelu_lo",
            "gelu_lo_pool", "down", "wide", "wide_copied", "weighted", "added", "adding", "shared_added")}
        block = ctx.enter_context(nc.Block())

        def prepare_tensor(pe, c, par, step):
            if step == 0:
                pe.wait_ge(s["combT_copied"], c)
                norm.tensor_mean(pe, c, 0, X[:, tok(c)])
            if step == 1:
                norm.tensor_var(pe, c, 0)
            if step == 2:
                norm.tensor_spread(pe, c, 0)
            if step == 3:
                pe.wait_ge(s["normed"], c + 1)
                for u in range(SUB):
                    out = bank_prep[:, u * N_EXP:(u + 1) * N_EXP]
                    pe.matmul(out, xn[:, u * P:(u + 1) * P], W["rw"][:], start=True, stop=False)
                    m = pe.matmul(out, K["ones_row"][:], W["rb"][:], start=False, stop=True)
                m.then_inc(s["logits"], 1)
            if step == 4:
                pe.wait_ge(s["comb_parts"], c + 1)
                for u in range(SUB):
                    m = pe.transpose(bank_prep[0:2 * N_EXP, u * P:(u + 1) * P], comb_parts[:, u].rearrange("p a e -> p (a e)").bitcast(F32), K["ident"][:])
                m.then_inc(s["combT"], 1)

        def prepare_scalar(act, c, par, step):
            if step == 0:
                norm.scalar_square(act, c, 0)
            if step == 1:
                act.wait_ge(s["gap"], c + 1)
                act.activation(th[:], gap[:], ACT.Tanh, scale=0.5).then_inc(s["tanh"], 1)

        def prepare_vector(dve, c, par, step):
            if step == 0:
                norm.vector_centre(dve, c, 0, X[:, tok(c)])
            if step == 1:
                norm.vector_var(dve, c, 0)
            if step == 2:
                norm.vector_diag(dve, c, 0)
            if step == 3:
                norm.vector_wait_spread(dve, c, 0)
                dve.tensor_tensor(xn[:], norm.centred[0][:], bank_prep[:], ALU.mult).then_inc(s["normed"], 1)
                dve.wait_ge(s["normed"], c + 1)
                if not isinstance(c, int):
                    dve.wait_ge(s["up"], (c - 1) * (N_FFN * NF))
                dve.tensor_copy(xn_hi[par][:], xn[:]).then_inc(s["split_x"], 1)
                dve.wait_ge(s["split_x"], 2 * c + 1)
                dve.tensor_tensor(xn_lo[par][:], xn[:], xn_hi[par][:].bitcast(F32), ALU.subtract).then_inc(s["split_x"], 1)
            if step == 4:
                dve.wait_ge(s["logits"], c + 1)
                dve.tensor_copy(lg[:], bank_prep[:, 0:SUB * N_EXP].rearrange("p (u e) -> p u e", u=SUB)).then_inc(s["logits_copied"], 1)
                dve.wait_ge(s["logits_copied"], 1)
                dve.wait_ge(s["logits_copied"], c + 1)
                for u in range(SUB):
                    m = dve.max(best[:, u, :], lg[:, u, :])
                m.then_inc(s["best"], 1)
                dve.wait_ge(s["best"], c + 1)
                dve.tensor_tensor(gap[:], best[:, :, 0], best[:, :, 1], ALU.subtract).then_inc(s["gap"], 1)
                for u in range(SUB):
                    m = dve.max_index(besti[:, u, :], best[:, u, :], lg[:, u, :])
                m.then_inc(s["besti"], 1)
                dve.wait_ge(s["besti"], c + 1)
                dve.tensor_copy(bestf[:], besti[:]).then_inc(s["bestf"], 1)
            if step == 5:
                dve.wait_ge(s["tanh"], c + 1)
                dve.tensor_scalar(wt[:, 0, :], th[:], 0.5, 0.5, ALU.mult, ALU.add)
                dve.tensor_scalar(wt[:, 1, :], th[:], -0.5, 0.5, ALU.mult, ALU.add).then_inc(s["weights"], 1)
                dve.wait_ge(s["weights"], c + 1)
                dve.wait_ge(s["bestf"], c + 1)
                for u in range(SUB):
                    dve.tensor_scalar(comb1[:, u, :], W["iota"][:], bestf[:, u, 0:1], wt[:, 0, u:u + 1], ALU.is_equal, ALU.mult)
                    m = dve.tensor_scalar(comb2[:, u, :], W["iota"][:], bestf[:, u, 1:2], wt[:, 1, u:u + 1], ALU.is_equal, ALU.mult)
                m.then_inc(s["picked"], 1)
                dve.wait_ge(s["picked"], c + 1)
                dve.tensor_tensor(comb[:], comb1[:], comb2[:], ALU.add).then_inc(s["comb"], 1)
                dve.wait_ge(s["comb"], c + 1)
                dve.tensor_copy(comb_parts[:, :, 0, :], comb[:]).then_inc(s["comb_hi"], 1)
                dve.wait_ge(s["comb_hi"], c + 1)
                dve.tensor_tensor(comb_parts[:, :, 1, :], comb[:], comb_parts[:, :, 0, :].bitcast(F32), ALU.subtract).then_inc(s["comb_parts"], 1)
            if step == 6:
                dve.wait_ge(s["combT"], c + 1)
                dve.tensor_copy(combT[par][:], bank_prep[0:2 * N_EXP, :]).then_inc(s["combT_copied"], 1)

        PE_AT, ACT_AT, DVE_AT = {1: 0, 2: 1, 4: 2, 6: 3, 8: 4}, {1: 0, 6: 1}, {1: 0, 2: 1, 3: 2, 4: 3, 6: 4, 7: 5, 8: 6}
        POOL_AT = 2
        AHEAD = {"gelu_hi": NF, "down": 1, "weighted": 2, "added": 1}

        def up(pe, c, par, e):
            n = c * N_FFN + e
            if e == N_FFN:
                pe.wait_ge(s["split_x"], 2 * c + 4)
                e, par = 0, 1 - par
            for f in range(NF):
                pe.wait_ge(s["gelu_hi"], n * NF + f + 1)
                w = slice(e * FF + f * P, e * FF + (f + 1) * P)
                split_matmul(pe, bank_h[f][:], W["w1_hi"][:, w], W["w1_lo"][:, w], xn_hi[par][:], xn_lo[par][:],
                             True, True).then_inc(s["up"], 1)

        def down(pe, c, par, e):
            n = c * N_FFN + e
            ep = (par + e) % 2
            if e:
                if e == 1:
                    pe.wait_ge(s["combT_copied"], c + 1)
                pe.wait_ge(s["wide_copied"], c * N_EXP + e - 1)
                pick = W["pick"][:, (e - 1) * P:e * P]
                pe.matmul(bank_wide[:], pick, combT[par][:], start=True, stop=True).then_inc(s["wide"], 1)
            if e == 0:
                pe.wait_ge(s["weighted"], c * N_EXP - 1 + 2)
            elif e == 1:
                pe.wait_ge(s["weighted"], c * N_EXP + 2)
            elif e == 2:
                pe.wait_ge(s["shared_added"], c + 1)
            else:
                pe.wait_ge(s["weighted"], c * N_EXP + e - 2 + 2)
            out = bank_o[ep][:]
            if e == 0:
                pe.wait_ge(s["combT_copied"], c + 1)
                pe.matmul(out, W["eb2"][:], combT[par][:].bitcast(F32), start=True, stop=False)
            for f in range(NF):
                w = slice((e * NF + f) * D, (e * NF + f + 1) * D)
                if f < NF - 1:
                    pe.wait_ge(s["gelu_lo"], n * (NF - 1) + f + 1)
                else:
                    pe.wait_ge(s["gelu_lo_pool"], n + 1)
                m = split_matmul(pe, out, W["w2_hi"][:, w], W["w2_lo"][:, w], h_hi[ep][:, f, :], h_lo[ep][:, f, :],
                                 f == 0 and e > 0, f == NF - 1)
            m.then_inc(s["down"], 1)

        @block.tensor
        def _(pe):
            def chunk(c, par):
                for e in range(1, N_FFN + 1):
                    up(pe, c, par, e)
                    down(pe, c, par, e - 1)
                    if e in PE_AT:
                        prepare_tensor(pe, c + 1, 1 - par, PE_AT[e])
            pe.sem_inc(s["down"], AHEAD["down"])
            for step in range(5):
                prepare_tensor(pe, 0, 0, step)
            pe.wait_ge(s["split_x"], 2)
            up(pe, 0, 0, 0)
            with pe.Fori(0, NCH // 2) as pair:
                for par in range(2):
                    chunk(pair * 2 + par, par)

        @block.scalar
        def _(act):
            def hidden(c, par, e):
                n = c * N_FFN + e
                ep = (par + e) % 2
                for f in range(NF):
                    act.wait_ge(s["up"], n * NF + f + 1)
                    if f == 0:
                        act.wait_ge(s["down"], n - 1 + 1)
                    at = e % N_FFN * NF + f
                    act.activation(h[ep][:, f, :], bank_h[f][:], ACT.Gelu_apprx_tanh, bias=W["b1"][:, at:at + 1])
                    act.activation(h_hi[ep][:, f, :], bank_h[f][:], ACT.Gelu_apprx_tanh, bias=W["b1"][:, at:at + 1]).then_inc(s["gelu_hi"], 1)

            def chunk(c, par):
                for e in range(1, N_FFN + 1):
                    hidden(c, par, e)
                    if e >= 2:
                        q = c * N_EXP + e - 2
                        act.wait_ge(s["wide"], q + 1)
                        act.wait_ge(s["weighted"], q - 1 + 2)
                        act.activation(wide[e % 2][:], bank_wide[:], ACT.Copy).then_inc(s["wide_copied"], 1)
                    if e in ACT_AT:
                        prepare_scalar(act, c + 1, 1 - par, ACT_AT[e])
            act.sem_inc(s["gelu_hi"], AHEAD["gelu_hi"])
            for step in range(2):
                prepare_scalar(act, 0, 0, step)
            hidden(0, 0, 0)
            with act.Fori(0, NCH // 2) as pair:
                for par in range(2):
                    chunk(pair * 2 + par, par)

        @block.vector
        def _(dve):
            def hidden_low(c, par, e):
                n = c * N_FFN + e
                ep = (par + e) % 2
                for f in range(NF - 1):
                    dve.wait_ge(s["gelu_hi"], n * NF + f + 1 + NF)
                    dve.tensor_tensor(h_lo[ep][:, f, :], h[ep][:, f, :], h_hi[ep][:, f, :].bitcast(F32), ALU.subtract).then_inc(s["gelu_lo"], 1)

            def chunk(c, par):
                for e in range(1, N_FFN + 1):
                    n = c * N_FFN + e
                    hidden_low(c, par, e)
                    if e == 1:
                        dve.wait_ge(s["down"], n + 1)
                        dve.scalar_tensor_tensor(X[:, tok(c)], bank_o[(par + e - 1) % 2][:], W["b2"][:, 0:1], X[:, tok(c)],
                                                 ALU.add, ALU.add).then_inc(s["shared_added"], 1)
                    if e >= 2:
                        q = c * N_EXP + e - 2
                        dve.wait_ge(s["down"], n + 1)
                        dve.wait_ge(s["wide_copied"], q + 1)
                        dve.wait_ge(s["added"], q - 1 + 1)
                        dve.tensor_tensor(part[e % 2][:], bank_o[(par + e - 1) % 2][:], wide[e % 2][:], ALU.mult).then_inc(s["weighted"], 1)
                    if e in DVE_AT:
                        prepare_vector(dve, c + 1, 1 - par, DVE_AT[e])
            dve.sem_inc(s["weighted"], AHEAD["weighted"])
            for step in range(7):
                prepare_vector(dve, 0, 0, step)
            hidden_low(0, 0, 0)
            with dve.Fori(0, NCH // 2) as pair:
                for par in range(2):
                    chunk(pair * 2 + par, par)

        @block.gpsimd
        def _(pool):
            def hidden_low(c, par, e):
                ep = (par + e) % 2
                pool.wait_ge(s["gelu_hi"], (c * N_FFN + e) * NF + NF + NF)
                pool.tensor_tensor(h_lo[ep][:, NF - 1, :], h[ep][:, NF - 1, :], h_hi[ep][:, NF - 1, :].bitcast(F32), ALU.subtract).then_inc(s["gelu_lo_pool"], 1)

            def chunk(c, par):
                for e in range(1, N_FFN + 1):
                    hidden_low(c, par, e)
                    if e >= 2:
                        q = c * N_EXP + e - 2
                        pool.wait_ge(s["weighted"], q + 1 + 2)
                        if e == 2:
                            pool.wait_ge(s["shared_added"], c + 1)
                        pool.wait_ge(s["added"], q + 1)
                        pool.sem_inc(s["adding"], 1)
                        pool.tensor_tensor(X[:, tok(c)], X[:, tok(c)], part[e % 2][:], ALU.add).then_inc(s["added"], 1)
                    if e == POOL_AT:
                        norm.pool_power(pool, c + 1, 0)
            pool.sem_inc(s["added"], AHEAD["added"])
            norm.pool_power(pool, 0, 0)
            hidden_low(0, 0, 0)
            with pool.Fori(0, NCH // 2) as pair:
                for par in range(2):
                    chunk(pair * 2 + par, par)


def ffn_stage(nc, name, X, K, w, raw, loaded):
    with ExitStack() as ctx:
        W = ffn_setup(nc, ctx, name + "_w", w, raw, loaded)
        ffn_phase(nc, name, X, K, W)


N_STATE = 16
INNER = 2 * D
CONV = 4
SCAN_CHUNK = 64


def after(engine, sem, count):
    if not isinstance(count, int) or count > 0:
        engine.wait_ge(sem, count)


def mamba_phase(nc, name, X, K, w, experts):
    G, NH = 2, 2
    AHEAD = 3
    WIDE = 4
    SUB = CH // P
    with ExitStack() as ctx:
        ph = Phase(nc, ctx, name)
        w_in = ph.sb("w_in", [P, 4, P])
        conv_w = ph.sb("conv_w", [P, NH, CONV])
        vecs = ph.sb("vecs", [P, 6, NH])
        w_proj = ph.sb("w_proj", [P, NH, P])
        w_dt = ph.sb("w_dt", [HEADS, INNER])
        w_out = ph.sb("w_out", [P, NH, D])
        w_gain = ph.sb("w_gain", [P, NH, D])
        out_bias = ph.sb("out_bias", [P, 1])
        select = ph.sb("select", [P, 2 * N_STATE + 1])
        pick = ph.sb("pick", [P, 2 * N_STATE, P], F32R)
        mean_inner = ph.sb("mean_inner", [P, P])
        restart = ph.sb("restart", [P, CH])
        a_exp = ph.sb("a_exp", [P, NH])
        a_neg = ph.sb("a_neg", [P, NH])
        xe = [ph.sb(f"xe{p}", [P, NH, CONV - 1 + CH]) for p in range(G)]
        z = [ph.sb(f"z{p}", [P, NH, CH]) for p in range(G)]
        xc = [ph.sb(f"xc{p}", [P, NH, CH]) for p in range(G)]
        proj = [ph.sb(f"proj{p}", [P, CH], F32R) for p in range(G)]
        decay = [ph.sb(f"decay{p}", [P, NH, CH]) for p in range(G)]
        u = [ph.sb(f"u{p}", [P, NH, CH]) for p in range(G)]
        xn = ph.sb("xn", [P, CH])
        conv = ph.sb("conv", [P, NH, CH])
        proj_hi = ph.sb("proj_hi", [P, CH], F32R)
        dt_raw = ph.sb("dt_raw", [HEADS, CH])
        v_abs = ph.sb("v_abs", [P, NH, CH])
        v_relu = ph.sb("v_relu", [P, NH, CH])
        dt = ph.sb("dt", [P, NH, CH])
        b_wide = [ph.sb(f"b_wide{r}", [P, CH]) for r in range(WIDE)]
        c_wide = [ph.sb(f"c_wide{r}", [P, CH]) for r in range(WIDE)]
        drive = [[ph.sb(f"drive{r}{h}", [P, CH]) for h in range(NH)] for r in range(2)]
        state = [[ph.sb(f"state{r}{h}", [P, CH]) for h in range(NH)] for r in range(2)]
        part = [[ph.sb(f"part{r}{h}", [P, CH]) for h in range(NH)] for r in range(2)]
        carry = ph.sb("carry", [P, NH, N_STATE])
        y1 = ph.sb("y1", [P, NH, CH])
        y2 = ph.sb("y2", [P, NH, CH])
        centred, squared = y2, y1
        var = ph.sb("var", [P, SUB])
        rsd = ph.sb("rsd", [P, SUB])
        diag = ph.sb("diag", [P, SUB, P])
        spread = ph.sb("spread", [P, CH])
        bank_y = [ph.ps(f"bank_y{h}") for h in range(NH)]
        bank_b, bank_c = ph.ps("bank_b"), ph.ps("bank_c")
        front = [ph.ps(f"front{i}") for i in range(2)]
        bank_n = ph.ps("bank_n")
        back = ph.ps("back")
        n1 = Norm(ph, "n1", K, [bank_n])
        s = {n: ph.sem(n) for n in (
            "loaded", "const", "a_exp", "a_neg", "setup", "bias", "out_bias", "xn", "proj_in", "xe", "prefix", "z", "conv", "xc",
            "proj", "proj_hi", "dt_raw", "split", "v", "v_abs", "v_relu", "v_exp", "v_log", "dt", "cum", "decay", "u",
            "b_bank", "c_bank", "b_wide", "c_wide", "drive", "state", "carried", "part", "summed", "y1", "y2", "mean", "centred",
            "squared", "var", "var_copied", "power", "diag", "spread", "spread_copied", "out", "weighted", "added")}
        block = ctx.enter_context(nc.Block())
        LOADS = ((w_in, "m_win"), (conv_w, "m_conv"), (vecs, "m_vecs"), (w_proj, "m_wproj"), (w_dt, "m_wdt"),
                 (w_out, "m_wout"), (select, "m_select"))
        CONV_B, B_DT, A_LOG, D_SKIP, LN_G, LN_B = range(6)

        @block.sync
        def _(sp):
            for dst, src in LOADS:
                sp.dma_start(dst[:], w[src]).then_inc(s["loaded"], 16)
            load_experts(sp, w, *experts)

        @block.tensor
        def _(pe):
            pe.wait_ge(s["loaded"], 16 * len(LOADS))
            for h in range(NH):
                m = pe.matmul(back[:, 0:1], w_out[:, h, :], vecs[:, LN_B, h:h + 1], start=h == 0, stop=h == NH - 1)
            m.then_inc(s["bias"], 1)

            def norm(m, n):
                if n == 5:
                    after(pe, s["xn"], m)
                    n1.tensor_mean(pe, m, 0, X[:, tok(m)])
                if n == 9:
                    n1.tensor_var(pe, m, 0)
                if n == 14:
                    n1.tensor_spread(pe, m, 0)

            def prepare(m, p, n):
                if n == 1:
                    after(pe, s["v_relu"], m * NH)
                    pe.wait_ge(s["xn"], m + 1)
                    for h in range(NH):
                        pe.matmul(front[h][:], w_in[:, h, :], xn[:], start=True, stop=True).then_inc(s["proj_in"], 1)
                if n == 2:
                    for h in range(NH):
                        pe.wait_ge(s["xe"], m * NH + h + 1)
                        pe.matmul(front[h][:], w_in[:, NH + h, :], xn[:], start=True, stop=True).then_inc(s["proj_in"], 1)
                if n == 7:
                    pe.wait_ge(s["z"], m * NH + 1)
                    for h in range(NH):
                        pe.wait_ge(s["xc"], m * NH + h + 1)
                        mm = pe.matmul(front[0][:], w_proj[:, h, :], xc[p][:, h, :], start=h == 0, stop=h == NH - 1)
                    mm.then_inc(s["proj"], 1)
                if n == 9:
                    pe.wait_ge(s["z"], (m + 1) * NH)
                    pe.wait_ge(s["dt_raw"], m + 1)
                    pe.matmul(front[1][:], w_dt[:, 0:P], dt_raw[:], start=True, stop=True).then_inc(s["v"], 1)
                if n == 10:
                    pe.wait_ge(s["split"], m + 1)
                    pe.matmul(front[0][:], w_dt[:, P:INNER], dt_raw[:], start=True, stop=True).then_inc(s["v"], 1)

            def broadcast(c, p, n):
                k = c * N_STATE + n
                if n == 0:
                    pe.wait_ge(s["split"], c + 1)
                for bank, row, bank_done, wide_done in ((bank_b, n, "b_bank", "b_wide"), (bank_c, N_STATE + n, "c_bank", "c_wide")):
                    after(pe, s[wide_done], k)
                    pe.matmul(bank[:], pick[0:112, row, :], proj[p][0:112, :], start=True, stop=True).then_inc(s[bank_done], 1)

            def finish(f, n):
                if n == 1:
                    for h in range(NH):
                        pe.wait_ge(s["y2"], f * NH + h + 1)
                        mm = pe.matmul(back[:], mean_inner[:], y2[:, h, :], start=h == 0, stop=h == NH - 1)
                    mm.then_inc(s["mean"], 1)
                if n == 5:
                    pe.wait_ge(s["squared"], (f + 1) * NH)
                    for t in range(SUB):
                        for h in range(NH):
                            mm = pe.matmul(back[:, t:t + 1], squared[:, h, t * P:(t + 1) * P], mean_inner[:, 0:1], start=h == 0, stop=h == NH - 1)
                    mm.then_inc(s["var"], 1)
                if n == 10:
                    pe.wait_ge(s["diag"], f + 1)
                    pe.matmul(back[:], K["ones"][:], diag[:].rearrange("p t m -> p (t m)"), start=True, stop=True).then_inc(s["spread"], 1)
                if n == 12:
                    pe.wait_ge(s["spread_copied"], f + 1)
                    for h in range(NH):
                        mm = pe.matmul(back[:], w_gain[:, h, :], centred[:, h, :], start=h == 0, stop=h == NH - 1)
                    mm.then_inc(s["out"], 1)

            def chunk(b, g, first):
                c = b * G + g
                for n in range(N_STATE):
                    broadcast(c + (n + AHEAD) // N_STATE, (g + (n + AHEAD) // N_STATE) % 2, (n + AHEAD) % N_STATE)
                    for h in range(NH):
                        k = (c * N_STATE + n) * NH + h
                        if n == 0:
                            after(pe, s["y1"], (c - 1) * NH + h + 1)
                        pe.wait_ge(s["part"], k + 1)
                        pe.matmul(bank_y[h][:], K["ident"][:], part[n % 2][h][:], start=n == 0, stop=n == N_STATE - 1).then_inc(s["summed"], 1)
                    if not first:
                        finish(c - 1, n)
                    prepare(c + 1, 1 - g, n)
                    norm(c + 2, n)

            for n in range(N_STATE):
                norm(0, n)
            for n in range(N_STATE):
                prepare(0, 0, n)
                norm(1, n)
            pe.wait_ge(s["setup"], 2)
            pe.wait_ge(s["out_bias"], 1)
            for n in range(AHEAD):
                broadcast(0, 0, n)
            chunk(0, 0, True)
            chunk(0, 1, False)
            with pe.Fori(1, BATCH) as b:
                for g in range(G):
                    chunk(b, g, False)
            for n in range(N_STATE):
                finish(NCH - 1, n)

        @block.scalar
        def _(act):
            act.wait_ge(s["loaded"], 16 * len(LOADS))
            act.activation(a_exp[:], vecs[:, A_LOG, :], ACT.Exp).then_inc(s["a_exp"], 1)
            act.wait_ge(s["a_exp"], 1)
            act.activation(a_neg[:], a_exp[:], ACT.Copy, scale=-1.0).then_inc(s["a_neg"], 1)
            act.wait_ge(s["bias"], 1)
            act.activation(out_bias[:], back[:, 0:1], ACT.Copy).then_inc(s["out_bias"], 1)
            act.wait_ge(s["a_neg"], 1)
            act.wait_ge(s["const"], 1)

            def norm(m, n):
                if n == 8:
                    n1.scalar_square(act, m, 0)

            def prepare(m, p, b, n):
                if n == 2:
                    for h in range(NH):
                        act.wait_ge(s["proj_in"], m * 4 + h + 1)
                        act.activation(xe[p][:, h, CONV - 1:], front[h][:], ACT.Copy).then_inc(s["xe"], 1)
                    if p == 1:
                        act.activation(xe[1][:, :, 0:CONV - 1], xe[0][:, :, CH:], ACT.Copy).then_inc(s["prefix"], 1)
                if n == 3:
                    after(act, s["y2"], (m - 1) * NH)
                    for h in range(NH):
                        act.wait_ge(s["proj_in"], m * 4 + 2 + h + 1)
                        act.activation(z[p][:, h, :], front[h][:], ACT.Silu).then_inc(s["z"], 1)
                if n == 7:
                    after(act, s["y1"], (m - 1) * NH)
                    for h in range(NH):
                        act.wait_ge(s["conv"], (m * CONV + CONV - 1) * NH + h + 1)
                        act.activation(xc[p][:, h, :], conv[:, h, :], ACT.Silu).then_inc(s["xc"], 1)
                if n == 8:
                    act.wait_ge(s["proj"], m + 1)
                    act.activation(dt_raw[:], front[0][0:HEADS, :], ACT.Copy).then_inc(s["dt_raw"], 1)
                    act.activation(proj_hi[:], front[0][:], ACT.Copy).then_inc(s["proj_hi"], 1)
                if n in (10, 11):
                    for h in (n - 10,):
                        act.wait_ge(s["v"], m * NH + h + 1)
                        act.activation(v_abs[:, h, :], front[1 - h][:], ACT.Abs, bias=vecs[:, B_DT, h:h + 1]).then_inc(s["v_abs"], 1)
                        act.activation(v_relu[:, h, :], front[1 - h][:], ACT.Relu, bias=vecs[:, B_DT, h:h + 1]).then_inc(s["v_relu"], 1)
                if n == 11:
                    for h in range(NH):
                        act.wait_ge(s["v_abs"], m * NH + h + 1)
                        act.activation(v_abs[:, h, :], v_abs[:, h, :], ACT.Exp, scale=-1.0).then_inc(s["v_exp"], 1)
                    for h in range(NH):
                        act.wait_ge(s["v_exp"], m * NH + h + 1)
                        act.activation(v_abs[:, h, :], v_abs[:, h, :], ACT.Ln, bias=K["ones"][:, 0:1]).then_inc(s["v_log"], 1)
                if n == 15:
                    for h in range(NH):
                        act.wait_ge(s["cum"], m * NH + h + 1)
                        act.activation(decay[p][:, h, :], decay[p][:, h, :], ACT.Exp, scale=a_neg[:, h:h + 1]).then_inc(s["decay"], 1)

            def copy_wide(c, n):
                k = c * N_STATE + n
                act.wait_ge(s["b_bank"], k + 1)
                after(act, s["drive"], (k + 1 - WIDE) * NH)
                act.activation(b_wide[n % WIDE][:], bank_b[:], ACT.Copy).then_inc(s["b_wide"], 1)
                act.wait_ge(s["c_bank"], k + 1)
                after(act, s["part"], (k + 1 - WIDE) * NH)
                act.activation(c_wide[n % WIDE][:], bank_c[:], ACT.Copy).then_inc(s["c_wide"], 1)

            def finish(f, n):
                if n == 4:
                    for h in range(NH):
                        act.wait_ge(s["centred"], f * NH + h + 1)
                        act.activation(squared[:, h, :], centred[:, h, :], ACT.Square).then_inc(s["squared"], 1)
                if n == 11:
                    act.wait_ge(s["spread"], f + 1)
                    act.activation(spread[:], back[:], ACT.Copy).then_inc(s["spread_copied"], 1)

            def chunk(b, g, first):
                c = b * G + g
                for n in range(N_STATE):
                    copy_wide(c + (n + AHEAD) // N_STATE, (n + AHEAD) % N_STATE)
                    if g == 0:
                        for h in range(NH):
                            act.wait_ge(s["state"], (c * N_STATE + n) * NH + h + 1)
                            act.activation(carry[:, h, n:n + 1], state[n % 2][h][:, CH - 1:CH], ACT.Copy).then_inc(s["carried"], 1)
                    if not first:
                        finish(c - 1, n)
                    prepare(c + 1, 1 - g, b, n)
                    norm(c + 2, n)

            for n in range(N_STATE):
                norm(0, n)
            for n in range(N_STATE):
                prepare(0, 0, 0, n)
                norm(1, n)
            for n in range(AHEAD):
                copy_wide(0, n)
            chunk(0, 0, True)
            chunk(0, 1, False)
            with act.Fori(1, BATCH) as b:
                for g in range(G):
                    chunk(b, g, False)
            for n in range(N_STATE):
                finish(NCH - 1, n)

        @block.vector
        def _(dve):
            dve.wait_ge(s["loaded"], 16 * len(LOADS))
            shape = [P, 2 * N_STATE, P]
            dve.tensor_copy(pick[:], select[:, 0:2 * N_STATE].unsqueeze(2).to_broadcast(shape)).then_inc(s["setup"], 1)
            for h in range(NH):
                m = dve.tensor_scalar(w_gain[:, h, :], w_out[:, h, :], vecs[:, LN_G, h:h + 1], None, ALU.mult)
            m.then_inc(s["setup"], 1)
            dve.wait_ge(s["const"], 1)

            def norm(m, n):
                if n == 7:
                    n1.vector_centre(dve, m, 0, X[:, tok(m)])
                if n == 10:
                    n1.vector_var(dve, m, 0)
                if n == 13:
                    n1.vector_diag(dve, m, 0)

            def prepare(m, p, b, n):
                if n == 0:
                    n1.vector_wait_spread(dve, m, 0)
                    dve.tensor_tensor(xn[:], n1.centred[0][:], bank_n[:], ALU.mult).then_inc(s["xn"], 1)
                if 3 <= n < 3 + CONV:
                    j = n - 3
                    for h in range(NH):
                        if j == 0:
                            dve.wait_ge(s["xe"], m * NH + h + 1)
                            if p == 1:
                                dve.wait_ge(s["prefix"], b + 1)
                            dve.tensor_scalar(conv[:, h, :], xe[p][:, h, 0:CH], conv_w[:, h, 0:1], vecs[:, CONV_B, h:h + 1],
                                              ALU.mult, ALU.add).then_inc(s["conv"], 1)
                        else:
                            dve.wait_ge(s["conv"], (m * CONV + j - 1) * NH + h + 1)
                            dve.scalar_tensor_tensor(conv[:, h, :], xe[p][:, h, j:j + CH], conv_w[:, h, j:j + 1], conv[:, h, :],
                                                     ALU.mult, ALU.add).then_inc(s["conv"], 1)
                if n == 9:
                    dve.wait_ge(s["proj_hi"], m + 1)
                    dve.scalar_tensor_tensor(proj[p][:], proj_hi[:].bitcast(F32), select[:, 2 * N_STATE:], front[0][:],
                                             ALU.mult, ALU.add).then_inc(s["split"], 1)
                if n == 14:
                    for h in range(NH):
                        dve.wait_ge(s["v_log"], m * NH + h + 1)
                        dve.tensor_tensor(dt[:, h, :], v_relu[:, h, :], v_abs[:, h, :], ALU.add).then_inc(s["dt"], 1)
                    for h in range(NH):
                        dve.wait_ge(s["dt"], m * NH + h + 1)
                        dve.tensor_tensor_scan(decay[p][:, h, :], restart[:], dt[:, h, :], 0.0, ALU.mult, ALU.add).then_inc(s["cum"], 1)
                    for h in range(NH):
                        dve.tensor_tensor(u[p][:, h, :], dt[:, h, :], xc[p][:, h, :], ALU.mult).then_inc(s["u"], 1)

            def take_sum(f, p):
                for h in range(NH):
                    dve.wait_ge(s["summed"], ((f + 1) * N_STATE - 1) * NH + h + 1)
                    dve.scalar_tensor_tensor(y1[:, h, :], xc[p][:, h, :], vecs[:, D_SKIP, h:h + 1], bank_y[h][:], ALU.mult, ALU.add).then_inc(s["y1"], 1)

            def finish(f, p, n):
                if n == 0:
                    for h in range(NH):
                        dve.wait_ge(s["y1"], f * NH + h + 1)
                        dve.tensor_tensor(y2[:, h, :], y1[:, h, :], z[p][:, h, :], ALU.mult).then_inc(s["y2"], 1)
                if n == 2:
                    dve.wait_ge(s["mean"], f + 1)
                    for h in range(NH):
                        dve.tensor_tensor(centred[:, h, :], y2[:, h, :], back[:], ALU.subtract).then_inc(s["centred"], 1)
                if n == 7:
                    dve.wait_ge(s["var"], f + 1)
                    dve.tensor_scalar(var[:], back[:, 0:SUB], EPS, None, ALU.add).then_inc(s["var_copied"], 1)
                if n == 9:
                    dve.wait_ge(s["power"], f + 1)
                    shape = [P, SUB, P]
                    dve.tensor_tensor(diag[:], K["ident"][:].unsqueeze(1).to_broadcast(shape), rsd[:].unsqueeze(2).to_broadcast(shape),
                                      ALU.mult).then_inc(s["diag"], 1)
                if n == 14:
                    dve.wait_ge(s["out"], f + 1)
                    dve.tensor_tensor(spread[:], back[:], spread[:], ALU.mult).then_inc(s["weighted"], 1)
                if n == 15:
                    dve.wait_ge(s["weighted"], f + 1)
                    dve.scalar_tensor_tensor(X[:, tok(f)], spread[:], out_bias[:, 0:1], X[:, tok(f)], ALU.add, ALU.add).then_inc(s["added"], 1)

            def chunk(b, g, first):
                c = b * G + g
                for n in range(N_STATE):
                    for h in range(NH):
                        k = (c * N_STATE + n) * NH + h
                        if n == 0:
                            dve.wait_ge(s["decay"], c * NH + h + 1)
                            if g == 1:
                                dve.wait_ge(s["carried"], (b + 1) * N_STATE * NH)
                        if g == 0 and n >= 2:
                            dve.wait_ge(s["carried"], b * N_STATE * NH + (n - 2) * NH + h + 1)
                        dve.wait_ge(s["drive"], k + 1)
                        start = carry[:, h, n:n + 1] if g else 0.0
                        dve.tensor_tensor_scan(state[n % 2][h][:], decay[g][:, h, :], drive[n % 2][h][:], start, ALU.mult, ALU.add).then_inc(s["state"], 1)
                    if n == 0 and not first:
                        take_sum(c - 1, 1 - g)
                    for h in range(NH):
                        k = (c * N_STATE + n) * NH + h
                        dve.wait_ge(s["c_wide"], c * N_STATE + n + 1)
                        after(dve, s["summed"], k - 2 * NH + 1)
                        dve.wait_ge(s["state"], k + 1)
                        dve.tensor_tensor(part[n % 2][h][:], state[n % 2][h][:], c_wide[n % WIDE][:], ALU.mult).then_inc(s["part"], 1)
                    if not first:
                        finish(c - 1, 1 - g, n)
                    prepare(c + 1, 1 - g, b, n)
                    norm(c + 2, n)

            for n in range(N_STATE):
                norm(0, n)
            for n in range(N_STATE):
                prepare(0, 0, 0, n)
                norm(1, n)
            dve.wait_ge(s["out_bias"], 1)
            chunk(0, 0, True)
            chunk(0, 1, False)
            with dve.Fori(1, BATCH) as b:
                for g in range(G):
                    chunk(b, g, False)
            take_sum(NCH - 1, 1)
            for n in range(N_STATE):
                finish(NCH - 1, 1, n)

        @block.gpsimd
        def _(pool):
            pool.memset(mean_inner[:], 1.0 / INNER)
            pool.memset(xe[0][:, :, 0:CONV - 1], 0.0)
            pool.memset(restart[:].rearrange("p (t m) -> p t m", m=SCAN_CHUNK)[:, :, 0:1], 0.0)
            pool.memset(restart[:].rearrange("p (t m) -> p t m", m=SCAN_CHUNK)[:, :, 1:], 1.0).then_inc(s["const"], 1)

            def chunk(b, g, first):
                c = b * G + g
                for n in range(N_STATE):
                    if n == 0:
                        pool.wait_ge(s["u"], (c + 1) * NH)
                    for h in range(NH):
                        k = (c * N_STATE + n) * NH + h
                        pool.wait_ge(s["b_wide"], c * N_STATE + n + 1)
                        after(pool, s["state"], k - 2 * NH + 1)
                        pool.tensor_tensor(drive[n % 2][h][:], u[g][:, h, :], b_wide[n % WIDE][:], ALU.mult).then_inc(s["drive"], 1)
                    if n == 10 and not first:
                        power(c - 1)
                    if n == 13:
                        n1.pool_power(pool, c + 2, 0)

            def power(f):
                pool.wait_ge(s["var_copied"], f + 1)
                pool.tensor_tensor(rsd[:], var[:], K["neg_half"][:, 0:SUB], ALU.pow).then_inc(s["power"], 1)

            for m in range(2):
                n1.pool_power(pool, m, 0)
            chunk(0, 0, True)
            chunk(0, 1, False)
            with pool.Fori(1, BATCH) as b:
                for g in range(G):
                    chunk(b, g, False)
            power(NCH - 1)


QUADS = HEADS // 4
NSTEP = QUADS * BATCH
NT = SEQ // P
GRID = 32
NEG = -1e30
REL, QK = 3 * GRID, 3 * HD
ROWS_A = REL + QK
ROWS_B = ROWS_A + 2


def attnb_phase(nc, name, X, K, w, ctx):
    q_dram = nc.dram_tensor(f"{name}_q", (NSTEP, 2, 4 * HD, SEQ), F32, kind="Internal").ap()
    k_dram = nc.dram_tensor(f"{name}_k", (NSTEP, 2, 4 * HD, SEQ), F32, kind="Internal").ap()
    rel_dram = nc.dram_tensor(f"{name}_rel", (QUADS, 4, REL, SEQ), F32, kind="Internal").ap()
    o_dram = nc.dram_tensor(f"{name}_o", (NSTEP + 1, 64, SEQ), F32, kind="Internal").ap()
    with ExitStack() as inner:
        keep = Phase(nc, inner, name)
        V = keep.sb("V", [P, BATCH * NT, D])
        grid_k = keep.sb("grid_k", [REL, SEQ], F32R)
        attnb_rel(nc, name, w, rel_dram, grid_k)
        attnb_project(nc, name, X, K, w, q_dram, k_dram, V)
        attnb_scores(nc, name, K, w, q_dram, k_dram, rel_dram, grid_k, V, o_dram)
    experts = expert_buffers(nc, ctx, name + "_experts")
    attnb_out(nc, name, X, w, o_dram, experts=experts)
    return experts


def attnb_rel(nc, name, w, rel_dram, grid_k):
    with ExitStack() as ctx:
        ph = Phase(nc, ctx, name + "r")
        grid = ph.sb("grid", [REL, SEQ])
        biases = ph.sb("biases", [GRID, HEADS, REL])
        masks = ph.sb("masks", [REL, 2])
        grid_high = ph.sb("grid_high", [REL, SEQ], F32R)
        high = [ph.sb(f"high{p}", [REL, SEQ], F32R) for p in range(2)]
        rows = [ph.sb(f"rows{p}", [REL, SEQ], F32R) for p in range(2)]
        bias = [ph.sb(f"bias{p}", [GRID, REL]) for p in range(2)]
        bank = [ph.ps(f"bank{p}", (P, SEQ)) for p in range(2)]
        loaded, picked, made, grid_high_done, high_done, rows_done, grid_done, stored0, stored1 = (ph.sem(n) for n in (
            "loaded", "picked", "made", "grid_high_done", "high_done", "rows_done", "grid_done", "stored0", "stored1"))
        stored = [stored0, stored1]
        block = ctx.enter_context(nc.Block())

        @block.sync
        def _(sp):
            sp.dma_start(grid[:], w["grid3"]).then_inc(loaded, 16)
            sp.dma_start(biases[:], w["ab_rel"].rearrange("p (h r) -> p h r", h=HEADS)).then_inc(loaded, 16)
            sp.dma_start(masks[:], w["negmask"]).then_inc(loaded, 16)
            with sp.Fori(0, HEADS // 2) as pair:
                for p in range(2):
                    h = pair * 2 + p
                    sp.wait_ge(rows_done, h + 1 + 2)
                    sp.dma_start(rel_dram.rearrange("q g r t -> (q g) r t")[bass.ds(h, 1), :, :], rows[p][:].bitcast(F32)).then_inc(stored[p], 16)
            for p in range(2):
                sp.wait_ge(stored[p], 16 * HEADS // 2)

        @block.tensor
        def _(pe):
            pe.wait_ge(loaded, 48)
            with pe.Fori(0, HEADS // 2) as pair:
                for p in range(2):
                    h = pair * 2 + p
                    pe.wait_ge(picked, h + 1)
                    pe.wait_ge(rows_done, h + 1)
                    for half in range(2):
                        n = slice(half * CH, (half + 1) * CH)
                        m = pe.matmul(bank[p][0:REL, n], bias[p][:], grid[0:GRID, n], start=True, stop=True)
                    m.then_inc(made, 1)

        @block.scalar
        def _(act):
            act.wait_ge(loaded, 48)
            act.activation(grid_high[:], grid[:], ACT.Copy).then_inc(grid_high_done, 1)
            with act.Fori(0, HEADS // 2) as pair:
                for p in range(2):
                    h = pair * 2 + p
                    act.wait_ge(made, h + 1 + 2)
                    act.activation(high[p][:], bank[p][0:REL, :], ACT.Copy).then_inc(high_done, 1)

        @block.vector
        def _(dve):
            dve.wait_ge(loaded, 48)
            dve.wait_ge(grid_high_done, 1)
            dve.scalar_tensor_tensor(grid_k[:], grid_high[:].bitcast(F32), masks[:, 1:2], grid[:], ALU.mult, ALU.add).then_inc(grid_done, 1)
            dve.sem_inc(rows_done, 2)
            with dve.Fori(0, HEADS // 2) as pair:
                for p in range(2):
                    h = pair * 2 + p
                    dve.wait_ge(high_done, h + 1)
                    dve.wait_ge(stored[p], pair * 16)
                    dve.scalar_tensor_tensor(rows[p][:], high[p][:].bitcast(F32), masks[:, 0:1], bank[p][0:REL, :], ALU.mult, ALU.add).then_inc(rows_done, 1)

        @block.gpsimd
        def _(pool):
            pool.wait_ge(loaded, 48)
            pool.sem_inc(made, 2)
            with pool.Fori(0, HEADS // 2) as pair:
                for p in range(2):
                    pool.wait_ge(made, pair * 2 + p + 1)
                    pool.tensor_copy(bias[p][:], biases[:, bass.ds(pair * 2 + p, 1), :]).then_inc(picked, 1)


def attnb_project(nc, name, X, K, w, q_dram, k_dram, V):
    SUB = CH // P
    G = 4
    NGROUP = NCH // G
    with ExitStack() as ctx:
        ph = Phase(nc, ctx, name + "p")
        wqk = [ph.sb("wq", [P, D]), ph.sb("wk", [P, D])]
        wv = ph.sb("wv", [P, D])
        vecs = ph.sb("vecs", [P, 4])
        bv = ph.sb("bv", [1, D])
        x1 = [ph.sb(f"x1{g}", [P, CH]) for g in range(G)]
        x2 = [ph.sb(f"x2{g}", [P, CH]) for g in range(G)]
        xg = [ph.sb(f"xg{g}", [P, CH]) for g in range(G)]
        whole = [ph.sb(f"whole{i}", [P, CH]) for i in range(2)]
        hi = [[ph.sb(f"hi{i}{p}", [P, CH], F32R) for i in range(2)] for p in range(G)]
        lo = [[ph.sb(f"lo{i}{p}", [P, CH], F32R) for i in range(2)] for p in range(G)]
        bank_n = [ph.ps(f"bank_n{g}") for g in range(G)]
        bank_qk = [ph.ps(f"bank_qk{i}") for i in range(2)]
        bank_v = [ph.ps(f"bank_v{i}") for i in range(2)]
        n1, n2 = Norm(ph, "n1", K, bank_n), Norm(ph, "n2", K, bank_n)
        s = {n: ph.sem(n) for n in ("loaded", "x1", "x2", "gained", "qk", "v", "v_copied", "whole", "hi", "lo", "stored0", "stored1", "stored2", "stored3")}
        stored = [s[f"stored{g}"] for g in range(G)]
        block = ctx.enter_context(nc.Block())
        scale = [float(np.float32(1) / np.sqrt(np.float32(HD))), 1.0]

        @block.sync
        def _(sp):
            for dst, src in ((wqk[0], "ab_wq"), (wqk[1], "ab_wk"), (wv, "ab_wv"), (vecs, "ab_vecs"), (bv, "ab_bv")):
                sp.dma_start(dst[:], w[src]).then_inc(s["loaded"], 16)
            with sp.Fori(0, NGROUP) as b:
                for g in range(G):
                    c = b * G + g
                    for i, dram in enumerate((q_dram, k_dram)):
                        sp.wait_ge(s["lo"], c * 2 + i + 1)
                        for part, src in enumerate((hi, lo)):
                            dst = dram.rearrange("(q b) r c t -> b r q c t", b=BATCH)[bass.ds(b * 2 + g // 2, 1), part, :, :, g % 2 * CH:(g % 2 + 1) * CH]
                            sp.dma_start(dst.rearrange("o q c t -> (o q) c t"), src[g][i][:].bitcast(F32)).then_inc(stored[g], 16)
            for g in range(G):
                sp.wait_ge(stored[g], 4 * 16 * NGROUP)

        @block.tensor
        def _(pe):
            pe.wait_ge(s["loaded"], 80)
            with pe.Fori(0, NGROUP) as b:
                for g in range(G):
                    pe.wait_ge(s["x2"], b * G)
                    n1.tensor_mean(pe, b, g, X[:, tok(b * G + g)])
                for g in range(G):
                    n1.tensor_var(pe, b, g)
                for g in range(G):
                    n1.tensor_spread(pe, b, g)
                for g in range(G):
                    pe.wait_ge(s["x1"], b * G + g + 1)
                    n2.tensor_mean(pe, b, g, x1[g][:])
                for g in range(G):
                    n2.tensor_var(pe, b, g)
                for g in range(G):
                    n2.tensor_spread(pe, b, g)
                for g in range(G):
                    c = b * G + g
                    pe.wait_ge(s["gained"], c + 1)
                    for i in range(2):
                        pe.wait_ge(s["whole"], c * 2 + i)
                        pe.matmul(bank_qk[i][:], wqk[i][:], xg[g][:], start=True, stop=True).then_inc(s["qk"], 1)
                    pe.wait_ge(s["v_copied"], c + 1)
                    for u in range(SUB):
                        out = bank_v[g % 2][:, u * D:(u + 1) * D]
                        pe.matmul(out, xg[g][:, u * P:(u + 1) * P], wv[:], start=True, stop=False)
                        m = pe.matmul(out, K["ones_row"][:], bv[:], start=False, stop=True)
                    m.then_inc(s["v"], 1)

        @block.scalar
        def _(act):
            act.wait_ge(s["loaded"], 80)
            act.sem_inc(s["v_copied"], 2)
            with act.Fori(0, NGROUP) as b:
                for n in (n1, n2):
                    for g in range(G):
                        n.scalar_square(act, b, g)
                for g in range(G):
                    c = b * G + g
                    act.wait_ge(s["v"], c + 1)
                    act.activation(V[:, bass.ds(c * SUB, SUB), :], bank_v[g % 2][:].rearrange("p (u d) -> p u d", u=SUB), ACT.Copy).then_inc(s["v_copied"], 1)

        @block.gpsimd
        def _(pool):
            with pool.Fori(0, NGROUP) as b:
                for n in (n1, n2):
                    for g in range(G):
                        n.pool_power(pool, b, g)

        @block.vector
        def _(dve):
            dve.wait_ge(s["loaded"], 80)
            with dve.Fori(0, NGROUP) as b:
                for g in range(G):
                    n1.vector_centre(dve, b, g, X[:, tok(b * G + g)])
                for g in range(G):
                    n1.vector_var(dve, b, g)
                for g in range(G):
                    n1.vector_diag(dve, b, g)
                for g in range(G):
                    n1.vector_wait_spread(dve, b, g)
                    dve.tensor_tensor(x1[g][:], n1.centred[g][:], bank_n[g][:], ALU.mult).then_inc(s["x1"], 1)
                for g in range(G):
                    dve.wait_ge(s["x1"], b * G + g + 1)
                    n2.vector_centre(dve, b, g, x1[g][:])
                for g in range(G):
                    n2.vector_var(dve, b, g)
                for g in range(G):
                    n2.vector_diag(dve, b, g)
                for g in range(G):
                    n2.vector_wait_spread(dve, b, g)
                    dve.scalar_tensor_tensor(x2[g][:], n2.centred[g][:], vecs[:, 2:3], bank_n[g][:], ALU.mult, ALU.mult).then_inc(s["x2"], 1)
                for g in range(G):
                    c = b * G + g
                    dve.wait_ge(s["x2"], c + 1)
                    dve.tensor_scalar(xg[g][:], x2[g][:], vecs[:, 3:4], None, ALU.add).then_inc(s["gained"], 1)
                for g in range(G):
                    c = b * G + g
                    dve.wait_ge(s["lo"], c * 2)
                    for i in range(2):
                        dve.wait_ge(s["qk"], c * 2 + i + 1)
                        dve.tensor_scalar(whole[i][:], bank_qk[i][:], vecs[:, i:i + 1], scale[i], ALU.add, ALU.mult).then_inc(s["whole"], 1)
                    for i in range(2):
                        dve.wait_ge(s["whole"], c * 2 + i + 1)
                        dve.wait_ge(stored[g], b * 4 * 16)
                        dve.tensor_copy(hi[g][i][:], whole[i][:]).then_inc(s["hi"], 1)
                    for i in range(2):
                        dve.wait_ge(s["hi"], c * 2 + i + 1)
                        dve.tensor_tensor(lo[g][i][:], whole[i][:], hi[g][i][:].bitcast(F32), ALU.subtract).then_inc(s["lo"], 1)


def attnb_scores(nc, name, K, w, q_dram, k_dram, rel_dram, grid_k, V, o_dram):
    HI, LO = 0, 1
    RING = 3
    with ExitStack() as ctx:
        ph = Phase(nc, ctx, name + "s")
        QA = [ph.sb(f"QA{p}", [ROWS_B, 4, SEQ], F32R) for p in range(2)]
        KA = [ph.sb(f"KA{p}", [ROWS_B, 4, SEQ], F32R) for p in range(2)]
        VA = [ph.sb(f"VA{p}", [P, NT, 4, 32]) for p in range(2)]
        PT = [ph.sb(f"PT{r}", [P, 4, CH]) for r in range(RING)]
        sums = ph.sb("sums", [P, SEQ])
        res = ph.sb("res", [64, SEQ])
        halves = ph.sb("halves", [P, 4, NT, 2])
        mx = ph.sb("mx", [P, 4, NT])
        nm = ph.sb("nm", [P, 4, 4, NT])
        nm_hi = ph.sb("nm_hi", [P, 4, NT], F32R)
        nmT = ph.sb("nmT", [2 * 4 * NT, P])
        ident_r = ph.sb("ident_r", [P, P], F32R)
        mask = ph.sb("mask", [P, P])
        mask_r = ph.sb("mask_r", [P, P], F32R)
        ones2 = ph.sb("ones2", [2, SEQ], F32R)
        sel = ph.sb("sel", [P, 64])
        bank_a = [ph.ps(f"bank_a{r}") for r in range(RING)]
        bank_b = [ph.ps(f"bank_b{r}") for r in range(RING)]
        bank_o = ph.ps("bank_o", (P, SEQ))
        s = {n: ph.sem(n) for n in ("const", "consts", "filled", "loaded00", "loaded01", "loaded10", "loaded11", "tile", "maxed", "nm_hi", "nm", "nmT", "nmT_copied",
                                    "maxima_loaded", "st", "exp", "zeroing", "zeroed", "pv", "cleared", "va", "sums", "sel", "res", "stored", "mx", "mx_clear")}
        loaded = [[s[f"loaded{p}{half}"] for half in range(2)] for p in range(2)]
        block = ctx.enter_context(nc.Block())

        groups = [(t, half) for t in range(NT) for half in range(t // 4, 2)]
        pieces = [(t, half, g) for t in range(NT) for half in range(t // 4 + 1) for g in range(4)]
        NGROUP, NPIECE = len(groups), len(pieces)
        NUNIT = NGROUP * 4
        FIRST_HALF = NT // 2 * 4
        A_UNITS = 38
        TRANSPOSE_AT, SELECT_AT = A_UNITS + 2, A_UNITS + 5
        slots = [list(enumerate(pieces))[NPIECE * u // A_UNITS:NPIECE * (u + 1) // A_UNITS] if u < A_UNITS else [] for u in range(NUNIT)]

        def load(sp, quad, b, i, half):
            p, n = b % 2, slice(half * CH, (half + 1) * CH)
            if b >= 2:
                sp.sem_inc(loaded[p][half], 16)
            else:
                sp.dma_start(QA[p][0:REL, :, n].bitcast(F32), rel_dram[bass.ds(quad, 1), :, :, n].rearrange("o g r t -> (o r) g t")).then_inc(loaded[p][half], 16)
            for tile, dram, parts in ((QA[p], q_dram, (0, 1, 0)), (KA[p], k_dram, (0, 0, 1))):
                for at, part in enumerate(parts):
                    rows = dram[bass.ds(i, 1), part, :, n].rearrange("o (g d) t -> (o d) g t", g=4)
                    sp.dma_start(tile[REL + at * HD:REL + (at + 1) * HD, :, n].bitcast(F32), rows).then_inc(loaded[p][half], 16)

        def loaded_count(pair):
            return (pair + 1) * 7 * 16

        @block.sync
        def _(sp):
            sp.dma_start(mask[:], w["causal"]).then_inc(s["const"], 16)
            sp.dma_start(sel[:], w["sel_b"]).then_inc(s["const"], 16)
            sp.wait_ge(s["consts"], 3)
            for p in range(2):
                for g in range(4):
                    sp.dma_start(KA[p][0:REL, g, :].bitcast(F32), grid_k[:].bitcast(F32)).then_inc(s["filled"], 16)
                    sp.dma_start(KA[p][ROWS_A:ROWS_B, g, :].bitcast(F32), ones2[:].bitcast(F32)).then_inc(s["filled"], 16)
            for b in range(2):
                for half in range(2):
                    load(sp, 0, b, b, half)

            def maxima(i, p):
                sp.wait_ge(s["nmT_copied"], i + 1)
                sp.dma_start(QA[p][ROWS_A:ROWS_B, :, :].rearrange("o g (t m) -> o (g t) m", t=NT).bitcast(F32),
                             nmT[:]).then_inc(s["maxima_loaded"], 16)

            def store(i):
                sp.wait_ge(s["res"], i + 1)
                sp.dma_start(o_dram[bass.ds(i, 1), :, :], res[:]).then_inc(s["stored"], 16)

            def step(quad, b, last):
                i = quad * BATCH + b
                if not (last and b >= 2):
                    sp.wait_ge(s["st"], i * NUNIT + NUNIT * 2 // 3)
                    load(sp, quad + (b + 2) // 4, (b + 2) % 4, i + 2, 0)
                if not (last and b == 3):
                    maxima(i + 1, (b + 1) % 2)
                store(i)
                if not (last and b >= 2):
                    sp.wait_ge(s["st"], (i + 1) * NUNIT)
                    load(sp, quad + (b + 2) // 4, (b + 2) % 4, i + 2, 1)

            maxima(0, 0)
            with sp.Fori(0, QUADS - 1) as quad:
                for b in range(BATCH):
                    step(quad, b, False)
            for b in range(BATCH):
                step(QUADS - 1, b, True)
            store(NSTEP)
            sp.wait_ge(s["stored"], 16 * (NSTEP + 1))

        @block.tensor
        def _(pe):
            pe.wait_ge(s["consts"], 3)
            pe.wait_ge(s["const"], 32)
            pe.wait_ge(s["filled"], 16 * 16)

            def pass_a(i, p, at, nt, half, g):
                pe.wait_ge(s["maxed"], i * (2 * NPIECE) + 2 * (at + 1))
                m0, m1 = half * CH, min((half + 1) * CH, (nt + 1) * P)
                diag = nt // 4 == half
                bank = bank_a[at % RING]
                m = pe.matmul(bank[:, 0:m1 - m0], QA[p][0:ROWS_A, g, nt * P:(nt + 1) * P], KA[p][0:ROWS_A, g, m0:m1], start=True, stop=not diag)
                if diag:
                    m = pe.matmul(bank[:, m1 - m0 - P:m1 - m0], ident_r[:], mask_r[:], start=False, stop=True)
                m.then_inc(s["tile"], 1)

            def transpose_maxima(i):
                pe.wait_ge(s["nm"], i + 1)
                pe.transpose(bank_a[0][:, 0:P], nm[:].rearrange("p a g t -> p (a g t)"), K["ident"][:]).then_inc(s["nmT"], 1)

            def pass_b(i, p, u, mt, half, g):
                pe.wait_ge(s["exp"], i * NUNIT + u + 1)
                n0, n1 = max(half * CH, mt * P), (half + 1) * CH
                pe.matmul(bank_b[u % RING][:, 0:n1 - n0], KA[p][:, g, mt * P:(mt + 1) * P], QA[p][:, g, n0:n1],
                          start=True, stop=True).then_inc(s["st"], 1)

            def values(i, p, q, mt, half):
                if q == 0:
                    pe.wait_ge(s["va"], i + 1)
                    pe.wait_ge(s["sums"], i + 1)
                if half == mt // 4:
                    pe.wait_ge(s["zeroed"], i * (2 * NT) + 2 * (mt + 1))
                else:
                    pe.wait_ge(s["exp"], i * NUNIT + (q + 1) * 4 + RING)
                n0, n1 = max(half * CH, mt * P), (half + 1) * CH
                for g in range(4):
                    m = pe.matmul(bank_o[32 * g:32 * g + 32, n0:n1], VA[p][:, mt, g, :], PT[q % RING][:, g, 0:n1 - n0],
                                  start=mt == 0, stop=mt == n1 // P - 1)
                m.then_inc(s["pv"], 1)

            def select(i):
                pe.wait_ge(s["sums"], i + 1)
                for half in range(2):
                    n = slice(half * CH, (half + 1) * CH)
                    m = pe.matmul(bank_a[1 + half][0:64, :], sel[:], sums[:, n], start=True, stop=True)
                m.then_inc(s["sel"], 1)

            def wait_piece(at, p, pair):
                if at == 0:
                    pe.wait_ge(loaded[p][0], loaded_count(pair))
                if at == FIRST_HALF:
                    pe.wait_ge(loaded[p][1], loaded_count(pair))

            def step(pair, p, last):
                i = pair * 2 + p
                more = not (last and p == 1)
                pe.wait_ge(s["maxima_loaded"], (i + 1) * 16)
                for u in range(NUNIT):
                    q, g = u // 4, u % 4
                    pass_b(i, p, u, *groups[q], g)
                    if more:
                        for at, piece in slots[u]:
                            wait_piece(at, 1 - p, pair + p)
                            pass_a(i + 1, 1 - p, at, *piece)
                    if u == TRANSPOSE_AT and more:
                        transpose_maxima(i + 1)
                    if u == SELECT_AT:
                        pe.wait_ge(s["maxed"], (i + 1 + more) * (2 * NPIECE) + 2 * RING)
                        select(i)
                    if q and g == 3:
                        values(i, p, q - 1, *groups[q - 1])
                values(i, p, NGROUP - 1, *groups[-1])
                pe.wait_ge(s["res"], i + 1)

            for at, piece in enumerate(pieces):
                wait_piece(at, 0, 0)
                pass_a(0, 0, at, *piece)
            transpose_maxima(0)
            with pe.Fori(0, NSTEP // 2 - 1) as pair:
                for p in range(2):
                    step(pair, p, False)
            for p in range(2):
                step(NSTEP // 2 - 1, p, True)
            select(NSTEP)

        @block.scalar
        def _(act):
            act.wait_ge(s["const"], 32)
            act.activation(ident_r[:], K["ident"][:], ACT.Copy).then_inc(s["consts"], 1)
            act.activation(mask_r[:], mask[:], ACT.Copy).then_inc(s["consts"], 1)
            act.activation(ones2[:], K["ones"][0:2, 0:1].to_broadcast([2, SEQ]), ACT.Copy).then_inc(s["consts"], 1)
            act.sem_inc(s["exp"], RING)

            def copy_sums(i):
                act.wait_ge(s["pv"], (i + 1) * NGROUP)
                act.activation(sums[:], bank_o[:], ACT.Copy).then_inc(s["sums"], 1)

            def step(pair, p):
                i = pair * 2 + p
                for u in range(NUNIT):
                    q, g = u // 4, u % 4
                    t, half = groups[q]
                    width = (half + 1) * CH - max(half * CH, t * P)
                    act.wait_ge(s["st"], i * NUNIT + u + 1)
                    if g == 0:
                        act.wait_ge(s["pv"], (i + 1) * NGROUP + q + 1 - RING)
                    act.activation(PT[q % RING][:, g, 0:width], bank_b[u % RING][:, 0:width], ACT.Exp).then_inc(s["exp"], 1)
                    if u == 3:
                        copy_sums(i)

            with act.Fori(0, NSTEP // 2) as pair:
                for p in range(2):
                    step(pair, p)
            copy_sums(NSTEP)

        @block.vector
        def _(dve):
            def reduce_piece(i, at, nt, half, g):
                dve.wait_ge(s["tile"], i * NPIECE + at + 1)
                width = min((half + 1) * CH, (nt + 1) * P) - half * CH
                dve.tensor_reduce(halves[:, g, nt, half:half + 1], bank_a[at % RING][:, 0:width], AX.X, ALU.max).then_inc(s["maxed"], 2)

            def negate(i):
                dve.wait_ge(s["maxed"], (i + 1) * (2 * NPIECE) + 2 * RING)
                dve.tensor_reduce(mx[:], halves[:], AX.X, ALU.max).then_inc(s["mx"], 1)
                dve.wait_ge(s["mx"], i + 1)
                dve.wait_ge(s["nmT"], i)
                dve.tensor_scalar(nm_hi[:], mx[:], -1.0, None, ALU.mult).then_inc(s["nm_hi"], 1)
                dve.wait_ge(s["nm_hi"], i + 1)
                dve.tensor_copy(nm[:, HI], nm_hi[:].bitcast(F32))
                dve.scalar_tensor_tensor(nm[:, LO], mx[:], -1.0, nm_hi[:].bitcast(F32), ALU.mult, ALU.subtract).then_inc(s["nm"], 1)
                dve.wait_ge(s["nmT"], i + 1)
                dve.wait_ge(s["maxima_loaded"], i * 16)
                dve.tensor_copy(nmT[:], bank_a[0][0:2 * 4 * NT, 0:P]).then_inc(s["nmT_copied"], 1)

            def unload(i):
                dve.wait_ge(s["sel"], i + 1)
                dve.wait_ge(s["stored"], i * 16)
                for half in range(2):
                    m = dve.tensor_copy(res[:, half * CH:(half + 1) * CH], bank_a[1 + half][0:64, :])
                m.then_inc(s["res"], 1)

            def step(pair, p, last):
                i = pair * 2 + p
                more = not (last and p == 1)
                if more:
                    for at, piece in enumerate(pieces):
                        reduce_piece(i + 1, at, *piece)
                    negate(i + 1)
                unload(i)

            dve.memset(bank_o[:], 1.0).then_inc(s["pv"], NGROUP)
            dve.sem_inc(s["maxed"], RING * 2)
            dve.memset(nm[:], 0.0).then_inc(s["mx_clear"], 1)
            dve.memset(halves[:], -3e38).then_inc(s["mx_clear"], 1)
            dve.wait_ge(s["mx_clear"], 2)
            for at, piece in enumerate(pieces):
                reduce_piece(0, at, *piece)
            negate(0)
            with dve.Fori(0, NSTEP // 2 - 1) as pair:
                for p in range(2):
                    step(pair, p, False)
            for p in range(2):
                step(NSTEP // 2 - 1, p, True)
            unload(NSTEP)

        @block.gpsimd
        def _(pool):
            for p in range(2):
                pool.memset(VA[p][:], 0.0).then_inc(s["cleared"], 1)
            pool.wait_ge(s["cleared"], 2)
            for p in range(2):
                pool.memset(VA[p][:, :, :, HD:HD + 1], 1.0)
            def step(quad, b):
                i = quad * BATCH + b
                pool.wait_ge(s["pv"], i * NGROUP)
                for g in range(4):
                    m = pool.tensor_copy(VA[b % 2][:, :, g, 0:HD], V[:, b * NT:(b + 1) * NT, bass.ds(quad * 32 + g * HD, HD)])
                m.then_inc(s["va"], 1)
                for q, (t, half) in enumerate(groups):
                    if half == t // 4:
                        for g in (0, 2):
                            pool.wait_ge(s["exp"], i * NUNIT + q * 4 + g + 2 + RING)
                            square = PT[q % RING][:, g:g + 2, 0:P]
                            pool.sem_inc(s["zeroing"], 1)
                            pool.affine_select(out=square, in_=square, compare_op=ALU.is_ge, fill=0.0, base=0, channel_multiplier=-1,
                                               pattern=[[0, 2], [1, P]]).then_inc(s["zeroed"], 1)

            with pool.Fori(0, QUADS) as quad:
                for b in range(BATCH):
                    step(quad, b)


def attnb_out(nc, name, X, w, o_dram, inverted=False, experts=None):
    with ExitStack() as ctx:
        ph = Phase(nc, ctx, name + "o")
        wo = ph.sb("wo", [P, D])
        bo = ph.sb("bo", [P, 1])
        den = [ph.sb(f"den{b}", [P, SEQ]) for b in range(BATCH)]
        num = [ph.sb(f"num{b}", [P, SEQ]) for b in range(BATCH)]
        inv = [ph.sb(f"inv{i}", [P, CH]) for i in range(2)]
        heads = [ph.sb(f"heads{i}", [P, CH]) for i in range(2)]
        bank = [ph.ps(f"bank{i}") for i in range(2)]
        loaded, inv_done, divided, made, added = (ph.sem(n) for n in ("loaded", "inv_done", "divided", "made", "added"))
        arrived = [ph.sem(f"arrived{b}") for b in range(BATCH)]
        block = ctx.enter_context(nc.Block())

        @block.sync
        def _(sp):
            sp.dma_start(wo[:], w[name + "_wo"]).then_inc(loaded, 16)
            sp.dma_start(bo[:], w[name + "_bo"]).then_inc(loaded, 16)
            for b in range(BATCH):
                for quad in range(QUADS):
                    rows = slice(32 * quad, 32 * quad + 32)
                    sp.dma_start(den[b][rows, :], o_dram[quad * BATCH + b + 1, 0:32, :]).then_inc(arrived[b], 16)
                    sp.dma_start(num[b][rows, :], o_dram[quad * BATCH + b + 1, 32:64, :]).then_inc(arrived[b], 16)
            if experts:
                load_experts(sp, w, *experts)

        @block.tensor
        def _(pe):
            pe.wait_ge(loaded, 32)
            for c in range(NCH):
                pe.wait_ge(divided, c + 1)
                if c >= 2:
                    pe.wait_ge(added, c - 1)
                pe.matmul(bank[c % 2][:], wo[:], heads[c % 2][:], start=True, stop=True).then_inc(made, 1)

        @block.vector
        def _(dve):
            dve.wait_ge(loaded, 32)
            for c in range(NCH + 1):
                if c < NCH:
                    n = slice((c % 2) * CH, (c % 2 + 1) * CH)
                    dve.wait_ge(arrived[c // 2], 8 * 16)
                    factor = den[c // 2][:, n]
                    if not inverted:
                        factor = inv[c % 2][:]
                        dve.reciprocal(factor, den[c // 2][:, n]).then_inc(inv_done, 1)
                        dve.wait_ge(inv_done, c + 1)
                    if c >= 2:
                        dve.wait_ge(made, c - 1)
                    dve.tensor_tensor(heads[c % 2][:], num[c // 2][:, n], factor, ALU.mult).then_inc(divided, 1)
                if c:
                    dve.wait_ge(made, c)
                    dve.scalar_tensor_tensor(X[:, tok(c - 1)], bank[(c - 1) % 2][:], bo[:, 0:1], X[:, tok(c - 1)], ALU.add, ALU.add).then_inc(added, 1)


def attna_phase(nc, name, X, K, w):
    q_dram = nc.dram_tensor(f"{name}_q", (NSTEP, 2, 4 * HD, SEQ), F32, kind="Internal").ap()
    k_dram = nc.dram_tensor(f"{name}_k", (NSTEP, 2, 4 * HD, SEQ), F32, kind="Internal").ap()
    o_dram = nc.dram_tensor(f"{name}_o", (NSTEP + 1, 64, SEQ), F32, kind="Internal").ap()
    with ExitStack() as ctx:
        keep = Phase(nc, ctx, name)
        V = keep.sb("V", [P, BATCH * NT, D])
        attna_project(nc, name, X, K, w, q_dram, k_dram, V)
        attna_scores(nc, name, w, q_dram, k_dram, V, o_dram)
        attnb_out(nc, name, X, w, o_dram, inverted=True)


def attna_project(nc, name, X, K, w, q_dram, k_dram, V):
    SUB = CH // P
    G = 2
    with ExitStack() as ctx:
        ph = Phase(nc, ctx, name + "p")
        wq = ph.sb("wq", [P, 4, D])
        wv = ph.sb("wv", [P, D])
        turn = ph.sb("turn", [P, 2, SEQ])
        head_ones = ph.sb("head_ones", [P, P])
        tiny = ph.sb("tiny", [P, 1])
        xn = [ph.sb(f"xn{g}", [P, CH]) for g in range(G)]
        tc = [ph.sb(f"tc{i}", [P, CH]) for i in range(2)]
        ts_ = [ph.sb(f"ts{i}", [P, CH]) for i in range(2)]
        turned = [ph.sb(f"turned{i}", [P, CH]) for i in range(2)]
        sq = [ph.sb(f"sq{i}", [P, CH]) for i in range(2)]
        length = [ph.sb(f"length{i}", [P, CH]) for i in range(2)]
        inv = [ph.sb(f"inv{i}", [P, CH]) for i in range(2)]
        whole = [ph.sb(f"whole{i}", [P, CH]) for i in range(2)]
        hi = [[ph.sb(f"hi{i}{p}", [P, CH], F32R) for i in range(2)] for p in range(G)]
        lo = [[ph.sb(f"lo{i}{p}", [P, CH], F32R) for i in range(2)] for p in range(G)]
        bank_n = [ph.ps(f"bank_n{g}") for g in range(G)]
        bank_q = [ph.ps(f"bank_q{i}") for i in range(4)]
        bank_ss = ph.ps("bank_ss")
        bank_v = ph.ps("bank_v")
        n1 = Norm(ph, "n1", K, bank_n)
        s = {n: ph.sem(n) for n in ("loaded", "tiny", "xn", "qk", "products", "turned", "sq", "ss", "length", "inv", "v", "v_copied", "whole", "hi", "lo", "stored0", "stored1")}
        stored = [s["stored0"], s["stored1"]]
        block = ctx.enter_context(nc.Block())
        scale = [float(1 / np.sqrt(HD)), 1.0]

        @block.sync
        def _(sp):
            sp.dma_start(wq[:], w["aa_wq"].rearrange("p (a d) -> p a d", a=4)).then_inc(s["loaded"], 16)
            sp.dma_start(wv[:], w["aa_wv"]).then_inc(s["loaded"], 16)
            sp.dma_start(turn[:], w["turn"].rearrange("p (a t) -> p a t", a=2)).then_inc(s["loaded"], 16)
            sp.dma_start(head_ones[:], w["head_ones"]).then_inc(s["loaded"], 16)
            with sp.Fori(0, BATCH) as b:
                for g in range(G):
                    c = b * G + g
                    for i, dram in enumerate((q_dram, k_dram)):
                        sp.wait_ge(s["lo"], c * 2 + i + 1)
                        for part, src in enumerate((hi, lo)):
                            dst = dram.rearrange("(q b) r c t -> b r q c t", b=BATCH)[bass.ds(b, 1), part, :, :, g * CH:(g + 1) * CH]
                            sp.dma_start(dst.rearrange("o q c t -> (o q) c t"), src[g][i][:].bitcast(F32)).then_inc(stored[g], 16)
            for g in range(G):
                sp.wait_ge(stored[g], 4 * 16 * BATCH)

        @block.tensor
        def _(pe):
            pe.wait_ge(s["loaded"], 64)
            for g in range(G):
                n1.tensor_mean(pe, 0, g, X[:, tok(g)])
            for g in range(G):
                n1.tensor_var(pe, 0, g)
            for g in range(G):
                n1.tensor_spread(pe, 0, g)
            with pe.Fori(0, BATCH) as b:
                for g in range(G):
                    c = b * G + g
                    pe.wait_ge(s["xn"], c + 1)
                    pe.wait_ge(s["products"], c * 4)
                    for i in range(4):
                        pe.matmul(bank_q[i][:], wq[:, i, :], xn[g][:], start=True, stop=True).then_inc(s["qk"], 1)
                    if g == 0:
                        pe.wait_ge(s["xn"], b * G + G)
                        for k in range(G):
                            n1.tensor_mean(pe, b + 1, k, X[:, tok(b * G + G + k)])
                    pe.wait_ge(s["v_copied"], c)
                    for u in range(SUB):
                        m = pe.matmul(bank_v[:, u * D:(u + 1) * D], xn[g][:, u * P:(u + 1) * P], wv[:], start=True, stop=True)
                    m.then_inc(s["v"], 1)
                    if g == 1:
                        for k in range(G):
                            n1.tensor_spread(pe, b + 1, k)
                    for i in range(2):
                        pe.wait_ge(s["sq"], c * 2 + i + 1)
                        pe.wait_ge(s["length"], c * 2 + i)
                        pe.matmul(bank_ss[:], head_ones[:], sq[i][:], start=True, stop=True).then_inc(s["ss"], 1)
                    if g == 0:
                        for k in range(G):
                            n1.tensor_var(pe, b + 1, k)

        @block.scalar
        def _(act):
            act.wait_ge(s["tiny"], 1)
            for g in range(G):
                n1.scalar_square(act, 0, g)
            with act.Fori(0, BATCH) as b:
                for g in range(G):
                    c = b * G + g
                    act.wait_ge(s["v"], c + 1)
                    act.activation(V[:, bass.ds(c * SUB, SUB), :], bank_v[:].rearrange("p (u d) -> p u d", u=SUB), ACT.Copy).then_inc(s["v_copied"], 1)
                    for i in range(2):
                        act.wait_ge(s["turned"], c * 2 + i + 1)
                        act.activation(sq[i][:], turned[i][:], ACT.Square).then_inc(s["sq"], 1)
                    for i in range(2):
                        act.wait_ge(s["ss"], c * 2 + i + 1)
                        act.wait_ge(s["inv"], c * 2)
                        act.activation(length[i][:], bank_ss[:], ACT.Sqrt, bias=tiny[:, 0:1]).then_inc(s["length"], 1)
                    if g == 0:
                        for k in range(G):
                            n1.scalar_square(act, b + 1, k)
                    for i in range(2):
                        act.wait_ge(s["whole"], c * 2 + i + 1)
                        act.wait_ge(stored[g], b * 4 * 16)
                        act.activation(hi[g][i][:], whole[i][:], ACT.Copy).then_inc(s["hi"], 1)

        @block.gpsimd
        def _(pool):
            pool.memset(tiny[:], 1e-6).then_inc(s["tiny"], 1)
            for g in range(G):
                n1.pool_power(pool, 0, g)
            with pool.Fori(0, BATCH) as b:
                for g in range(G):
                    n1.pool_power(pool, b + 1, g)
                for g in range(G):
                    c = b * G + g
                    for i in range(2):
                        pool.wait_ge(s["hi"], c * 2 + i + 1)
                        pool.tensor_tensor(lo[g][i][:], whole[i][:], hi[g][i][:].bitcast(F32), ALU.subtract).then_inc(s["lo"], 1)

        @block.vector
        def _(dve):
            dve.wait_ge(s["loaded"], 64)

            def norm_end(b):
                for g in range(G):
                    n1.vector_wait_spread(dve, b, g)
                    dve.tensor_tensor(xn[g][:], n1.centred[g][:], bank_n[g][:], ALU.mult).then_inc(s["xn"], 1)

            for g in range(G):
                n1.vector_centre(dve, 0, g, X[:, tok(g)])
            for g in range(G):
                n1.vector_var(dve, 0, g)
            for g in range(G):
                n1.vector_diag(dve, 0, g)
            norm_end(0)
            with dve.Fori(0, BATCH) as b:
                for g in range(G):
                    c = b * G + g
                    pos = slice(g * CH, (g + 1) * CH)
                    for i in range(2):
                        dve.wait_ge(s["qk"], c * 4 + 2 * i + 2)
                        dve.tensor_tensor(tc[i][:], bank_q[2 * i][:], turn[:, 0, pos], ALU.mult).then_inc(s["products"], 1)
                        dve.tensor_tensor(ts_[i][:], bank_q[2 * i + 1][:], turn[:, 1, pos], ALU.mult).then_inc(s["products"], 1)
                    for i in range(2):
                        dve.wait_ge(s["products"], c * 4 + 2 * i + 2)
                        dve.tensor_tensor(turned[i][:], tc[i][:], ts_[i][:], ALU.add).then_inc(s["turned"], 1)
                    if g == 0:
                        for k in range(G):
                            n1.vector_centre(dve, b + 1, k, X[:, tok(b * G + G + k)])
                    else:
                        dve.wait_ge(s["v"], c + 1)
                        norm_end(b + 1)
                    for i in range(2):
                        dve.wait_ge(s["length"], c * 2 + i + 1)
                        dve.reciprocal(inv[i][:], length[i][:]).then_inc(s["inv"], 1)
                    if g == 0:
                        for k in range(G):
                            n1.vector_var(dve, b + 1, k)
                    for i in range(2):
                        dve.wait_ge(s["inv"], c * 2 + i + 1)
                        dve.wait_ge(s["lo"], c * 2)
                        dve.scalar_tensor_tensor(whole[i][:], turned[i][:], scale[i], inv[i][:], ALU.mult, ALU.mult).then_inc(s["whole"], 1)
                    if g == 0:
                        for k in range(G):
                            n1.vector_diag(dve, b + 1, k)


def attna_scores(nc, name, w, q_dram, k_dram, V, o_dram):
    UNITS = NT * 2
    RING = 4
    PAIRS = 3
    SELECT = 12
    pairs = [(u, pr) for u in range(UNITS) for pr in range(2)]
    pairs.insert(SELECT, None)
    assert len(pairs) % PAIRS == 0
    bank_of = {pair: at % PAIRS for at, pair in enumerate(pairs)}
    with ExitStack() as ctx:
        ph = Phase(nc, ctx, name + "s")
        QA = [ph.sb(f"QA{p}", [P, SEQ], F32R) for p in range(2)]
        KA = [ph.sb(f"KA{p}", [P, SEQ], F32R) for p in range(2)]
        VA = [ph.sb(f"VA{p}", [P, NT, 4, 32]) for p in range(2)]
        PT = [ph.sb(f"PT{r}", [P, 4, CH]) for r in range(RING)]
        sums = ph.sb("sums", [P, SEQ])
        res = ph.sb("res", [64, SEQ])
        sel = ph.sb("sel", [P, 64])
        ST = [ph.ps(f"ST{i}", (P, 2, CH)) for i in range(PAIRS)]
        O = ph.ps("O", (P, SEQ))
        s = {n: ph.sem(n) for n in ("const", "loaded0", "loaded1", "st", "exp", "pv", "cleared", "va", "sums", "sel", "taken", "res", "stored")}
        loaded = [s["loaded0"], s["loaded1"]]
        block = ctx.enter_context(nc.Block())

        LOADS = 20

        @block.sync
        def _(sp):
            sp.dma_start(sel[:], w["sel_b"]).then_inc(s["const"], 16)

            def load(i, p):
                for tile, dram, order in ((QA[p], q_dram, ((0, 0, 2), (16, 0, 2))), (KA[p], k_dram, ((0, 0, 1), (8, 0, 2), (24, 1, 2)))):
                    for at, r0, r1 in order:
                        for g in range(4):
                            rows = dram[bass.ds(i, 1), r0:r1, g * HD:(g + 1) * HD, :].rearrange("o r d t -> (o r) d t")
                            sp.dma_start(tile[32 * g + at:32 * g + at + (r1 - r0) * HD, :].bitcast(F32), rows).then_inc(loaded[p], 16)

            def store(i):
                sp.wait_ge(s["res"], i + 1)
                sp.dma_start(o_dram[bass.ds(i + 1, 1), :, :], res[:]).then_inc(s["stored"], 16)

            load(0, 0)
            load(1, 1)
            with sp.Fori(0, NSTEP // 2 - 1) as pair:
                for p in range(2):
                    i = pair * 2 + p
                    sp.wait_ge(s["pv"], (i + 1) * UNITS)
                    load(i + 2, p)
                    store(i)
            store(NSTEP - 2)
            store(NSTEP - 1)
            sp.wait_ge(s["stored"], 16 * NSTEP)

        @block.tensor
        def _(pe):
            pe.wait_ge(s["const"], 16)

            def wait_banks(i, at):
                last = at - PAIRS
                if last == SELECT:
                    after(pe, s["taken"], i)
                else:
                    after(pe, s["exp"], i * 2 * UNITS + last + (last < SELECT))

            def scores(i, p, u):
                mt, half = u // 2, u % 2
                for pr in range(2):
                    wait_banks(i, pairs.index((u, pr)))
                    for g in (2 * pr, 2 * pr + 1):
                        rows = slice(32 * g, 32 * g + 32)
                        m = pe.matmul(ST[bank_of[u, pr]][:, g % 2, :], KA[p][rows, mt * P:(mt + 1) * P], QA[p][rows, half * CH:(half + 1) * CH],
                                      start=True, stop=True)
                    m.then_inc(s["st"], 1)

            def values(i, p, u):
                mt, half = u // 2, u % 2
                if u == 0:
                    pe.wait_ge(s["va"], i + 1)
                    after(pe, s["sums"], i)
                pe.wait_ge(s["exp"], i * 2 * UNITS + 2 * u + 2)
                for g in range(4):
                    m = pe.matmul(O[32 * g:32 * g + 32, half * CH:(half + 1) * CH], VA[p][:, mt, g, :], PT[u % RING][:, g, :],
                                  start=mt == 0, stop=mt == NT - 1)
                m.then_inc(s["pv"], 1)

            def select(i):
                pe.wait_ge(s["sums"], i + 1)
                for half in range(2):
                    n = slice(half * CH, (half + 1) * CH)
                    m = pe.matmul(ST[bank_of[None]][0:64, half, :], sel[:], sums[:, n], start=True, stop=True)
                m.then_inc(s["sel"], 1)

            def step(pair, p, first):
                i = pair * 2 + p
                begin = first and p == 0
                pe.wait_ge(loaded[p], (pair + 1) * LOADS * 16)
                for u in range(UNITS):
                    scores(i, p, u)
                    if u >= 2:
                        values(i, p, u - 2)
                    elif not begin:
                        values(i - 1, 1 - p, UNITS - 2 + u)
                    if 2 * (u + 1) == SELECT and not begin:
                        wait_banks(i, SELECT)
                        select(i - 1)

            for p in range(2):
                step(0, p, True)
            with pe.Fori(1, NSTEP // 2) as pair:
                for p in range(2):
                    step(pair, p, False)
            for u in (UNITS - 2, UNITS - 1):
                values(NSTEP - 1, 1, u)
            wait_banks(NSTEP, 0)
            select(NSTEP - 1)

        @block.scalar
        def _(act):
            def exponentials(i, u):
                for pr in range(2):
                    act.wait_ge(s["st"], i * 2 * UNITS + 2 * u + pr + 1)
                    if pr == 0 and not (isinstance(i, int) and i == 0 and u < RING):
                        act.wait_ge(s["pv"], i * UNITS + u - RING + 1)
                    act.activation(PT[u % RING][:, 2 * pr:2 * pr + 2, :], ST[bank_of[u, pr]][:], ACT.Exp).then_inc(s["exp"], 1)

            for u in range(UNITS):
                exponentials(0, u)
            with act.Fori(1, NSTEP) as i:
                for u in range(UNITS):
                    exponentials(i, u)

        @block.vector
        def _(dve):
            def collect(i, first):
                dve.wait_ge(s["pv"], (i + 1) * UNITS)
                if not first:
                    dve.wait_ge(s["sel"], i)
                dve.tensor_copy(sums[:], O[:]).then_inc(s["sums"], 1)
                dve.wait_ge(s["sel"], i + 1)
                if not first:
                    dve.wait_ge(s["stored"], i * 16)
                dve.tensor_copy(res[:].rearrange("p (h t) -> p h t", h=2), ST[bank_of[None]][0:64, :, :]).then_inc(s["taken"], 1)
                dve.wait_ge(s["taken"], i + 1)
                dve.reciprocal(res[0:32, :], res[0:32, :]).then_inc(s["res"], 1)

            collect(0, True)
            with dve.Fori(1, NSTEP) as i:
                collect(i, False)

        @block.gpsimd
        def _(pool):
            for p in range(2):
                pool.memset(VA[p][:], 0.0).then_inc(s["cleared"], 1)
            pool.wait_ge(s["cleared"], 2)
            for p in range(2):
                pool.memset(VA[p][:, :, :, HD:HD + 1], 1.0)

            def place(quad, b, i, first):
                if not first:
                    pool.wait_ge(s["pv"], (i - 1) * UNITS)
                for g in range(4):
                    m = pool.tensor_copy(VA[b % 2][:, :, g, 0:HD], V[:, b * NT:(b + 1) * NT, bass.ds(quad * 32 + g * HD, HD)])
                m.then_inc(s["va"], 1)

            for b in range(BATCH):
                place(0, b, b, b < 2)
            with pool.Fori(1, QUADS) as quad:
                for b in range(BATCH):
                    place(quad, b, quad * BATCH + b, False)


def tern_phase(nc, name, X, K, w):
    G = 2
    NGROUP = NCH // G
    COUNT = FF * D
    with ExitStack() as ctx:
        ph = Phase(nc, ctx, name)
        raw = [ph.sb(f"raw{i}", [P, FF]) for i in range(2)]
        wt = [ph.sb(f"wt{i}", [P, FF], F32R) for i in range(2)]
        above = [ph.sb(f"above{i}", [P, FF]) for i in range(2)]
        below = [ph.sb(f"below{i}", [P, FF]) for i in range(2)]
        total = ph.sb("total", [P, 2])
        scale = ph.sb("scale", [P, 2])
        limit = ph.sb("limit", [P, 2, 2])
        b1 = ph.sb("b1", [P, NF])
        b2 = ph.sb("b2", [P, 1])
        xn = [ph.sb(f"xn{g}", [P, CH]) for g in range(G)]
        x_hi = [[ph.sb(f"x_hi{p}{g}", [P, CH], F32R) for g in range(G)] for p in range(2)]
        x_lo = [[ph.sb(f"x_lo{p}{g}", [P, CH], F32R) for g in range(G)] for p in range(2)]
        h = [ph.sb(f"h{g}", [P, NF, CH]) for g in range(G)]
        h_hi = [ph.sb(f"h_hi{g}", [P, NF, CH], F32R) for g in range(G)]
        h_lo = [ph.sb(f"h_lo{g}", [P, NF, CH], F32R) for g in range(G)]
        bank_n = [ph.ps(f"bank_n{g}") for g in range(G)]
        bank_h = [ph.ps(f"bank_h{f}") for f in range(NF)]
        bank_o = [ph.ps(f"bank_o{g}") for g in range(G)]
        n1 = Norm(ph, "n1", K, bank_n)
        s = {n: ph.sem(n) for n in ("loaded", "total", "total_all", "scale", "limit", "compared", "ternary",
                                    "xn", "x_hi", "x_lo", "up", "h_hi", "h_lo", "h_lo_pool", "down", "added")}
        block = ctx.enter_context(nc.Block())

        @block.sync
        def _(sp):
            for dst, src in ((raw[0], "tern_w1"), (raw[1], "tern_w2"), (b1, "tern_b1"), (b2, "tern_b2")):
                sp.dma_start(dst[:], w[src]).then_inc(s["loaded"], 16)

        def norm_tensor(pe, group, step, g):
            if step == 0:
                pe.wait_ge(s["xn"], group * G)
                n1.tensor_mean(pe, group, g, X[:, tok(group * G + g)])
            if step == 1:
                n1.tensor_var(pe, group, g)
            if step == 2:
                n1.tensor_spread(pe, group, g)

        def norm_vector(dve, group, par, step, g):
            c = group * G + g
            if step == 0:
                n1.vector_centre(dve, group, g, X[:, tok(c)])
            if step == 1:
                n1.vector_var(dve, group, g)
            if step == 2:
                n1.vector_diag(dve, group, g)
            if step == 3:
                n1.vector_wait_spread(dve, group, g)
                dve.tensor_tensor(xn[g][:], n1.centred[g][:], bank_n[g][:], ALU.mult).then_inc(s["xn"], 1)
            if step == 4:
                dve.wait_ge(s["xn"], c + 1)
                dve.tensor_copy(x_hi[par][g][:], xn[g][:]).then_inc(s["x_hi"], 1)
            if step == 5:
                dve.wait_ge(s["x_hi"], c + 1)
                dve.tensor_tensor(x_lo[par][g][:], xn[g][:], x_hi[par][g][:].bitcast(F32), ALU.subtract).then_inc(s["x_lo"], 1)

        @block.tensor
        def _(pe):
            for g in range(G):
                norm_tensor(pe, 0, 0, g)
            pe.wait_ge(s["total"], 1)
            pe.matmul(bank_h[0][:, 0:2], K["ones"][:], total[:], start=True, stop=True).then_inc(s["total_all"], 1)
            for step in range(1, 3):
                for g in range(G):
                    norm_tensor(pe, 0, step, g)
            pe.wait_ge(s["ternary"], 2)

            def group(j, par):
                for k in range(G):
                    norm_tensor(pe, j + 1, 0, k)
                for g in range(G):
                    c = j * G + g
                    pe.wait_ge(s["x_lo"], c + 1)
                    for f in range(NF):
                        pe.wait_ge(s["h_hi"], c * NF + f + 1)
                        wf = wt[0][:, f * P:(f + 1) * P]
                        pe.matmul(bank_h[f][:], wf, x_hi[par][g][:], start=True, stop=False)
                        pe.matmul(bank_h[f][:], wf, x_lo[par][g][:], start=False, stop=True).then_inc(s["up"], 1)
                    for k in range(G):
                        norm_tensor(pe, j + 1, g + 1, k)
                for g in range(G):
                    c = j * G + g
                    pe.wait_ge(s["added"], c - 1 + 1)
                    for f in range(NF):
                        pe.wait_ge(*((s["h_lo"], c * 2 + f + 1) if f < 2 else (s["h_lo_pool"], c * 2 + f - 1)))
                        wf = wt[1][:, f * D:(f + 1) * D]
                        pe.matmul(bank_o[g][:], wf, h_hi[g][:, f, :], start=f == 0, stop=False)
                        m = pe.matmul(bank_o[g][:], wf, h_lo[g][:, f, :], start=False, stop=f == NF - 1)
                    m.then_inc(s["down"], 1)

            with pe.Fori(0, NGROUP // 2) as jj:
                for par in range(2):
                    group(jj * 2 + par, par)

        @block.scalar
        def _(act):
            for g in range(G):
                n1.scalar_square(act, 0, g)
            act.wait_ge(s["loaded"], 64)
            act.sem_inc(s["h_hi"], NF)

            def group(j, par):
                for g in range(G):
                    c = j * G + g
                    for f in range(NF):
                        act.wait_ge(s["up"], c * NF + f + 1)
                        if f == 0:
                            act.wait_ge(s["down"], j * G - G + g + 1 + G - 1)
                        act.activation(h[g][:, f, :], bank_h[f][:], ACT.Gelu, bias=b1[:, f:f + 1])
                        act.activation(h_hi[g][:, f, :], bank_h[f][:], ACT.Gelu, bias=b1[:, f:f + 1]).then_inc(s["h_hi"], 1)
                        if g == 0 and f < G:
                            n1.scalar_square(act, j + 1, f)

            with act.Fori(0, NGROUP // 2) as jj:
                for par in range(2):
                    group(jj * 2 + par, par)

        @block.vector
        def _(dve):
            for g in range(G):
                norm_vector(dve, 0, 0, 0, g)
            dve.wait_ge(s["loaded"], 64)
            for i in range(2):
                m = dve.tensor_reduce(total[:, i:i + 1], raw[i][:], AX.X, ALU.add, apply_absolute_value=True)
            m.then_inc(s["total"], 1)
            for g in range(G):
                norm_vector(dve, 0, 0, 1, g)
            dve.wait_ge(s["total_all"], 1)
            dve.tensor_scalar(scale[:], bank_h[0][:, 0:2], 1.0 / COUNT, 1e-8, ALU.mult, ALU.max).then_inc(s["scale"], 1)
            dve.wait_ge(s["scale"], 1)
            dve.tensor_scalar(limit[:, 0, :], scale[:], 0.5, None, ALU.mult).then_inc(s["limit"], 1)
            dve.tensor_scalar(limit[:, 1, :], scale[:], -0.5, None, ALU.mult).then_inc(s["limit"], 1)
            dve.wait_ge(s["limit"], 2)
            for i in range(2):
                dve.tensor_scalar(above[i][:], raw[i][:], limit[:, 0, i:i + 1], None, ALU.is_gt)
                dve.tensor_scalar(below[i][:], raw[i][:], limit[:, 1, i:i + 1], None, ALU.is_lt).then_inc(s["compared"], 1)
            for i in range(2):
                dve.wait_ge(s["compared"], i + 1)
                dve.tensor_tensor(wt[i][:], above[i][:], below[i][:], ALU.subtract).then_inc(s["ternary"], 1)
            for step in range(2, 6):
                for g in range(G):
                    norm_vector(dve, 0, 0, step, g)
            dve.sem_inc(s["added"], 1)

            def group(j, par):
                for k in range(G):
                    norm_vector(dve, j + 1, 1 - par, 0, k)
                for g in range(G):
                    c = j * G + g
                    for f in range(2):
                        dve.wait_ge(s["h_hi"], c * NF + f + 1 + NF)
                        dve.tensor_tensor(h_lo[g][:, f, :], h[g][:, f, :], h_hi[g][:, f, :].bitcast(F32), ALU.subtract).then_inc(s["h_lo"], 1)
                        if g == 0:
                            for k in range(G):
                                norm_vector(dve, j + 1, 1 - par, 1 + f, k)
                for step in range(3, 6):
                    for k in range(G):
                        norm_vector(dve, j + 1, 1 - par, step, k)
                for g in range(G):
                    c = j * G + g
                    dve.wait_ge(s["down"], c + 1 + G - 1)
                    dve.scalar_tensor_tensor(X[:, tok(c)], bank_o[g][:], b2[:, 0:1], X[:, tok(c)], ALU.add, ALU.add).then_inc(s["added"], 1)

            with dve.Fori(0, NGROUP // 2) as jj:
                for par in range(2):
                    group(jj * 2 + par, par)

        @block.gpsimd
        def _(pool):
            pool.sem_inc(s["down"], G - 1)
            for g in range(G):
                n1.pool_power(pool, 0, g)

            def group(j, par):
                for g in range(G):
                    n1.pool_power(pool, j + 1, g)
                for g in range(G):
                    c = j * G + g
                    for f in range(2, NF):
                        pool.wait_ge(s["h_hi"], c * NF + f + 1 + NF)
                        pool.tensor_tensor(h_lo[g][:, f, :], h[g][:, f, :], h_hi[g][:, f, :].bitcast(F32), ALU.subtract).then_inc(s["h_lo_pool"], 1)

            with pool.Fori(0, NGROUP // 2) as jj:
                for par in range(2):
                    group(jj * 2 + par, par)


def lru_phase(nc, name, X, K, w):
    G = 2
    NH = 2
    with ExitStack() as ctx:
        ph = Phase(nc, ctx, name)
        w_in = ph.sb("w_in", [P, 4, P])
        w_dt = ph.sb("w_dt", [P, NH, NH, P])
        w_out = ph.sb("w_out", [P, NH, D])
        vecs = ph.sb("vecs", [P, 1 + NH])
        half_b = ph.sb("half_b", [P, NH])
        xn = [ph.sb(f"xn{g}", [P, CH]) for g in range(G)]
        hh = [ph.sb(f"hh{g}", [P, CH]) for g in range(G)]
        u = [ph.sb(f"u{g}", [P, NH, CH]) for g in range(G)]
        z = [ph.sb(f"z{g}", [P, NH, CH]) for g in range(G)]
        th = [ph.sb(f"th{g}", [P, NH, CH]) for g in range(G)]
        lam = [ph.sb(f"lam{g}", [P, NH, CH]) for g in range(G)]
        oml = [ph.sb(f"oml{g}", [P, NH, CH]) for g in range(G)]
        drive = [ph.sb(f"drive{g}", [P, NH, CH]) for g in range(G)]
        state = [ph.sb(f"state{g}", [P, NH, CH]) for g in range(G)]
        gated = [ph.sb(f"gated{g}", [P, NH, CH]) for g in range(G)]
        xy = [ph.sb(f"xy{g}", [P, CH]) for g in range(G)]
        bank_n = [ph.ps(f"bank_n{g}") for g in range(G)]
        bank_u = [ph.ps(f"bank_u{i}") for i in range(4)]
        bank_o = [ph.ps(f"bank_o{g}") for g in range(G)]
        n1, n2 = Norm(ph, "n1", K, bank_n), Norm(ph, "n2", K, bank_n, rms=True)
        s = {n: ph.sem(n) for n in ("loaded", "half_b", "xn", "hh", "uv", "silu", "gate", "tanh", "lam", "drive", "state", "gated", "down", "xy", "added")}
        block = ctx.enter_context(nc.Block())

        @block.sync
        def _(sp):
            sp.dma_start(w_in[:], w["lru_win"].rearrange("p (a d) -> p a d", a=4)).then_inc(s["loaded"], 16)
            sp.dma_start(w_dt[:], w["lru_wdt"].rearrange("p (a b d) -> p a b d", a=NH, b=NH)).then_inc(s["loaded"], 16)
            sp.dma_start(w_out[:], w["lru_wout"].rearrange("p (a d) -> p a d", a=NH)).then_inc(s["loaded"], 16)
            sp.dma_start(vecs[:], w["lru_vecs"]).then_inc(s["loaded"], 16)

        @block.tensor
        def _(pe):
            pe.wait_ge(s["loaded"], 64)

            def norm(b, step):
                for g in range(G):
                    if step == 0:
                        n1.tensor_mean(pe, b, g, X[:, tok(b * G + g)])
                    if step == 1:
                        n1.tensor_var(pe, b, g)
                    if step == 2:
                        n1.tensor_spread(pe, b, g)
                    if step == 3:
                        n2.tensor_var(pe, b, g)
                    if step == 4:
                        n2.tensor_spread(pe, b, g)

            for step in range(5):
                norm(0, step)
            with pe.Fori(0, BATCH) as b:
                pe.wait_ge(s["hh"], (b + 1) * G)
                for g in range(G):
                    c = b * G + g
                    for i in range(4):
                        if i < NH:
                            pe.wait_ge(s["tanh"], c * NH)
                        pe.wait_ge(s["silu"], c * 4)
                        pe.matmul(bank_u[i][:], w_in[:, i, :], hh[g][:], start=True, stop=True).then_inc(s["uv"], 1)
                    norm(b + 1, 2 * g)
                    for o in range(NH):
                        pe.wait_ge(s["silu"], c * 4 + NH)
                        for i in range(NH):
                            m = pe.matmul(bank_u[o][:], w_dt[:, i, o, :], u[g][:, i, :], start=i == 0, stop=i == NH - 1)
                        m.then_inc(s["gate"], 1)
                    norm(b + 1, 2 * g + 1)
                for g in range(G):
                    c = b * G + g
                    pe.wait_ge(s["added"], b * G)
                    for i in range(NH):
                        pe.wait_ge(s["gated"], c * NH + i + 1)
                        m = pe.matmul(bank_o[g][:], w_out[:, i, :], gated[g][:, i, :], start=i == 0, stop=i == NH - 1)
                    m.then_inc(s["down"], 1)
                    if g == 0:
                        norm(b + 1, 4)

        @block.scalar
        def _(act):
            act.wait_ge(s["loaded"], 64)
            act.activation(half_b[:], vecs[:, 1:1 + NH], ACT.Copy, scale=0.5).then_inc(s["half_b"], 1)
            act.wait_ge(s["half_b"], 1)

            def square(b, first):
                for g in range(G):
                    if first:
                        n1.scalar_square(act, b, g)
                    else:
                        act.wait_ge(s["xn"], b * G + g + 1)
                        n2.scalar_square(act, b, g, xn[g][:])

            square(0, True)
            square(0, False)
            with act.Fori(0, BATCH) as b:
                act.wait_ge(s["gated"], (b * G) * NH)
                for g in range(G):
                    c = b * G + g
                    for i in range(4):
                        act.wait_ge(s["uv"], c * 4 + i + 1)
                        act.activation((u, z)[i // NH][g][:, i % NH, :], bank_u[i][:], ACT.Silu).then_inc(s["silu"], 1)
                    square(b + 1, g == 0)
                    for i in range(NH):
                        act.wait_ge(s["gate"], c * NH + i + 1)
                        act.activation(th[g][:, i, :], bank_u[i][:], ACT.Tanh, bias=half_b[:, i:i + 1], scale=0.5).then_inc(s["tanh"], 1)

        @block.gpsimd
        def _(pool):
            def power(b):
                for n in (n1, n2):
                    for g in range(G):
                        n.pool_power(pool, b, g)

            power(0)
            with pool.Fori(0, BATCH) as b:
                power(b + 1)

        @block.vector
        def _(dve):
            dve.wait_ge(s["loaded"], 64)

            def norm(b, step):
                for g in range(G):
                    if step == 0:
                        n1.vector_centre(dve, b, g, X[:, tok(b * G + g)])
                    if step == 1:
                        n1.vector_var(dve, b, g)
                    if step == 2:
                        n1.vector_diag(dve, b, g)
                    if step == 3:
                        n1.vector_wait_spread(dve, b, g)
                        dve.tensor_tensor(xn[g][:], n1.centred[g][:], bank_n[g][:], ALU.mult).then_inc(s["xn"], 1)
                    if step == 4:
                        n2.vector_var(dve, b, g)
                    if step == 5:
                        n2.vector_diag(dve, b, g)
                    if step == 6:
                        n2.vector_wait_spread(dve, b, g)
                        dve.scalar_tensor_tensor(hh[g][:], xn[g][:], vecs[:, 0:1], bank_n[g][:], ALU.mult, ALU.mult).then_inc(s["hh"], 1)
                    if step == 7:
                        after(dve, s["added"], b * G)
                        dve.tensor_tensor(xy[g][:], X[:, tok(b * G + g)], xn[g][:], ALU.add).then_inc(s["xy"], 1)

            for step in range(8):
                norm(0, step)
            with dve.Fori(0, BATCH) as b:
                norm(b + 1, 0)
                for g in range(G):
                    c = b * G + g
                    for i in range(NH):
                        k = c * NH + i
                        dve.wait_ge(s["tanh"], k + 1)
                        dve.tensor_scalar(lam[g][:, i, :], th[g][:, i, :], 0.5, 0.5, ALU.mult, ALU.add)
                        dve.tensor_scalar(oml[g][:, i, :], th[g][:, i, :], -0.5, 0.5, ALU.mult, ALU.add).then_inc(s["lam"], 1)
                    for i in range(NH):
                        k = c * NH + i
                        dve.wait_ge(s["lam"], k + 1)
                        dve.tensor_tensor(drive[g][:, i, :], oml[g][:, i, :], u[g][:, i, :], ALU.mult).then_inc(s["drive"], 1)
                    norm(b + 1, 1 if g == 0 else 4)
                    for i in range(NH):
                        k = c * NH + i
                        dve.wait_ge(s["drive"], k + 1)
                        if g:
                            dve.wait_ge(s["state"], k - 1)
                        start = state[0][:, i, CH - 1:CH] if g else 0.0
                        dve.tensor_tensor_scan(state[g][:, i, :], lam[g][:, i, :], drive[g][:, i, :], start, ALU.mult, ALU.add).then_inc(s["state"], 1)
                    norm(b + 1, 2 if g == 0 else 5)
                    for i in range(NH):
                        k = c * NH + i
                        dve.wait_ge(s["state"], k + 1)
                        dve.wait_ge(s["silu"], c * 4 + NH + i + 1)
                        dve.wait_ge(s["down"], b * G)
                        dve.tensor_tensor(gated[g][:, i, :], state[g][:, i, :], z[g][:, i, :], ALU.mult).then_inc(s["gated"], 1)
                    norm(b + 1, 3 if g == 0 else 6)
                for g in range(G):
                    c = b * G + g
                    dve.wait_ge(s["xy"], c + 1)
                    dve.wait_ge(s["down"], c + 1)
                    dve.tensor_tensor(X[:, tok(c)], bank_o[g][:], xy[g][:], ALU.add).then_inc(s["added"], 1)
                norm(b + 1, 7)


def load_constants(nc, ctx, w, X):
    keep = Phase(nc, ctx, "const")
    K = {"mean": keep.sb("mean", [P, P]), "ones_row": keep.sb("ones_row", [1, P]), "ident": keep.sb("ident", [P, P]),
         "ones": keep.sb("ones", [P, P]), "neg_half": keep.sb("neg_half", [P, CH // P])}
    with ExitStack() as c2:
        ph = Phase(nc, c2, "const_load")
        loaded = ph.sem("loaded")
        block = c2.enter_context(nc.Block())

        @block.sync
        def _(sp):
            sp.dma_start(X[:, 0:TOK], w["x"]).then_inc(loaded, 16)
            sp.dma_start(K["ident"][:], w["ident"]).then_inc(loaded, 16)
            sp.wait_ge(loaded, 32)

        @block.gpsimd
        def _(pool):
            pool.memset(X[:, TOK:TOK + 2 * CH], 0.0)
            pool.memset(K["mean"][:], 1.0 / D)
            pool.memset(K["ones_row"][:], 1.0)
            pool.memset(K["ones"][:], 1.0)
            pool.memset(K["neg_half"][:], -0.5)
    return K


def store_output(nc, X, out):
    with ExitStack() as ctx:
        ph = Phase(nc, ctx, "store")
        stored = ph.sem("stored")
        block = ctx.enter_context(nc.Block())

        @block.sync
        def _(sp):
            sp.dma_start(out, X[:, 0:TOK]).then_inc(stored, 16)
            sp.wait_ge(stored, 16)


def shape_constants():
    t = {}
    pos = np.arange(SEQ, dtype=np.float32) * np.float32((GRID - 1) / (SEQ - 1))
    low = np.floor(pos).astype(np.int32)
    frac = pos - low.astype(np.float32)
    grid = np.zeros((SEQ, GRID), np.float32)
    np.add.at(grid, (np.arange(SEQ), low), np.float32(1) - frac)
    np.add.at(grid, (np.arange(SEQ), np.minimum(low + 1, GRID - 1)), frac)
    grid[-1] = 0
    t["grid3"] = np.tile(grid.T, (3, 1))
    negmask = np.zeros((REL, 2), np.float32)
    negmask[GRID:2 * GRID, 0] = -1
    negmask[2 * GRID:, 1] = -1
    t["negmask"] = negmask
    row, col = np.meshgrid(np.arange(P), np.arange(P), indexing="ij")
    t["causal"] = np.where(col > row, NEG, 0).astype(np.float32)
    sel = np.zeros((P, 64), np.float32)
    for g in range(4):
        sel[32 * g + HD, g * HD:(g + 1) * HD] = 1
        sel[32 * g + np.arange(HD), 32 + g * HD + np.arange(HD)] = 1
    t["sel_b"] = sel
    half = HD // 2
    inv_freq = (np.float32(1) / np.float32(10000.0) ** (np.arange(half, dtype=np.float32) / np.float32(half))).astype(np.float32)
    angles = np.arange(SEQ, dtype=np.float32)[None, :] * inv_freq[:, None]
    cos, sin = np.cos(angles), np.sin(angles)
    t["turn"] = np.concatenate([np.tile(cos, (2 * HEADS, 1)), np.tile(np.concatenate([-sin, sin]), (HEADS, 1))], axis=1)
    select = np.zeros((P, 2 * N_STATE + 1), np.float32)
    for r in range(2 * N_STATE):
        select[[HEADS + r, 64 + HEADS + r], r] = 1
    select[64:, 2 * N_STATE] = -1
    t["m_select"] = select
    t["head_ones"] = np.kron(np.eye(HEADS, dtype=np.float32), np.ones((HD, HD), np.float32))
    return t


def host_layout(i):
    a = {k: np.ascontiguousarray(v) for k, v in i.items()}
    t = {}
    t["x"] = a["L0_attn_a_x"].reshape(TOK, D).T
    m = "L0_attn_a_"
    t["m_win"] = a[m + "W_in"].reshape(D, 4, P)
    t["m_conv"] = a[m + "conv_w"].reshape(2, P, CONV).transpose(1, 0, 2)
    per_channel = [a[m + "conv_b"], a[m + "b_dt"], np.repeat(a[m + "A_log"], INNER // HEADS), np.repeat(a[m + "D_skip"], INNER // HEADS),
                   a[m + "ln_g"], a[m + "ln_b"]]
    t["m_vecs"] = np.stack(per_channel).reshape(6, 2, P).transpose(2, 0, 1)
    wp = a[m + "W_xproj"].reshape(2, P, HEADS + 2 * N_STATE).transpose(1, 0, 2)
    gap = np.zeros((P, 2, 64 - wp.shape[2]), np.float32)
    t["m_wproj"] = np.concatenate([wp, gap, wp, gap], axis=2)
    t["m_wdt"] = a[m + "W_dt"]
    t["m_wout"] = a[m + "W_out"].reshape(2, P, D).transpose(1, 0, 2)
    m = "L0_ffn_"
    w1 = np.concatenate([a[m + "shared_w1"][None], a[m + "spec_w1"]])
    t["ffn_w1"] = w1.transpose(2, 0, 1).reshape(D, N_FFN * FF)
    w2 = np.concatenate([a[m + "shared_w2"][None], a[m + "spec_w2"]])
    t["ffn_w2"] = w2.reshape(N_FFN, D, NF, P).transpose(3, 0, 2, 1).reshape(P, N_FFN * NF * D)
    b1 = np.concatenate([a[m + "shared_b1"][None], a[m + "spec_b1"]])
    t["ffn_b1"] = b1.reshape(N_FFN * NF, P).T
    t["ffn_b2"] = a[m + "shared_b2"].reshape(D, 1)
    t["ffn_eb2"] = np.tile(a[m + "spec_b2"], (2, 1))
    t["ffn_rw"] = a[m + "router_w"].T
    t["ffn_rb"] = a[m + "router_b"].reshape(1, N_EXP)
    t["iota8"] = np.tile(np.arange(N_EXP, dtype=np.float32), (P, 1))
    t["ident"] = np.eye(P, dtype=np.float32)
    t["pick8"] = np.tile(np.repeat(np.eye(N_EXP, dtype=np.float32), P, axis=1), (2, 1))
    m = "L0_attn_b_"
    t["ab_wq"], t["ab_wk"], t["ab_wv"], t["attnb_wo"] = (a[m + n].T for n in ("Wq", "Wk", "Wv", "Wo"))
    t["ab_vecs"] = np.stack([a[m + n] for n in ("bq", "bk", "gamma", "beta")], axis=1)
    t["ab_bv"] = a[m + "bv"].reshape(1, D)
    t["attnb_bo"] = a[m + "bo"].reshape(D, 1)
    t["ab_rel"] = np.tile(a[m + "rel_bias"].transpose(1, 0, 2)[:, :, None, :], (1, 1, 3, 1)).reshape(GRID, HEADS * REL)
    wqkv = a["L1_attn_a_Wqkv"]
    partner = np.arange(D) ^ (HD // 2)
    t["aa_wq"] = np.concatenate([wqkv[:, 0:D], wqkv[:, 0:D][:, partner], wqkv[:, D:2 * D], wqkv[:, D:2 * D][:, partner]], axis=1)
    t["aa_wv"] = wqkv[:, 2 * D:]
    t["attna_wo"] = a["L1_attn_a_Wo"]
    t["attna_bo"] = a["L1_attn_a_bo"].reshape(D, 1)
    t["tern_w1"] = a["L1_ffn_W1"].T
    t["tern_w2"] = a["L1_ffn_W2"].reshape(D, NF, P).transpose(2, 1, 0).reshape(P, NF * D)
    t["tern_b1"] = a["L1_ffn_b1"].reshape(NF, P).T
    t["tern_b2"] = a["L1_ffn_b2"].reshape(D, 1)
    m = "L1_attn_b_"
    t["lru_win"] = a[m + "W_in"].T
    t["lru_wdt"] = a[m + "W_dt"].reshape(2, P, 2, P).transpose(3, 2, 0, 1).reshape(P, 4 * P)
    t["lru_wout"] = a[m + "W_out"].reshape(D, 2, P).transpose(2, 1, 0).reshape(P, 2 * D)
    t["lru_vecs"] = np.concatenate([a[m + "w_norm"].reshape(D, 1), a[m + "b_dt"].reshape(2, P).T], axis=1)
    t.update(shape_constants())
    return {k: np.ascontiguousarray(v) for k, v in t.items()}


def hybrid_stack(nc, w, out):
    with ExitStack() as ctx:
        X = ctx.enter_context(nc.sbuf_tensor("X", [P, TOK + 2 * CH], F32))
        K = load_constants(nc, ctx, w, X)
        with ExitStack() as stage:
            experts = expert_buffers(nc, stage, "moe_a_experts")
            mamba_phase(nc, "mamba", X, K, w, experts)
            ffn_stage(nc, "moe_a", X, K, w, *experts)
        with ExitStack() as stage:
            experts = attnb_phase(nc, "attnb", X, K, w, stage)
            ffn_stage(nc, "moe_b", X, K, w, *experts)
        attna_phase(nc, "attna", X, K, w)
        tern_phase(nc, "tern_a", X, K, w)
        lru_phase(nc, "lru", X, K, w)
        tern_phase(nc, "tern_b", X, K, w)
        store_output(nc, X, out)


def kernel(**inputs):
    import concourse.bacc as _bacc
    from concourse.bass_utils import run_bass_kernel_spmd as _run

    nc = _bacc.Bacc("TRN2", target_bir_lowering=False, num_devices=1)
    arrays = {f"in_{k}": v for k, v in host_layout(inputs).items()}
    w = {k[3:]: nc.dram_tensor(k, v.shape, F32, kind="ExternalInput").ap() for k, v in arrays.items()}
    out = nc.dram_tensor("out", (D, TOK), F32, kind="ExternalOutput").ap()
    hybrid_stack(nc, w, out)
    r = _run(nc, [arrays], core_ids=[0])
    return np.ascontiguousarray(r.results[0]["out"].T).reshape(BATCH, SEQ, D)
```
